# Optimizing a Trainium2 kernel written in Bass

```python
import numpy as np
import jax
import jax.numpy as jnp

def _softmax(x, axis=-1):
    return jax.nn.softmax(x, axis=axis)

def _gelu(x):
    return jax.nn.gelu(x, approximate=True)

def _silu(x):
    return jax.nn.silu(x)

def _sigmoid(x):
    return jax.nn.sigmoid(x)

def _layernorm(x, axis=-1, eps=1e-05):
    m = jnp.mean(x, axis=axis, keepdims=True)
    v = jnp.var(x, axis=axis, keepdims=True)
    return (x - m) / jnp.sqrt(v + eps)

def _scatter_add(tgt, idx, src, axis=0):
    return tgt.at[idx].add(src)

def _segment_sum(src, seg, n):
    return jax.ops.segment_sum(src, seg, n)
kernel_name = 'mk_decoder_preln_d1_seqx_r8_ebac73'

def setup_inputs(seed: int=0):
    np.random.seed(seed)
    _w = jnp.asarray

    def _rec_inputs():
        import jax
        import jax.numpy as jnp
        _rk = jax.random.key(seed)
        x = -0.000125 + 0.9999 * jax.random.normal(jax.random.fold_in(_rk, 1), (4, 256, 256), jnp.float32)
        _lenS = 256 - jax.random.randint(jax.random.fold_in(_rk, 7), (4,), 0, max(1, 256 // 4) + 1, jnp.int32)
        _lenS2 = 256 - jax.random.randint(jax.random.fold_in(_rk, 8), (4,), 0, max(1, 256 // 4) + 1, jnp.int32)
        fside_BxS2xS2_0 = -3.05549e-07 + 0.0199987 * jax.random.normal(jax.random.fold_in(_rk, 11), (4, 256, 256), jnp.float32)
        _ctx_1024P = jax.random.normal(jax.random.fold_in(_rk, 12), (4, 16, 128), jnp.float32)
        _ctx_1024c = jax.random.dirichlet(jax.random.fold_in(_rk, 512), 0.3 * jnp.ones((16,), jnp.float32), (4, 256))
        _ctx_1024t = jnp.einsum('bsk,bkd->bsd', _ctx_1024c, _ctx_1024P)
        _ctx_1024t = _ctx_1024t * jax.lax.rsqrt(jnp.mean(jnp.square(_ctx_1024t)) + 1e-12) * 0.953939
        ctx_1024 = 6.82029e-06 + 0.0200006 * (_ctx_1024t + 0.3 * jax.random.normal(jax.random.fold_in(_rk, 612), (4, 256, 128), jnp.float32))
        return (x, fside_BxS2xS2_0, ctx_1024)
    x, fside_BxS2xS2_0, ctx_1024 = _rec_inputs()

    def _L0_attn_setup():
        import math
        import jax, jax.numpy as jnp
        import numpy as np
        B, S, H = (1, 256, 256)
        NH = 16
        DN = 128
        DR = 64
        DV = 128
        QL = 192
        KL = 64
        EPS = 1e-06
        ROPE_BASE = 10000.0

        def _rmsnorm(x, gamma, eps=EPS):
            return x * gamma * jax.lax.rsqrt(jnp.mean(x * x, axis=-1, keepdims=True) + eps)

        def _rope_tables(seq_len, dim, dtype):
            inv_freq = 1.0 / ROPE_BASE ** (jnp.arange(0, dim, 2, dtype=jnp.float32) / dim)
            ang = jnp.arange(seq_len, dtype=jnp.float32)[:, None] * inv_freq
            cos = jnp.concatenate([jnp.cos(ang)] * 2, axis=-1).astype(dtype)
            sin = jnp.concatenate([jnp.sin(ang)] * 2, axis=-1).astype(dtype)
            return (cos[None, :, None, :], sin[None, :, None, :])

        def _rotate_half(x):
            h = x.shape[-1] // 2
            return jnp.concatenate([-x[..., h:], x[..., :h]], axis=-1)
        key = jax.random.key(seed)
        ks = jax.random.split(key, 6)
        w = 0.02
        return {'hidden': jax.random.normal(ks[0], (B, S, H), jnp.float32), 'w_kv_a': jax.random.normal(ks[1], (H, QL + KL + DR), jnp.float32) * w, 'q_a_gamma': jnp.ones((QL,), jnp.float32), 'w_qb': jax.random.normal(ks[2], (QL, NH * (DN + DR)), jnp.float32) * w, 'kv_a_gamma': jnp.ones((KL,), jnp.float32), 'w_kvb': jax.random.normal(ks[3], (KL, NH * (DN + DV)), jnp.float32) * w, 'w_o': jax.random.normal(ks[4], (NH * DV, H), jnp.float32) * w}
    _L0_attn_all = _L0_attn_setup()
    _L0_attn_in = {k: v for k, v in _L0_attn_all.items() if k in ('w_kv_a', 'q_a_gamma', 'w_qb', 'kv_a_gamma', 'w_kvb', 'w_o')}
    del _L0_attn_all

    def _L0_xattn_setup():
        import jax, jax.numpy as jnp
        import numpy as np
        EPS = 1e-06
        QMAX = 127.0

        def _smooth_quant_linear(x, w):
            amax_x = jnp.max(jnp.abs(x), axis=0)
            amax_w = jnp.max(jnp.abs(w), axis=0)
            s = jnp.sqrt(jnp.maximum(amax_x, EPS) / jnp.maximum(amax_w, EPS))
            s = jnp.maximum(s, EPS)
            xs = x / s
            ws = w * s
            x_scale = jnp.maximum(jnp.max(jnp.abs(xs), axis=-1, keepdims=True), EPS) / QMAX
            w_scale = jnp.maximum(jnp.max(jnp.abs(ws), axis=-1, keepdims=True), EPS) / QMAX
            x_q = jnp.clip(jnp.round(xs / x_scale), -QMAX, QMAX)
            w_q = jnp.clip(jnp.round(ws / w_scale), -QMAX, QMAX)
            return x_q @ w_q.T * x_scale * w_scale.T

        def _expert_forward(xe, guw, dw):
            h = _smooth_quant_linear(xe, guw)
            gate, up = jnp.split(h, 2, axis=-1)
            a = jax.nn.silu(gate) * up
            return _smooth_quant_linear(a, dw)
        key = jax.random.key(seed)
        k1, k2, k3 = jax.random.split(key, 3)
        E, T, D, I = (8, 256, 256, 128)
        x = jax.random.normal(k1, (E, T, D), dtype=jnp.float32)
        gate_up_weight = jax.random.normal(k2, (E, 2 * I, D), dtype=jnp.float32) * 0.02
        down_weight = jax.random.normal(k3, (E, D, I), dtype=jnp.float32) * 0.02
        return {'x': x, 'gate_up_weight': gate_up_weight, 'down_weight': down_weight}
    _L0_xattn_all = _L0_xattn_setup()
    _L0_xattn_in = {k: v for k, v in _L0_xattn_all.items() if k in ()}
    del _L0_xattn_all

    def _L0_ffn_setup():
        import math
        import jax, jax.numpy as jnp
        import numpy as np
        from jax import lax
        D = 256
        I = 128
        E = 32
        K = 4
        NG = 8
        TKG = 3
        NSH = 2
        SCALE = 2.5
        CF = 1.25
        B, S = (2, 256)

        def _router(x, router_w, e_bias):
            scores = jax.nn.sigmoid(x @ router_w.T)
            sc = scores + e_bias[None, :]
            T = x.shape[0]
            gs = sc.reshape(T, NG, E // NG)
            group_scores = lax.top_k(gs, 2)[0].sum(-1)
            _, gidx = lax.top_k(group_scores, TKG)
            gmask = jnp.zeros((T, NG), sc.dtype).at[jnp.arange(T)[:, None], gidx].set(1.0)
            smask = jnp.repeat(gmask, E // NG, axis=1)
            masked = jnp.where(smask > 0, sc, 0.0)
            _, topk_idx = lax.top_k(masked, K)
            topk_w = jnp.take_along_axis(scores, topk_idx, axis=1)
            topk_w = topk_w / (topk_w.sum(-1, keepdims=True) + 1e-20)
            topk_w = topk_w * SCALE
            return (topk_idx.astype(jnp.int32), topk_w)

        def _moe_forward(hidden_states, router_w, e_bias, W_gate, W_up, W_down, shared_gate, shared_up, shared_down):
            b, s, d = hidden_states.shape
            T = b * s
            C = int(math.ceil(CF * T / E))
            EC = E * C
            x = hidden_states.reshape(T, d)
            topk_idx, topk_w = _router(x, router_w, e_bias)
            expert_flat = topk_idx.reshape(-1)
            w_flat = topk_w.reshape(-1)
            tok_flat = jnp.repeat(jnp.arange(T, dtype=jnp.int32), K)
            sort_ix = jnp.argsort(expert_flat)
            e_sorted = expert_flat[sort_ix]
            tok_s = tok_flat[sort_ix]
            w_s = w_flat[sort_ix]
            counts = jnp.zeros(E, jnp.int32).at[e_sorted].add(1)
            group_start = jnp.concatenate([jnp.zeros(1, jnp.int32), jnp.cumsum(counts)[:-1].astype(jnp.int32)])
            pos = jnp.arange(T * K, dtype=jnp.int32) - group_start[e_sorted]
            valid = pos < C
            dest = e_sorted * C + jnp.where(valid, pos, 0)
            slots_token = jnp.zeros(EC, jnp.int32).at[dest].add(jnp.where(valid, tok_s, 0))
            slots_w = jnp.zeros(EC, w_s.dtype).at[dest].add(jnp.where(valid, w_s, 0.0))
            Xp = x[slots_token].reshape(E, C, d)
            G = jnp.einsum('ecd,edi->eci', Xp, W_gate)
            U = jnp.einsum('ecd,edi->eci', Xp, W_up)
            Y = jnp.einsum('eci,eid->ecd', jax.nn.silu(G) * U, W_down)
            Yf = Y.reshape(EC, d) * slots_w[:, None]
            out = jnp.zeros((T, d), x.dtype).at[slots_token].add(Yf)
            shared = jax.nn.silu(x @ shared_gate.T) * (x @ shared_up.T) @ shared_down.T
            return (out + shared).reshape(b, s, d)
        key = jax.random.key(seed)
        ks = jax.random.split(key, 8)

        def rn(k, shape, scale=0.02):
            return jax.random.normal(k, shape, jnp.float32) * scale
        return {'hidden_states': jax.random.normal(ks[0], (B, S, D), jnp.float32), 'router_w': rn(ks[1], (E, D)), 'e_bias': jnp.zeros((E,), jnp.float32), 'W_gate': rn(ks[2], (E, D, I)), 'W_up': rn(ks[3], (E, D, I)), 'W_down': rn(ks[4], (E, I, D)), 'shared_gate': rn(ks[5], (I * NSH, D)), 'shared_up': rn(ks[6], (I * NSH, D)), 'shared_down': rn(ks[7], (D, I * NSH))}
    _L0_ffn_all = _L0_ffn_setup()
    _L0_ffn_in = {k: v for k, v in _L0_ffn_all.items() if k in ('router_w', 'e_bias', 'W_gate', 'W_up', 'W_down', 'shared_gate', 'shared_up', 'shared_down')}
    del _L0_ffn_all
    return {'x': x, 'fside_BxS2xS2_0': fside_BxS2xS2_0, 'ctx_1024': ctx_1024, 'L0_attn_w_kv_a': _L0_attn_in['w_kv_a'], 'L0_attn_q_a_gamma': _L0_attn_in['q_a_gamma'], 'L0_attn_w_qb': _L0_attn_in['w_qb'], 'L0_attn_kv_a_gamma': _L0_attn_in['kv_a_gamma'], 'L0_attn_w_kvb': _L0_attn_in['w_kvb'], 'L0_attn_w_o': _L0_attn_in['w_o'], 'L0_ffn_router_w': _L0_ffn_in['router_w'], 'L0_ffn_e_bias': _L0_ffn_in['e_bias'], 'L0_ffn_W_gate': _L0_ffn_in['W_gate'], 'L0_ffn_W_up': _L0_ffn_in['W_up'], 'L0_ffn_W_down': _L0_ffn_in['W_down'], 'L0_ffn_shared_gate': _L0_ffn_in['shared_gate'], 'L0_ffn_shared_up': _L0_ffn_in['shared_up'], 'L0_ffn_shared_down': _L0_ffn_in['shared_down']}

def reference(x, fside_BxS2xS2_0, ctx_1024, L0_attn_w_kv_a, L0_attn_q_a_gamma, L0_attn_w_qb, L0_attn_kv_a_gamma, L0_attn_w_kvb, L0_attn_w_o, L0_ffn_router_w, L0_ffn_e_bias, L0_ffn_W_gate, L0_ffn_W_up, L0_ffn_W_down, L0_ffn_shared_gate, L0_ffn_shared_up, L0_ffn_shared_down):
    import jax
    import jax.numpy as jnp

    def _L0_attn_ref(hidden, w_kv_a, q_a_gamma, w_qb, kv_a_gamma, w_kvb, w_o):
        import math
        import jax, jax.numpy as jnp
        import numpy as np
        B, S, H = (1, 256, 256)
        NH = 16
        DN = 128
        DR = 64
        DV = 128
        QL = 192
        KL = 64
        EPS = 1e-06
        ROPE_BASE = 10000.0

        def _rmsnorm(x, gamma, eps=EPS):
            return x * gamma * jax.lax.rsqrt(jnp.mean(x * x, axis=-1, keepdims=True) + eps)

        def _rope_tables(seq_len, dim, dtype):
            inv_freq = 1.0 / ROPE_BASE ** (jnp.arange(0, dim, 2, dtype=jnp.float32) / dim)
            ang = jnp.arange(seq_len, dtype=jnp.float32)[:, None] * inv_freq
            cos = jnp.concatenate([jnp.cos(ang)] * 2, axis=-1).astype(dtype)
            sin = jnp.concatenate([jnp.sin(ang)] * 2, axis=-1).astype(dtype)
            return (cos[None, :, None, :], sin[None, :, None, :])

        def _rotate_half(x):
            h = x.shape[-1] // 2
            return jnp.concatenate([-x[..., h:], x[..., :h]], axis=-1)
        b, s, _ = hidden.shape
        fused = hidden @ w_kv_a
        q_c = fused[..., :QL]
        kv_c = fused[..., QL:QL + KL]
        k_pe = fused[..., QL + KL:]
        q = _rmsnorm(q_c, q_a_gamma) @ w_qb
        q = q.reshape(b, s, NH, DN + DR)
        q_nope, q_pe = (q[..., :DN], q[..., DN:])
        kv = _rmsnorm(kv_c, kv_a_gamma) @ w_kvb
        kv = kv.reshape(b, s, NH, DN + DV)
        k_nope, v = (kv[..., :DN], kv[..., DN:])
        cos, sin = _rope_tables(s, DR, hidden.dtype)
        q_pe = q_pe * cos + _rotate_half(q_pe) * sin
        k_pe = k_pe[:, :, None, :]
        k_pe = k_pe * cos + _rotate_half(k_pe) * sin
        q_full = jnp.concatenate([q_nope, q_pe], axis=-1)
        k_full = jnp.concatenate([k_nope, jnp.broadcast_to(k_pe, (b, s, NH, DR))], axis=-1)
        scale = 1.0 / math.sqrt(DN + DR)
        scores = jnp.einsum('bqhd,bkhd->bhqk', q_full, k_full) * scale
        pos = jnp.arange(s)
        causal = pos[:, None] >= pos[None, :]
        scores = jnp.where(causal[None, None], scores, jnp.asarray(-1e+30, scores.dtype))
        probs = jax.nn.softmax(scores, axis=-1)
        attn = jnp.einsum('bhqk,bkhd->bqhd', probs, v)
        return attn.reshape(b, s, NH * DV) @ w_o

    def _L0_xattn_ref(x, gate_up_weight, down_weight):
        import jax, jax.numpy as jnp
        import numpy as np
        EPS = 1e-06
        QMAX = 127.0

        def _smooth_quant_linear(x, w):
            amax_x = jnp.max(jnp.abs(x), axis=0)
            amax_w = jnp.max(jnp.abs(w), axis=0)
            s = jnp.sqrt(jnp.maximum(amax_x, EPS) / jnp.maximum(amax_w, EPS))
            s = jnp.maximum(s, EPS)
            xs = x / s
            ws = w * s
            x_scale = jnp.maximum(jnp.max(jnp.abs(xs), axis=-1, keepdims=True), EPS) / QMAX
            w_scale = jnp.maximum(jnp.max(jnp.abs(ws), axis=-1, keepdims=True), EPS) / QMAX
            x_q = jnp.clip(jnp.round(xs / x_scale), -QMAX, QMAX)
            w_q = jnp.clip(jnp.round(ws / w_scale), -QMAX, QMAX)
            return x_q @ w_q.T * x_scale * w_scale.T

        def _expert_forward(xe, guw, dw):
            h = _smooth_quant_linear(xe, guw)
            gate, up = jnp.split(h, 2, axis=-1)
            a = jax.nn.silu(gate) * up
            return _smooth_quant_linear(a, dw)
        return jax.vmap(_expert_forward)(x, gate_up_weight, down_weight)

    def _L0_ffn_ref(hidden_states, router_w, e_bias, W_gate, W_up, W_down, shared_gate, shared_up, shared_down):
        import math
        import jax, jax.numpy as jnp
        import numpy as np
        from jax import lax
        D = 256
        I = 128
        E = 32
        K = 4
        NG = 8
        TKG = 3
        NSH = 2
        SCALE = 2.5
        CF = 1.25
        B, S = (2, 256)

        def _router(x, router_w, e_bias):
            scores = jax.nn.sigmoid(x @ router_w.T)
            sc = scores + e_bias[None, :]
            T = x.shape[0]
            gs = sc.reshape(T, NG, E // NG)
            group_scores = lax.top_k(gs, 2)[0].sum(-1)
            _, gidx = lax.top_k(group_scores, TKG)
            gmask = jnp.zeros((T, NG), sc.dtype).at[jnp.arange(T)[:, None], gidx].set(1.0)
            smask = jnp.repeat(gmask, E // NG, axis=1)
            masked = jnp.where(smask > 0, sc, 0.0)
            _, topk_idx = lax.top_k(masked, K)
            topk_w = jnp.take_along_axis(scores, topk_idx, axis=1)
            topk_w = topk_w / (topk_w.sum(-1, keepdims=True) + 1e-20)
            topk_w = topk_w * SCALE
            return (topk_idx.astype(jnp.int32), topk_w)

        def _moe_forward(hidden_states, router_w, e_bias, W_gate, W_up, W_down, shared_gate, shared_up, shared_down):
            b, s, d = hidden_states.shape
            T = b * s
            C = int(math.ceil(CF * T / E))
            EC = E * C
            x = hidden_states.reshape(T, d)
            topk_idx, topk_w = _router(x, router_w, e_bias)
            expert_flat = topk_idx.reshape(-1)
            w_flat = topk_w.reshape(-1)
            tok_flat = jnp.repeat(jnp.arange(T, dtype=jnp.int32), K)
            sort_ix = jnp.argsort(expert_flat)
            e_sorted = expert_flat[sort_ix]
            tok_s = tok_flat[sort_ix]
            w_s = w_flat[sort_ix]
            counts = jnp.zeros(E, jnp.int32).at[e_sorted].add(1)
            group_start = jnp.concatenate([jnp.zeros(1, jnp.int32), jnp.cumsum(counts)[:-1].astype(jnp.int32)])
            pos = jnp.arange(T * K, dtype=jnp.int32) - group_start[e_sorted]
            valid = pos < C
            dest = e_sorted * C + jnp.where(valid, pos, 0)
            slots_token = jnp.zeros(EC, jnp.int32).at[dest].add(jnp.where(valid, tok_s, 0))
            slots_w = jnp.zeros(EC, w_s.dtype).at[dest].add(jnp.where(valid, w_s, 0.0))
            Xp = x[slots_token].reshape(E, C, d)
            G = jnp.einsum('ecd,edi->eci', Xp, W_gate)
            U = jnp.einsum('ecd,edi->eci', Xp, W_up)
            Y = jnp.einsum('eci,eid->ecd', jax.nn.silu(G) * U, W_down)
            Yf = Y.reshape(EC, d) * slots_w[:, None]
            out = jnp.zeros((T, d), x.dtype).at[slots_token].add(Yf)
            shared = jax.nn.silu(x @ shared_gate.T) * (x @ shared_up.T) @ shared_down.T
            return (out + shared).reshape(b, s, d)
        return _moe_forward(hidden_states, router_w, e_bias, W_gate, W_up, W_down, shared_gate, shared_up, shared_down)
    x = x + _L0_attn_ref(_layernorm(x, axis=-1), L0_attn_w_kv_a, L0_attn_q_a_gamma, L0_attn_w_qb, L0_attn_kv_a_gamma, L0_attn_w_kvb, L0_attn_w_o)
    x = x + _L0_xattn_ref(_layernorm(x, axis=-1), fside_BxS2xS2_0, ctx_1024)
    x = x + _L0_ffn_ref(_layernorm(x, axis=-1), L0_ffn_router_w, L0_ffn_e_bias, L0_ffn_W_gate, L0_ffn_W_up, L0_ffn_W_down, L0_ffn_shared_gate, L0_ffn_shared_up, L0_ffn_shared_down)
    return x

_drawn_inputs = setup_inputs


def setup_inputs(seed=0):
    import zlib

    import numpy as np

    out = dict(_drawn_inputs(seed))
    spreads = {'L0_attn_q_a_gamma': (1.0, 0.6),
     'L0_attn_kv_a_gamma': (1.0, 0.6),
     'L0_ffn_e_bias': (0.0, 0.8)}
    factors = {'fside_BxS2xS2_0': 4.771,
     'ctx_1024': 4.739,
     'L0_attn_w_qb': 8.0,
     'L0_ffn_router_w': 8.0,
     'L0_ffn_W_gate': 8.0,
     'L0_ffn_W_up': 8.0,
     'L0_ffn_W_down': 8.0,
     'L0_ffn_shared_gate': 3.389,
     'L0_ffn_shared_up': 3.355,
     'L0_ffn_shared_down': 3.353}
    for name, (base, spread) in spreads.items():
        noise = np.random.default_rng([zlib.crc32(name.encode()), seed]).standard_normal(out[name].shape)
        drawn = base * np.exp(spread * noise) if base else spread * noise
        out[name] = jnp.asarray(drawn.astype(out[name].dtype))
    for name, factor in factors.items():
        out[name] = (out[name] * factor).astype(out[name].dtype)
    return out
```

```python
from contextlib import ExitStack

import concourse.bass as bass
from concourse import mybir

ALU = mybir.AluOpType
ACT = mybir.ActivationFunctionType
AX = mybir.AxisListType
F32 = mybir.dt.float32
BF16 = mybir.dt.bfloat16
U32 = mybir.dt.uint32

P = 128
B, S, D = 4, 256, 256
NT = B * S // P
NJ = S // P
KD = D // P
NH, DN, DR, DV, QL, KL = 16, 128, 64, 128, 192, 64
DQK = KL + DR
HC = 4
GH = 8
NHU = B * NH
E, TOPK, NG, TKG = 32, 4, 8, 3
EG = E // NG
CAP = 40
SLOTS = E * CAP
NS = SLOTS // P
XG = 4
I = 128
WE = 2 * KD * I + D
SM_SCALE = 1.0 / float(DN + DR) ** 0.5
EPS_LN, EPS_RMS, EPS_Q, QMAX = 1e-5, 1e-6, 1e-6, 127.0
ROUND = 12582912.0
NOSLOT = 4096.0
NW = 3

C_ID, C_MASK, C_TRI, C_COS, C_SIN, C_I32, C_I8, C_SLOT0 = 0, 128, 256, 384, 512, 640, 672, 680
NCONST = 712

SLOTS_A, SLOTS_B, SLOTS_C = 9, 10, 5
NHOME = SLOTS_A + SLOTS_B + SLOTS_C


def plan():
    steps = [("setup",)]
    steps += [("ln1", b) for b in range(1)]
    steps += [("hT", 0), ("hT", 1), ("fused", 0), ("fused", 1), ("ln1", 1), ("latT", 0), ("latT", 1)]
    front = []
    for t in range(2, NT):
        if t % 2 == 0 and t > 2:
            front.append(("ln1", t // 2))
        front += [("hT", t), ("fused", t), ("latT", t)]
    for p in range(NH // 2):
        steps += [("prepT", 2 * p), ("prepT", 2 * p + 1)]
        steps += front[:1]
        front = front[1:]
        steps += [("prepM", p)]
        steps += front[:2]
        front = front[2:]
    steps += front

    def q_units(b):
        return [(2 * b + j, c) for c in range(NH // HC) for j in range(NJ)]

    units = q_units(0)
    for i in range(len(units) + 1):
        if i < len(units):
            steps.append(("q",) + units[i])
        if i > 0:
            steps.append(("qT",) + units[i - 1])

    def cross(b):
        return [(f"x{i}", b) for i in range(13)]

    def route(b):
        return [(f"r{i}", b) for i in range(5)] + [("scatter", b, i) for i in range(4)]

    for b in range(B):
        first = [[] for _ in range(NH)]
        second = [[] for _ in range(NH)]
        if b + 1 < B:
            for u, unit in enumerate(q_units(b + 1)):
                first[2 * u].append(("q",) + unit)
                first[2 * u + 1].append(("qT",) + unit)
        second[11] += [("oT", 2 * b, 0), ("oT", 2 * b + 1, 0)]
        if b > 0:
            second[3] += [("oT", 2 * b - 2, 1), ("oT", 2 * b - 1, 1)]
            second[4] += [("y", 2 * b - 2), ("y", 2 * b - 1)]
            rest = cross(b - 1) + route(b - 1)
            halves = [(n, h) for n in range(5, NH) for h in (0, 1)]
            for i, st in enumerate(rest):
                n, h = halves[min(i, len(halves) - 1)]
                (second if h else first)[n].append(st)
        second[14 if b else 2].append(("wx", b))
        if b == 0:
            second[5].append(("rwT",))
            for i in range(3):
                second[6 + i].append(("shT", i))
        for n in range(NH):
            hn = b * NH + n
            steps.append(("scores", hn))
            steps += first[n]
            if hn >= 1:
                steps.append(("probsT", hn - 1))
            steps += second[n]
            if hn >= 2:
                steps.append(("pv", hn - 2))
                if (hn - 2) % GH == GH - 1:
                    steps.append(("norm", (hn - 2) // GH))
    steps += [("probsT", NHU - 1), ("pv", NHU - 2), ("pv", NHU - 1), ("norm", NHU // GH - 1)]
    steps += [("late_loads",)]
    b = B - 1
    steps += [("oT", 2 * b, 1), ("oT", 2 * b + 1, 1), ("y", 2 * b), ("y", 2 * b + 1)]
    fill = [(f"s{i}", bb) for bb in range(B - 1) for i in range(3)]
    for i, st in enumerate(cross(b) + route(b)):
        steps.append(st)
        if i % 2 == 0 and fill:
            steps.append(fill.pop(0))
    steps += fill
    steps += [("s0", b), ("s1", b), ("s2", b)]
    steps += [("xp_load",)]
    steps += [("xpT", i) for i in range(NS // 2)]
    stored = 0
    for g in range(E // XG + 1):
        if g < E // XG:
            steps.append(("gate_up", g))
        if g > 0:
            steps.append(("down", g - 1))
            while (stored + 1) * 2 * P <= g * XG * CAP:
                steps.append(("yT", stored))
                stored += 1
    for t in range(NT):
        steps.append(("combine", t))
    return steps


ITEMS = {
    "hT": [("hT", 1)], "fused": [("fused", 1)], "latT": [("latT", 1)],
    "prepT": [("prepT", 1)], "prepM": [("prepM", 1)],
    "q": [("q", 1)], "qT": [("qT", 1)], "oT": [("oT", 1)], "y": [("y", 1)],
    "wx": [("fsT", 1), ("cxT", 1)], "rwT": [("rwT", 1)], "shT": [("shT", 1)],
    "x1": [("xT", 1)], "x3": [("xs", 1), ("ws", 1)], "x5": [("xqT", 1)],
    "x6": [("xb", 1), ("h1", 1)], "x9": [("as", 1)], "x11": [("aqT", 1), ("wb", 1)],
    "x12": [("h2", 1)],
    "r1": [("h3T", 1)], "r2": [("logit", 1)], "r4": [("pos", 1)],
    "s0": [("sg", 1), ("su", 1)], "s2": [("sd", 1)],
    "xpT": [("xpT", 1)], "gate_up": [("gu", 1)], "down": [("dn", 1)], "yT": [("yT", 1)],
}


class Ring:

    def __init__(self, steps):
        self.at = {}
        filled, emptied, n = [0] * NW, [0] * NW, 0
        for step in steps:
            for name, empties in ITEMS.get(step[0], []):
                k = n % NW
                self.at[(name,) + step[1:]] = (k, emptied[k], filled[k] + 1, emptied[k] + empties)
                filled[k] += 1
                emptied[k] += empties
                n += 1


def decoder_layer(nc, x, fside, ctx_w, w_kv_a, q_gamma, w_qb, kv_gamma, w_kvb, w_o, router_w, e_bias,
                  w_gate, w_up, w_down, sh_gate, sh_up, sh_down, consts, out):
    steps = plan()
    ring = Ring(steps)
    xp_dram = nc.dram_tensor("expert_rows", (SLOTS, D), F32, kind="Internal").ap()
    y_dram = nc.dram_tensor("expert_out", (SLOTS, D), F32, kind="Internal").ap()

    with ExitStack() as stack:
        def sb(name, shape, dt=F32):
            return stack.enter_context(nc.sbuf_tensor(name, shape, dt))

        def sem(name):
            return stack.enter_context(nc.semaphore(name))

        ps_s = stack.enter_context(nc.psum_tensor("ps_scores", [P, 2, 512], F32))
        ps_pt = stack.enter_context(nc.psum_tensor("ps_probsT", [P, 512], F32))
        ps_o = stack.enter_context(nc.psum_tensor("ps_heads", [P, NJ, 512], F32))
        ps_w = stack.enter_context(nc.psum_tensor("ps_work", [P, NW, 512], F32))

        cst = sb("consts", [P, NCONST])
        id_bf = sb("ident_bf16", [P, P], BF16)
        mask_bf = sb("mask_bf16", [P, P], BF16)
        tri_bf = sb("tri_bf16", [P, P], BF16)
        ones_bf = sb("ones_bf16", [P, P], BF16)
        xres = sb("x_residual", [P, NT, D])
        neg_half = sb("neg_half", [P, 1])
        pos_half = sb("pos_half", [P, 1])
        gam_q = sb("gamma_q", [P, QL])
        gam_kv = sb("gamma_kv", [P, KL])
        bias_e = sb("e_bias", [P, E])
        w_mo = sb("w_folded_out", [P, NH // 2, D])
        fs = sb("fside", [P, B, 2, D])
        cx = sb("ctx", [P, B, 2, I])
        rw = sb("router_w", [P, D])
        rwT = sb("router_wT", [P, KD, E])
        shT = sb("shared_wT", [P, 3, KD, D])
        reg_a = sb("region_a", [P, 6912])
        reg_b = sb("region_b", [P, 8192])
        reg_c = sb("region_c", [P, 4096])
        reg_g = sb("region_g", [P, 4096])
        reg_h = sb("region_h", [P, 4096])
        wq0 = reg_a[:, 0:NH * DN].rearrange("p (h m) -> p h m", h=NH)
        wkq = reg_a[:, 2048:6144].rearrange("p (h m) -> p h m", h=NH)
        wo = reg_b[:, 0:4096].rearrange("p (h d) -> p h d", h=NH)
        qT = reg_b[:, :].rearrange("p (b h t) -> p b h t", b=2, h=NH)
        wf0 = reg_c[:, 0:2048].rearrange("p (h m) -> p h m", h=NH)
        wf1 = reg_c[0:64, 2048:4096].rearrange("p (h m) -> p h m", h=NH)
        on = reg_g[:, 0:2048].rearrange("p (g j m) -> p g j m", g=2, j=NJ)
        oT = reg_g[:, 2048:4096].rearrange("p (j h t) -> p j h t", j=NJ, h=NH // 2)
        xpT = reg_g[:, 0:KD * SLOTS].rearrange("p (k s) -> p k s", k=KD)
        kv = reg_h[:, 0:1024].rearrange("p (t m) -> p t m", t=NT)
        kT = reg_h[:, 1024:2048].rearrange("p (b m) -> p b m", b=B)
        qn0 = reg_h[:, 2048:3072].rearrange("p (t m) -> p t m", t=NT)
        qn1 = reg_h[0:64, 3072:4096].rearrange("p (t m) -> p t m", t=NT)
        rows = reg_h[:, 0:NS * D].rearrange("p (i d) -> p i d", i=NS)

        def home(e):
            s = e % NHOME
            if s < SLOTS_A:
                r, o = reg_a, s * WE
            elif s < SLOTS_A + SLOTS_B:
                r, o = reg_b, (s - SLOTS_A) * WE
            else:
                r, o = reg_c, (s - SLOTS_A - SLOTS_B) * WE
            return r[:, o:o + WE]

        def gate_of(e):
            return home(e)[:, 0:KD * I].rearrange("p (k i) -> p k i", k=KD)

        def up_of(e):
            return home(e)[:, KD * I:2 * KD * I].rearrange("p (k i) -> p k i", k=KD)

        def down_of(e):
            return home(e)[:, 2 * KD * I:WE]

        reg_t = sb("region_t", [P, 3072])
        reg_r = sb("region_r", [P, 2048])
        wkva = reg_t[:, 0:640].rearrange("p (k n) -> p k n", k=KD)
        probs = reg_t[:, 640:1408].rearrange("p (u q) -> p u q", u=2)
        probsT = reg_t[:, 1408:2176].rearrange("p (u q) -> p u q", u=2)
        es = reg_t[:, 0:1024].rearrange("p (u q) -> p u q", u=2)
        act_s = reg_t[:, 1024:1536].rearrange("p (k t) -> p k t", k=2)
        ee = reg_t[:, 1536:1536 + 2 * XG * CAP].rearrange("p (u q) -> p u q", u=2)
        hE = reg_t[:, 1856:1856 + 2 * XG * CAP].rearrange("p (u q) -> p u q", u=2)
        hn_f = reg_r[:, 0:512].rearrange("p (j d) -> p j d", j=NJ)
        hT_f = reg_r[:, 512:768]
        wT = reg_r[:, 768:1408].rearrange("p (i m) -> p i m", i=2)
        sq = reg_r[:, 1408:1664]
        qn = reg_r[:, 1664:1664 + QL]
        qa = reg_r[:, 0:1024].rearrange("p (i d) -> p i d", i=4)
        gu = reg_r[:, 1024:2048].rearrange("p (i d) -> p i d", i=4)
        zeros = reg_g[:, 0:512]

        ssq = sb("sum_squares", [P, NT, 2])
        rrms = sb("rrms", [P, NT, 2])
        weps = sb("rms_eps", [P, NT, 2])
        kr = sb("k_rope_tmp", [P, 2, DR])
        qs = sb("q_chunk", [P, 2, HC * DQK])
        qr = sb("q_rope_tmp", [P, 2, HC * DR])
        nmax = sb("neg_max", [P, NHU, 2])
        psum_ = sb("prob_sums", [P, NHU // GH, NJ, GH])
        rsum = sb("prob_rsums", [P, NHU // GH, NJ, GH])
        stats = sb("bn_stats", [P, 2, 6])
        mv = sb("mean_var", [P, 3, NT, 2])
        rstd = sb("rstd", [P, 3, NT])
        vtmp = sb("var_eps", [P, 3, NT])
        h2 = sb("h_cross", [P, NJ, D])
        fsT = sb("fsideT", [P, 512])
        cxT = sb("ctxT", [P, 256])
        xsT = sb("x_scaledT", [P, 512])
        wsT = sb("w_scaledT", [P, 512])
        rden = sb("rden", [P, B, 3])
        sm = sb("smooth", [P, B, 36])
        qb = sb("q_bf16", [P, 4, D], BF16)
        qTs = sb("qT_bf16", [P, 4, D], BF16)
        sbc = sb("scale_rows", [P, 2, D])
        h3 = sb("h_moe", [P, 2, NJ, D])
        h3T = sb("h_moeT", [P, B, KD, S])
        sc = sb("scores", [P, 3, NJ * E])
        rt = reg_r[:, 0:12 * NJ * E].rearrange("p (i m) -> p i m", i=12)
        top = sb("top", [P, NJ, 8])
        topi = sb("top_index", [P, NJ, 8], U32)
        tif = sb("top_index_f32", [P, NJ, TOPK])
        oh = reg_r[:, 768:1024]
        ohp = reg_r[:, 1024:1280]
        chosen = sb("chosen", [P, NT, E], BF16)
        slotf = sb("slot_f32", [P, 4, NJ * TOPK])
        scat = sb("slot_scatter", [P, NT, TOPK], U32)
        gath = sb("slot_gather", [P, NT, TOPK], U32)
        wtok = sb("token_weights", [P, NT, TOPK])
        h3T_flat = h3T[:].rearrange("p b k t -> p (b k t)")
        shw = h3T_flat[:, 0:1536].rearrange("p (i o d) -> p i o d", i=3, o=2)
        yT = [fs[:].rearrange("p b o d -> p (b o d)")[:, 0:SLOTS], h3T_flat[:, 0:SLOTS]]
        gbuf = reg_b[:, 0:2048].rearrange("p (n d) -> p n d", n=8)

        ld = {k: sem("ld_" + k) for k in ("consts", "x0", "x1", "x2", "x3", "wkva", "gam", "wkv", "wq", "rope_cols",
                                          "wo", "fs", "cx", "rw", "sh", "bias")}
        ld_experts = [sem(f"ld_experts{g}") for g in range(E // XG)]
        ld_rows = [sem(f"ld_rows{i}") for i in range(NS // 2)]
        bank_filled = [sem(f"bank_filled{k}") for k in range(NW)]
        bank_emptied = [sem(f"bank_emptied{k}") for k in range(NW)]
        names = """consts_ready halves_ready zeros_ready ln_stats ln_rstd h_ready squares_ready
            rms_ready lat_ready scores_ready max_ready exp_done probsT_done probsT_copied pv_done heads_normed
            rope_parts rope_added ratio_ready smooth_root smooth_ready scaledT_w inv_ready q_ready exp_gate act_ready
            ratio2_ready smooth_root2 smooth_ready2 scaledT_a scaledT_c inv2_ready q2_ready
            chosen_ready slots_ready shared_exp xp_zeroed expert_exp y_stored combined out_stored
            dve_chain act_chain pool_chain""".split()
        sg = {n: sem(n) for n in names}
        scattered = [sem(f"scattered{b}") for b in range(B)]
        gathered = [sem(f"gathered{i}") for i in range(8)]
        block = stack.enter_context(nc.Block())

        def c_(o, n):
            return cst[:, o:o + n]

        ident = c_(C_ID, P)

        def bank(item):
            return ps_w[:, ring.at[item][0], :]

        def wait_empty(eng, item):
            k, before, _, _ = ring.at[item]
            if before:
                eng.wait_ge(bank_emptied[k], before)

        def wait_filled(eng, item):
            k, _, filled, _ = ring.at[item]
            eng.wait_ge(bank_filled[k], filled)

        def wait_emptied(eng, item):
            k, _, _, after = ring.at[item]
            eng.wait_ge(bank_emptied[k], after)

        def fills(ins, item):
            ins.then_inc(bank_filled[ring.at[item][0]], 1)

        def empties(ins, item):
            ins.then_inc(bank_emptied[ring.at[item][0]], 1)

        step_no = {}
        for step in steps:
            kind = "ln" if step[0] in ("ln1", "x0", "r0") else step[0]
            step_no[step] = sum(1 for k in step_no.values() if k[0] == kind), kind
            step_no[step] = (kind, step_no[step][0])

        def nth(*step):
            return step_no[step][1]

        q_order = [step for step in steps if step[0] == "qT"]

        @block.sync
        def _(sp):
            def load_expert(e, s):
                sp.dma_start(gate_of(e), w_gate[e].rearrange("(k p) i -> p k i", p=P)).then_inc(s, 16)
                sp.dma_start(up_of(e), w_up[e].rearrange("(k p) i -> p k i", p=P)).then_inc(s, 16)
                sp.dma_start(down_of(e), w_down[e]).then_inc(s, 16)

            xt = x.rearrange("b (j p) d -> b p j d", p=P)
            sp.dma_start(xres[:, 0:2, :], xt[0]).then_inc(ld["x0"], 16)
            sp.dma_start(cst[:], consts).then_inc(ld["consts"], 16)
            sp.dma_start(wkva[:], w_kv_a.rearrange("(k p) n -> p k n", p=P)).then_inc(ld["wkva"], 16)
            sp.dma_start(gam_q[:], q_gamma.partition_broadcast(P)).then_inc(ld["gam"], 16)
            sp.dma_start(gam_kv[:], kv_gamma.partition_broadcast(P)).then_inc(ld["gam"], 16)
            sp.dma_start(xres[:, 2:4, :], xt[1]).then_inc(ld["x1"], 16)
            wqh = w_qb.rearrange("p (h m) -> p h m", h=NH)
            sp.dma_start(wkq[0:KL], w_kvb.rearrange("p (h m) -> p h m", h=NH)).then_inc(ld["wkv"], 16)
            sp.dma_start(wq0, wqh[0:P, :, 0:DN]).then_inc(ld["wq"], 16)
            sp.dma_start(wkq[KL:P, :, 0:DN], wqh[P:QL, :, 0:DN]).then_inc(ld["wq"], 16)
            sp.dma_start(wf0[:, :, KL:], wqh[0:P, :, DN:]).then_inc(ld["rope_cols"], 16)
            sp.dma_start(wf1[:, :, KL:], wqh[P:QL, :, DN:]).then_inc(ld["rope_cols"], 16)
            sp.dma_start(wo, w_o.rearrange("(h p) d -> p h d", p=P)).then_inc(ld["wo"], 16)
            sp.dma_start(xres[:, 4:6, :], xt[2]).then_inc(ld["x2"], 16)
            sp.dma_start(xres[:, 6:8, :], xt[3]).then_inc(ld["x3"], 16)
            sp.dma_start(fs[:], fside.rearrange("b (o p) d -> p b o d", p=P)).then_inc(ld["fs"], 16)
            sp.dma_start(cx[:], ctx_w.rearrange("b (o p) i -> p b o i", p=P)).then_inc(ld["cx"], 16)
            sp.dma_start(rw[0:E, :], router_w).then_inc(ld["rw"], 16)
            sp.dma_start(bias_e[:], e_bias.partition_broadcast(P)).then_inc(ld["bias"], 16)
            for i, w in enumerate((sh_gate, sh_up, sh_down)):
                sp.dma_start(shw[:, i], w.rearrange("(o p) d -> p o d", p=P)).then_inc(ld["sh"], 16)
            sp.wait_ge(sg["zeros_ready"], 1)
            xz = xp_dram.rearrange("(p a) d -> p (a d)", p=P)
            for i in range(NS // 2):
                sp.dma_start(xz[:, 512 * i:512 * i + 512], zeros).then_inc(sg["xp_zeroed"], 16)
            for p in range(NH // 2):
                wait_emptied(sp, ("prepM", p))
            for e in range(SLOTS_A):
                load_expert(e, ld_experts[e // XG])
            sp.wait_ge(sg["pv_done"], NHU)
            for e in range(SLOTS_A, NHOME):
                load_expert(e, ld_experts[e // XG])
            for b in range(B):
                sp.wait_ge(scattered[b], 16 * NJ * TOPK)
            for i in range(NS // 2):
                sp.dma_start(rows[:, 2 * i:2 * i + 2, :],
                             xp_dram.rearrange("(i p) d -> p i d", p=P)[:, 2 * i:2 * i + 2, :]
                             ).then_inc(ld_rows[i], 16)
            for e in range(NHOME, E):
                if (e - NHOME) % XG == 0:
                    wait_filled(sp, ("dn", (e - NHOME) // XG))
                load_expert(e, ld_experts[e // XG])
            yv = y_dram.rearrange("(i p) d -> p i d", p=P)
            for i in range(NS // 2):
                wait_emptied(sp, ("yT", i))
                sp.dma_start(yv[:, 2 * i:2 * i + 2, :], rows[:, 2 * i:2 * i + 2, :]).then_inc(sg["y_stored"], 16)
            ov = out.rearrange("b (j p) d -> p (b j) d", p=P)
            for t in range(NT):
                sp.wait_ge(sg["combined"], t + 1)
                sp.dma_start(ov[:, t, :], xres[:, t, :]).then_inc(sg["out_stored"], 16)
            sp.wait_ge(sg["out_stored"], 16 * NT)

        @block.tensor
        def _(pe):
            def mm(out_, lhsT, rhs, first=True, last=True):
                return nc.tensor.matmul(out_, lhsT, rhs, start=first, stop=last)

            def turn(out_, in_, idn=None):
                return nc.tensor.transpose(out_, in_, ident if idn is None else idn)

            def bf(item):
                return bank(item).bitcast(BF16)

            for step in steps:
                kind, a = step[0], step[1:]
                if kind == "setup":
                    pe.wait_ge(ld["consts"], 16)
                elif kind == "hT":
                    t, = a
                    pe.wait_ge(sg["h_ready"], nth("ln1", t // NJ) + 1)
                    wait_empty(pe, step)
                    for k in range(KD):
                        last = turn(bank(step)[:, k * P:(k + 1) * P], hn_f[:, t % 2, k * P:(k + 1) * P])
                    fills(last, step)
                elif kind == "fused":
                    t, = a
                    if t == 0:
                        pe.wait_ge(ld["wkva"], 16)
                    wait_emptied(pe, ("hT", t))
                    wait_empty(pe, step)
                    for k in range(KD):
                        last = mm(bank(step)[:, 0:QL + KL + DR], hT_f[:, k * P:(k + 1) * P], wkva[:, k, :],
                                  k == 0, k == KD - 1)
                    fills(last, step)
                elif kind == "latT":
                    t, = a
                    pe.wait_ge(sg["lat_ready"], t + 1)
                    wait_empty(pe, step)
                    turn(bank(step)[:, 0:P], qn[:, 0:P])
                    turn(bank(step)[:, P:2 * P], kv[:, t, :])
                    fills(turn(bank(step)[0:64, 2 * P:3 * P], qn[:, P:QL]), step)
                elif kind == "prepT":
                    h, = a
                    if h == 0:
                        pe.wait_ge(ld["wkv"], 16)
                        pe.wait_ge(ld["wq"], 32)
                    wait_empty(pe, step)
                    turn(bank(step)[:, 0:P], wq0[:, h, :])
                    turn(bank(step)[:, P:2 * P], wkq[:, h, 0:DN])
                    fills(turn(bank(step)[:, 256:320], wkq[0:KL, h, DN:], ident[0:KL, 0:KL]), step)
                elif kind == "prepM":
                    p, = a
                    if p == 0:
                        pe.wait_ge(ld["wo"], 16)
                    wait_emptied(pe, ("prepT", 2 * p))
                    wait_emptied(pe, ("prepT", 2 * p + 1))
                    wait_empty(pe, step)
                    for i in range(2):
                        wkT = wT[:, i, P:P + KL]
                        mm(bank(step)[:, i * KL:(i + 1) * KL], wT[:, i, 0:P], wkT)
                        mm(bank(step)[0:64, 128 + i * KL:128 + (i + 1) * KL], wT[:, i, P + KL:2 * P], wkT)
                        last = mm(bank(step)[i * KL:(i + 1) * KL, 256:512], wT[:, i, 256:320], wo[:, 2 * p + i, :])
                    fills(last, step)
                elif kind == "q":
                    t, c = a
                    if nth(*step) == 0:
                        for p in range(NH // 2):
                            wait_emptied(pe, ("prepM", p))
                        pe.wait_ge(ld["rope_cols"], 32)
                    wait_emptied(pe, ("latT", t))
                    wait_empty(pe, step)
                    mm(bank(step), qn0[:, t, :], wf0[:, HC * c:HC * (c + 1), :], True, False)
                    fills(mm(bank(step), qn1[:, t, :], wf1[:, HC * c:HC * (c + 1), :], False, True), step)
                elif kind == "qT":
                    u = nth(*step)
                    pe.wait_ge(sg["rope_added"], u + 1)
                    wait_empty(pe, step)
                    for i in range(HC):
                        last = turn(bank(step)[:, i * P:(i + 1) * P], qs[:, u % 2, i * P:(i + 1) * P])
                    fills(last, step)
                elif kind == "scores":
                    hn, = a
                    b, n = hn // NH, hn % NH
                    if n == 0:
                        for j in range(NJ):
                            wait_emptied(pe, ("latT", NJ * b + j))
                        pe.wait_ge(sg["consts_ready"], 1)
                    if n % HC == 0:
                        for j in range(NJ):
                            wait_emptied(pe, ("qT", NJ * b + j, n // HC))
                    if hn >= 2:
                        pe.wait_ge(sg["exp_done"], hn - 1)
                    o = ps_s[:, hn % 2, :]
                    mm(o[:, 0:P], qT[:, b % 2, n, 0:P], kT[:, b, 0:P], True, False)
                    mm(o[:, 0:P], id_bf[:], mask_bf[:], False, True)
                    mm(o[:, P:3 * P], qT[:, b % 2, n, P:2 * P], kT[:, b, :], True, False)
                    mm(o[:, 2 * P:3 * P], id_bf[:], mask_bf[:], False, True).then_inc(sg["scores_ready"], 1)
                elif kind == "probsT":
                    hn, = a
                    pe.wait_ge(sg["exp_done"], hn + 1)
                    if hn >= 1:
                        pe.wait_ge(sg["probsT_copied"], hn)
                    for i in range(3):
                        last = turn(ps_pt[:, i * P:(i + 1) * P], probs[:, hn % 2, i * P:(i + 1) * P])
                    last.then_inc(sg["probsT_done"], 1)
                elif kind == "pv":
                    hn, = a
                    b, n8 = hn // NH, hn % GH
                    pe.wait_ge(sg["probsT_copied"], hn + 1)
                    if n8 == 0 and hn:
                        pe.wait_ge(sg["heads_normed"], hn // GH)
                    cols = slice(n8 * KL, (n8 + 1) * KL)
                    pT = probsT[:, hn % 2, :]
                    mm(ps_o[:, 0, cols], pT[:, 0:P], kv[:, 2 * b, 0:KL])
                    mm(ps_o[:, 1, cols], pT[:, P:2 * P], kv[:, 2 * b, 0:KL], True, False)
                    mm(ps_o[:, 1, cols], pT[:, 2 * P:3 * P], kv[:, 2 * b + 1, 0:KL], False, True
                       ).then_inc(sg["pv_done"], 1)
                elif kind == "oT":
                    t, g = a
                    G = (t // NJ) * 2 + g
                    pe.wait_ge(sg["heads_normed"], G + 1)
                    wait_empty(pe, step)
                    for i in range(4):
                        last = turn(bank(step)[:, i * P:(i + 1) * P], on[:, G % 2, t % 2, i * P:(i + 1) * P])
                    fills(last, step)
                elif kind == "y":
                    t, = a
                    for g in range(2):
                        wait_emptied(pe, ("oT", t, g))
                    wait_empty(pe, step)
                    for i in range(NH // 2):
                        last = mm(bank(step)[:, 0:D], oT[:, t % 2, i, :], w_mo[:, i, :], i == 0, i == NH // 2 - 1)
                    fills(last, step)
                elif kind == "wx":
                    b, = a
                    item = ("fsT", b)
                    if b == 0:
                        pe.wait_ge(ld["fs"], 16)
                        pe.wait_ge(ld["cx"], 16)
                    wait_empty(pe, item)
                    for k in range(KD):
                        for o in range(2):
                            last = turn(bank(item)[:, k * 256 + o * P:k * 256 + (o + 1) * P],
                                        fs[:, b, o, k * P:(k + 1) * P])
                    fills(last, item)
                    item = ("cxT", b)
                    wait_empty(pe, item)
                    for o in range(2):
                        last = turn(bank(item)[:, o * P:(o + 1) * P], cx[:, b, o, :])
                    fills(last, item)
                elif kind == "rwT":
                    pe.wait_ge(ld["rw"], 16)
                    wait_empty(pe, step)
                    for k in range(KD):
                        last = turn(bank(step)[:, k * E:(k + 1) * E], rw[0:E, k * P:(k + 1) * P], ident[0:E, 0:E])
                    fills(last, step)
                elif kind == "shT":
                    i, = a
                    if i == 0:
                        pe.wait_ge(ld["sh"], 48)
                    wait_empty(pe, step)
                    for k in range(KD):
                        for o in range(2):
                            last = turn(bank(step)[:, k * 256 + o * P:k * 256 + (o + 1) * P],
                                        shw[:, i, o, k * P:(k + 1) * P])
                    fills(last, step)
                elif kind == "x1":
                    b, = a
                    item = ("xT", b)
                    pe.wait_ge(sg["h_ready"], nth("x0", b) + 1)
                    wait_empty(pe, item)
                    for k in range(KD):
                        for j in range(NJ):
                            last = turn(bank(item)[:, k * 256 + j * P:k * 256 + (j + 1) * P],
                                        h2[:, j, k * P:(k + 1) * P])
                    fills(last, item)
                elif kind == "x3":
                    b, = a
                    for item, src in ((("xs", b), xsT), (("ws", b), wsT)):
                        if item[0] == "xs":
                            wait_emptied(pe, ("xT", b))
                        else:
                            pe.wait_ge(sg["scaledT_w"], b + 1)
                        wait_empty(pe, item)
                        for j in range(NJ):
                            for k in range(KD):
                                last = turn(bank(item)[:, j * 256 + k * P:j * 256 + (k + 1) * P],
                                            src[:, k * 256 + j * P:k * 256 + (j + 1) * P])
                        fills(last, item)
                elif kind == "x5":
                    b, = a
                    item = ("xqT", b)
                    pe.wait_ge(sg["q_ready"], b + 1)
                    wait_empty(pe, item)
                    for i in range(4):
                        for k in range(KD):
                            o = (i // 2) * 512 + k * 256 + (i % 2) * P
                            last = turn(bf(item)[:, o:o + P], qb[:, i, k * P:(k + 1) * P], id_bf[:])
                    fills(last, item)
                elif kind == "x6":
                    b, = a
                    item = ("xb", b)
                    wait_empty(pe, item)
                    for j in range(NJ):
                        last = mm(bank(item)[:, j * P:(j + 1) * P],
                                  sm[:, b, 10 + j:11 + j].broadcast_to([P, P]), ident)
                    fills(last, item)
                    item = ("h1", b)
                    wait_emptied(pe, ("xqT", b))
                    wait_empty(pe, item)
                    f = qTs[:].rearrange("p a d -> p (a d)")
                    for oh_ in range(2):
                        for k in range(KD):
                            w0 = 512 + k * 256 + oh_ * P
                            last = mm(bank(item)[:, oh_ * 256:(oh_ + 1) * 256], f[:, w0:w0 + P],
                                      f[:, k * 256:(k + 1) * 256], k == 0, k == KD - 1)
                    fills(last, item)
                elif kind == "x9":
                    b, = a
                    item = ("as", b)
                    pe.wait_ge(sg["scaledT_a"], b + 1)
                    pe.wait_ge(sg["scaledT_c"], b + 1)
                    wait_empty(pe, item)
                    for i in range(4):
                        src = xsT if i < 2 else wsT
                        last = turn(bank(item)[:, i * P:(i + 1) * P], src[:, (i % 2) * P:(i % 2 + 1) * P])
                    fills(last, item)
                elif kind == "x11":
                    b, = a
                    item = ("aqT", b)
                    pe.wait_ge(sg["q2_ready"], b + 1)
                    wait_empty(pe, item)
                    f = qb[:].rearrange("p a d -> p (a d)")
                    for i in range(4):
                        last = turn(bf(item)[:, i * P:(i + 1) * P], f[:, i * P:(i + 1) * P], id_bf[:])
                    fills(last, item)
                    item = ("wb", b)
                    wait_empty(pe, item)
                    for o in range(2):
                        last = mm(bank(item)[:, o * P:(o + 1) * P],
                                  sm[:, b, 25 + o:26 + o].broadcast_to([P, P]), ident)
                    fills(last, item)
                elif kind == "x12":
                    b, = a
                    item = ("h2", b)
                    wait_emptied(pe, ("aqT", b))
                    wait_empty(pe, item)
                    f = qTs[:].rearrange("p a d -> p (a d)")
                    for j in range(NJ):
                        last = mm(bank(item)[:, j * 256:(j + 1) * 256], f[:, j * P:(j + 1) * P], f[:, 256:512])
                    fills(last, item)
                elif kind == "r1":
                    b, = a
                    item = ("h3T", b)
                    pe.wait_ge(sg["h_ready"], nth("r0", b) + 1)
                    wait_empty(pe, item)
                    for k in range(KD):
                        for j in range(NJ):
                            last = turn(bank(item)[:, k * 256 + j * P:k * 256 + (j + 1) * P],
                                        h3[:, b % 2, j, k * P:(k + 1) * P])
                    fills(last, item)
                elif kind == "r2":
                    b, = a
                    item = ("logit", b)
                    wait_emptied(pe, ("rwT",))
                    wait_emptied(pe, ("h3T", b))
                    wait_empty(pe, item)
                    for j in range(NJ):
                        for k in range(KD):
                            last = mm(bank(item)[:, j * E:(j + 1) * E], h3T[:, b, k, j * P:(j + 1) * P],
                                      rwT[:, k, :], k == 0, k == KD - 1)
                    fills(last, item)
                elif kind == "r4":
                    b, = a
                    item = ("pos", b)
                    pe.wait_ge(sg["chosen_ready"], b + 1)
                    wait_empty(pe, item)
                    for j in range(NJ):
                        t = NJ * b + j
                        last = mm(bank(item)[:, j * E:(j + 1) * E], tri_bf[:], chosen[:, t, :], True, t == 0)
                        for tt in range(t):
                            last = mm(bank(item)[:, j * E:(j + 1) * E], ones_bf[:], chosen[:, tt, :],
                                      False, tt == t - 1)
                    fills(last, item)
                elif kind == "s0":
                    b, = a
                    for i, name in enumerate(("sg", "su")):
                        item = (name, b)
                        wait_emptied(pe, ("shT", i))
                        wait_emptied(pe, ("h3T", b))
                        wait_empty(pe, item)
                        for oh_ in range(2):
                            for k in range(KD):
                                last = mm(bank(item)[:, oh_ * 256:(oh_ + 1) * 256],
                                          shT[:, i, k, oh_ * P:(oh_ + 1) * P], h3T[:, b, k, :], k == 0, k == KD - 1)
                        fills(last, item)
                elif kind == "s2":
                    b, = a
                    item = ("sd", b)
                    wait_emptied(pe, ("shT", 2))
                    wait_emptied(pe, ("su", b))
                    wait_empty(pe, item)
                    for j in range(NJ):
                        for k in range(2):
                            last = mm(bank(item)[:, j * 256:(j + 1) * 256], act_s[:, k, j * P:(j + 1) * P],
                                      shT[:, 2, k, :], k == 0, k == 1)
                    fills(last, item)
                elif kind == "xpT":
                    i, = a
                    pe.wait_ge(ld_rows[i], 16)
                    wait_empty(pe, step)
                    for k in range(KD):
                        for s in range(2):
                            last = turn(bank(step)[:, k * 256 + s * P:k * 256 + (s + 1) * P],
                                        rows[:, 2 * i + s, k * P:(k + 1) * P])
                    fills(last, step)
                elif kind == "gate_up":
                    g, = a
                    item = ("gu", g)
                    pe.wait_ge(ld_experts[g], 16 * 3 * XG)
                    for i in range((g * XG * CAP) // 256, ((g + 1) * XG * CAP - 1) // 256 + 1):
                        wait_emptied(pe, ("xpT", i))
                    wait_empty(pe, item)
                    for e in range(XG):
                        s0 = (g * XG + e) * CAP
                        for i, w in enumerate((gate_of(g * XG + e), up_of(g * XG + e))):
                            for k in range(KD):
                                c0 = i * XG * CAP + e * CAP
                                last = mm(bank(item)[:, c0:c0 + CAP], w[:, k, :], xpT[:, k, s0:s0 + CAP],
                                          k == 0, k == KD - 1)
                    fills(last, item)
                elif kind == "down":
                    g, = a
                    item = ("dn", g)
                    wait_emptied(pe, ("gu", g))
                    wait_empty(pe, item)
                    for e in range(XG):
                        for k in range(KD):
                            c0 = k * XG * CAP + e * CAP
                            last = mm(bank(item)[:, c0:c0 + CAP], down_of(g * XG + e)[:, k * P:(k + 1) * P],
                                      hE[:, g % 2, e * CAP:(e + 1) * CAP])
                    fills(last, item)
                elif kind == "yT":
                    i, = a
                    wait_emptied(pe, ("dn", -(-(i + 1) * 256 // (XG * CAP)) - 1))
                    wait_empty(pe, step)
                    for s in range(2):
                        for k in range(KD):
                            last = turn(bank(step)[:, s * 256 + k * P:s * 256 + (k + 1) * P],
                                        yT[k][:, (2 * i + s) * P:(2 * i + s + 1) * P])
                    fills(last, step)

        @block.scalar
        def _(act):
            def copy(out_, in_, scale=1.0):
                return nc.scalar.activation(out_, in_, ACT.Copy, scale=scale)

            for step in steps:
                kind, a = step[0], step[1:]
                if kind == "hT":
                    t, = a
                    wait_filled(act, step)
                    if t >= 1:
                        wait_filled(act, ("fused", t - 1))
                    empties(copy(hT_f, bank(step)[:, 0:256]), step)
                elif kind == "fused":
                    t, = a
                    wait_filled(act, step)
                    if t >= 1:
                        act.wait_ge(sg["squares_ready"], t)
                    nc.scalar.activation(sq[:, 0:QL], bank(step)[:, 0:QL], ACT.Square, scale=float(QL) ** -0.5,
                                         accum_out=ssq[:, t, 0:1])
                    nc.scalar.activation(sq[:, QL:QL + KL], bank(step)[:, QL:QL + KL], ACT.Square,
                                         scale=float(KL) ** -0.5, accum_out=ssq[:, t, 1:2]
                                         ).then_inc(sg["squares_ready"], 1)
                elif kind == "latT":
                    t, = a
                    wait_filled(act, step)
                    copy(qn0[:, t, :], bank(step)[:, 0:P])
                    copy(kT[:, t // 2, (t % 2) * P:(t % 2 + 1) * P], bank(step)[:, P:2 * P])
                    empties(copy(qn1[:, t, :], bank(step)[0:64, 2 * P:3 * P]), step)
                elif kind == "prepT" and a[0] % 2 == 0:
                    h, = a
                    wait_filled(act, step)
                    if h >= 2:
                        wait_filled(act, ("prepM", h // 2 - 1))
                    empties(copy(wT[:, 0, :], bank(step)[:, 0:320]), step)
                elif kind == "q":
                    t, c = a
                    u = nth(*step)
                    wait_filled(act, step)
                    if u >= 2:
                        wait_filled(act, q_order[u - 2])
                    empties(copy(qs[:, u % 2], bank(step), SM_SCALE), step)
                elif kind == "qT":
                    t, c = a
                    b = t // NJ
                    wait_filled(act, step)
                    if b >= 2:
                        act.wait_ge(sg["scores_ready"], NH * (b - 1))
                    empties(copy(qT[:, b % 2, HC * c:HC * (c + 1), (t % 2) * P:(t % 2 + 1) * P],
                                 bank(step).rearrange("p (h m) -> p h m", h=HC)), step)
                elif kind == "scores":
                    hn, = a
                    act.wait_ge(sg["max_ready"], hn + 1)
                    if hn >= 2:
                        act.wait_ge(sg["probsT_done"], hn - 1)
                    G, n8 = hn // GH, hn % GH
                    s = ps_s[:, hn % 2, :]
                    nc.scalar.activation(probs[:, hn % 2, 0:P], s[:, 0:P], ACT.Exp, bias=nmax[:, hn, 0:1],
                                         accum_out=psum_[:, G, 0, n8:n8 + 1])
                    nc.scalar.activation(probs[:, hn % 2, P:3 * P], s[:, P:3 * P], ACT.Exp, bias=nmax[:, hn, 1:2],
                                         accum_out=psum_[:, G, 1, n8:n8 + 1]).then_inc(sg["exp_done"], 1)
                elif kind == "oT":
                    t, g = a
                    wait_filled(act, step)
                    if t >= 2:
                        wait_filled(act, ("y", t - 2))
                    empties(copy(oT[:, t % 2, 4 * g:4 * g + 4, :], bank(step).rearrange("p (h m) -> p h m", h=4)),
                            step)
                elif kind == "wx":
                    b, = a
                    if b >= 1:
                        act.wait_ge(sg["scaledT_w"], b)
                        act.wait_ge(sg["scaledT_c"], b)
                    wait_filled(act, ("fsT", b))
                    empties(copy(fsT[:], bank(("fsT", b))), ("fsT", b))
                    wait_filled(act, ("cxT", b))
                    empties(copy(cxT[:], bank(("cxT", b))[:, 0:256]), ("cxT", b))
                elif kind == "rwT":
                    wait_filled(act, step)
                    empties(copy(rwT[:].rearrange("p k e -> p (k e)"), bank(step)[:, 0:KD * E]), step)
                elif kind == "shT":
                    i, = a
                    wait_filled(act, step)
                    empties(copy(shT[:, i].rearrange("p k d -> p (k d)"), bank(step)), step)
                elif kind == "x2":
                    b, = a
                    act.wait_ge(sg["smooth_ready"], b + 1)
                    if b >= 1:
                        wait_filled(act, ("as", b - 1))
                    for k in range(KD):
                        last = copy(xsT[:, k * 256:(k + 1) * 256], bank(("xT", b))[:, k * 256:(k + 1) * 256],
                                    sm[:, b, 8 + k:9 + k])
                    empties(last, ("xT", b))
                elif kind == "x4":
                    b, = a
                    act.wait_ge(sg["inv_ready"], b + 1)
                    if b >= 1:
                        act.wait_ge(sg["q2_ready"], b)
                    for i, item in enumerate((("xs", b), ("ws", b))):
                        for j in range(2):
                            last = copy(qa[:, 2 * i + j, :], bank(item)[:, j * 256:(j + 1) * 256],
                                        sm[:, b, 14 + 2 * i + j:15 + 2 * i + j])
                        empties(last, item)
                elif kind == "x5":
                    b, = a
                    wait_filled(act, ("xqT", b))
                    if b >= 1:
                        wait_filled(act, ("h2", b - 1))
                    empties(copy(qTs[:].rearrange("p a d -> p (a d)"), bank(("xqT", b)).bitcast(BF16)), ("xqT", b))
                elif kind == "x6":
                    b, = a
                    wait_filled(act, ("xb", b))
                    if b >= 1:
                        wait_emptied(act, ("h1", b - 1))
                    empties(copy(sbc[:, 0, :], bank(("xb", b))[:, 0:256]), ("xb", b))
                elif kind == "x7":
                    b, = a
                    wait_emptied(act, ("h1", b))
                    nc.scalar.activation(gu[:, 2, :], gu[:, 0, :], ACT.Exp, scale=-1.0).then_inc(sg["exp_gate"], 1)
                elif kind == "x8":
                    b, = a
                    act.wait_ge(sg["smooth_ready2"], b + 1)
                    wait_filled(act, ("xs", b))
                    copy(xsT[:, 0:256], gu[:, 3, :], sm[:, b, 22:23]).then_inc(sg["scaledT_a"], 1)
                elif kind == "x10":
                    b, = a
                    act.wait_ge(sg["inv2_ready"], b + 1)
                    act.wait_ge(sg["q_ready"], b + 1)
                    f = reg_r[:, 0:1024]
                    for i in range(4):
                        last = copy(f[:, i * P:(i + 1) * P], bank(("as", b))[:, i * P:(i + 1) * P],
                                    sm[:, b, 27 + i:28 + i])
                    empties(last, ("as", b))
                elif kind == "x11":
                    b, = a
                    wait_filled(act, ("aqT", b))
                    wait_filled(act, ("h1", b))
                    empties(copy(qTs[:].rearrange("p a d -> p (a d)")[:, 0:512],
                                 bank(("aqT", b)).bitcast(BF16)[:, 0:512]), ("aqT", b))
                    wait_filled(act, ("wb", b))
                    empties(copy(sbc[:, 1, :], bank(("wb", b))[:, 0:256]), ("wb", b))
                elif kind == "r1":
                    b, = a
                    wait_filled(act, ("h3T", b))
                    empties(copy(h3T[:, b].rearrange("p k t -> p (k t)"), bank(("h3T", b))), ("h3T", b))
                elif kind == "r2":
                    b, = a
                    wait_filled(act, ("logit", b))
                    if b >= 1:
                        act.wait_ge(sg["slots_ready"], b)
                    empties(nc.scalar.activation(sc[:, 0, :], bank(("logit", b))[:, 0:NJ * E], ACT.Exp, scale=-1.0),
                            ("logit", b))
                elif kind == "s0":
                    b, = a
                    wait_filled(act, ("sg", b))
                    if b >= 1:
                        wait_emptied(act, ("su", b - 1))
                    nc.scalar.activation(es[:, 0, :], bank(("sg", b)), ACT.Exp, scale=-1.0
                                         ).then_inc(sg["shared_exp"], 1)
                elif kind == "xpT" and a[0] % 2 == 0:
                    i, = a
                    wait_filled(act, step)
                    empties(copy(xpT[:, :, i * 256:(i + 1) * 256],
                                 bank(step).rearrange("p (k s) -> p k s", k=KD)), step)
                elif kind == "gate_up":
                    g, = a
                    wait_filled(act, ("gu", g))
                    if g >= 2:
                        wait_emptied(act, ("gu", g - 2))
                    nc.scalar.activation(ee[:, g % 2, :], bank(("gu", g))[:, 0:XG * CAP], ACT.Exp, scale=-1.0
                                         ).then_inc(sg["expert_exp"], 1)
                elif kind == "down":
                    g, = a
                    wait_filled(act, ("dn", g))
                    for k in range(KD):
                        last = copy(yT[k][:, g * XG * CAP:(g + 1) * XG * CAP],
                                    bank(("dn", g))[:, k * XG * CAP:(k + 1) * XG * CAP])
                    empties(last, ("dn", g))

        @block.vector
        def _(dve):
            v = nc.vector
            chain = [0]

            def link(ins):
                chain[0] += 1
                ins.then_inc(sg["dve_chain"], 1)
                dve.wait_ge(sg["dve_chain"], chain[0])

            def layernorm(tag, b, step, dst, free):
                i = nth(*step)
                for j in range(NJ):
                    link(v.bn_stats(stats[:, j, :], xres[:, NJ * b + j, :]))
                for j in range(NJ):
                    last = v.bn_aggr(mv[:, tag, NJ * b + j, :], stats[:, j, :])
                last.then_inc(sg["ln_stats"], 1)
                free()
                dve.wait_ge(sg["ln_rstd"], i + 1)
                for j in range(NJ):
                    t = NJ * b + j
                    last = v.tensor_scalar(dst(j), xres[:, t, :], mv[:, tag, t, 0:1], rstd[:, tag, t:t + 1],
                                           ALU.subtract, ALU.mult)
                last.then_inc(sg["h_ready"], 1)

            for step in steps:
                kind, a = step[0], step[1:]
                if kind == "setup":
                    v.memset(zeros, 0.0).then_inc(sg["zeros_ready"], 1)
                    link(v.memset(ones_bf[:], 1.0))
                elif kind == "ln1":
                    b, = a
                    dve.wait_ge(ld[f"x{b}"], 16)

                    def free():
                        if b >= 1:
                            for j in range(NJ):
                                wait_filled(dve, ("hT", NJ * (b - 1) + j))
                    layernorm(0, b, step, lambda j: hn_f[:, j, :], free)
                    if b == 0:
                        dve.wait_ge(ld["consts"], 16)
                        v.tensor_copy(id_bf[:], ident)
                        v.tensor_copy(mask_bf[:], c_(C_MASK, P))
                        v.tensor_copy(tri_bf[:], c_(C_TRI, P)).then_inc(sg["consts_ready"], 1)
                elif kind == "fused":
                    t, = a
                    if t == 0:
                        dve.wait_ge(ld["gam"], 32)
                    dve.wait_ge(sg["rms_ready"], t + 1)
                    if t >= 1:
                        wait_filled(dve, ("latT", t - 1))
                    pb = bank(step)
                    v.scalar_tensor_tensor(qn, pb[:, 0:QL], rrms[:, t, 0:1], gam_q[:], ALU.mult, ALU.mult)
                    v.scalar_tensor_tensor(kv[:, t, 0:KL], pb[:, QL:QL + KL], rrms[:, t, 1:2], gam_kv[:],
                                           ALU.mult, ALU.mult)
                    kp = pb[:, QL + KL:QL + KL + DR]
                    o = (t % NJ) * DR
                    v.tensor_tensor(kr[:, 0, :], kp, c_(C_COS + o, DR), ALU.mult)
                    empties(v.tensor_tensor(kr[:, 1, :].rearrange("p (two x) -> p two x", two=2)[:, ::-1, :],
                                            kp.rearrange("p (two x) -> p two x", two=2),
                                            c_(C_SIN + o, DR).rearrange("p (two x) -> p two x", two=2), ALU.mult),
                            step)
                    wait_emptied(dve, step)
                    v.tensor_tensor(kv[:, t, KL:], kr[:, 0, :], kr[:, 1, :], ALU.add).then_inc(sg["lat_ready"], 1)
                elif kind == "prepT" and a[0] % 2 == 1:
                    h, = a
                    wait_filled(dve, step)
                    if h >= 2:
                        wait_filled(dve, ("prepM", h // 2 - 1))
                    empties(v.tensor_copy(wT[:, 1, :], bank(step)[:, 0:320]), step)
                elif kind == "prepM":
                    p, = a
                    wait_filled(dve, step)
                    pb = bank(step)
                    v.tensor_copy(wf0[:, 2 * p:2 * p + 2, 0:KL], pb[:, 0:128].rearrange("p (h m) -> p h m", h=2))
                    v.tensor_copy(wf1[:, 2 * p:2 * p + 2, 0:KL],
                                  pb[0:64, 128:256].rearrange("p (h m) -> p h m", h=2))
                    empties(v.tensor_copy(w_mo[:, p, :], pb[:, 256:512]), step)
                elif kind == "q":
                    t, c = a
                    u = nth(*step)
                    wait_emptied(dve, step)
                    if u >= 2:
                        dve.wait_ge(sg["rope_added"], u - 1)
                    o = (t % NJ) * DR
                    qp = qs[:, u % 2].rearrange("p (h m) -> p h m", h=HC)[:, :, KL:]
                    v.tensor_tensor(
                        qr[:, u % 2].rearrange("p (h two x) -> p h two x", h=HC, two=2)[:, :, ::-1, :],
                        qp.rearrange("p h (two x) -> p h two x", two=2),
                        c_(C_SIN + o, DR).rearrange("p (o two x) -> p o two x", o=1, two=2
                                                    ).broadcast_to([P, HC, 2, DR // 2]), ALU.mult)
                    v.tensor_tensor(qp, qp,
                                    c_(C_COS + o, DR).rearrange("p (o x) -> p o x", o=1).broadcast_to([P, HC, DR]),
                                    ALU.mult).then_inc(sg["rope_parts"], 1)
                elif kind == "scores":
                    hn, = a
                    dve.wait_ge(sg["scores_ready"], hn + 1)
                    s = ps_s[:, hn % 2, :]
                    v.tensor_reduce(nmax[:, hn, 0:1], s[:, 0:P], AX.X, ALU.max, negate=True)
                    v.tensor_reduce(nmax[:, hn, 1:2], s[:, P:3 * P], AX.X, ALU.max, negate=True
                                    ).then_inc(sg["max_ready"], 1)
                elif kind == "probsT":
                    hn, = a
                    dve.wait_ge(sg["probsT_done"], hn + 1)
                    if hn >= 2:
                        dve.wait_ge(sg["pv_done"], hn - 1)
                    v.tensor_copy(probsT[:, hn % 2, :], ps_pt[:, 0:384]).then_inc(sg["probsT_copied"], 1)
                elif kind == "norm":
                    G, = a
                    dve.wait_ge(sg["pv_done"], GH * (G + 1))
                    link(v.reciprocal(rsum[:, G], psum_[:, G]))
                    if G == 0:
                        dve.wait_ge(sg["xp_zeroed"], 16 * (NS // 2))
                    if G >= 2:
                        for j in range(NJ):
                            wait_filled(dve, ("oT", NJ * ((G - 2) // 2) + j, G % 2))
                    for j in range(NJ):
                        last = v.tensor_tensor(
                            on[:, G % 2, j, :].rearrange("p (h c) -> p h c", h=GH),
                            ps_o[:, j, :].rearrange("p (h c) -> p h c", h=GH),
                            rsum[:, G, j, :].rearrange("p (h o) -> p h o", o=1).broadcast_to([P, GH, KL]), ALU.mult)
                    last.then_inc(sg["heads_normed"], 1)
                elif kind == "y":
                    t, = a
                    wait_filled(dve, step)
                    empties(v.tensor_tensor(xres[:, t, :], bank(step)[:, 0:D], xres[:, t, :], ALU.add), step)
                elif kind == "wx":
                    b, = a
                    wait_emptied(dve, ("fsT", b))
                    v.tensor_reduce(rden[:, b, 0:2], fsT[:].rearrange("p (k o) -> p k o", k=KD), AX.X, ALU.max,
                                    apply_absolute_value=True)
                    wait_emptied(dve, ("cxT", b))
                    link(v.tensor_reduce(rden[:, b, 2:3], cxT[:], AX.X, ALU.max, apply_absolute_value=True))
                    link(v.tensor_scalar(rden[:, b, :], rden[:, b, :], EPS_Q, None, ALU.max))
                    link(v.reciprocal(rden[:, b, :], rden[:, b, :]))
                elif kind == "x0":
                    b, = a
                    for j in range(NJ):
                        wait_emptied(dve, ("y", NJ * b + j))

                    def free():
                        if b >= 1:
                            wait_filled(dve, ("xT", b - 1))
                    layernorm(1, b, step, lambda j: h2[:, j, :], free)
                elif kind == "x1":
                    b, = a
                    item = ("xT", b)
                    wait_filled(dve, item)
                    link(v.tensor_reduce(sm[:, b, 0:2], bank(item).rearrange("p (k t) -> p k t", k=KD), AX.X, ALU.max,
                                         apply_absolute_value=True))
                    v.scalar_tensor_tensor(sm[:, b, 2:4], sm[:, b, 0:2], EPS_Q, rden[:, b, 0:2], ALU.max, ALU.mult
                                           ).then_inc(sg["ratio_ready"], 1)
                    dve.wait_ge(sg["smooth_root"], b + 1)
                    link(v.tensor_scalar(sm[:, b, 6:8], sm[:, b, 4:6], EPS_Q, None, ALU.max))
                    v.reciprocal(sm[:, b, 8:10], sm[:, b, 6:8]).then_inc(sg["smooth_ready"], 1)
                elif kind == "x3":
                    b, = a
                    for i, item in enumerate((("xs", b), ("ws", b))):
                        wait_filled(dve, item)
                        last = v.tensor_reduce(sm[:, b, 10 + 2 * i:12 + 2 * i],
                                               bank(item).rearrange("p (j d) -> p j d", j=2), AX.X, ALU.max,
                                               apply_absolute_value=True)
                    link(last)
                    link(v.tensor_scalar(sm[:, b, 10:14], sm[:, b, 10:14], EPS_Q, 1.0 / QMAX, ALU.max, ALU.mult))
                    v.reciprocal(sm[:, b, 14:18], sm[:, b, 10:14]).then_inc(sg["inv_ready"], 1)
                elif kind == "x4":
                    b, = a
                    for item in (("xs", b), ("ws", b)):
                        wait_emptied(dve, item)
                    link(v.tensor_scalar(qa, qa, QMAX, -QMAX, ALU.min, ALU.max))
                    if b >= 1:
                        wait_filled(dve, ("aqT", b - 1))
                    v.tensor_scalar(qb[:], qa, ROUND, ROUND, ALU.add, ALU.subtract).then_inc(sg["q_ready"], 1)
                elif kind == "x6":
                    b, = a
                    item = ("h1", b)
                    wait_filled(dve, item)
                    wait_emptied(dve, ("xb", b))
                    for i in range(2):
                        last = v.scalar_tensor_tensor(gu[:, i, :], bank(item)[:, i * 256:(i + 1) * 256],
                                                      sm[:, b, 12 + i:13 + i], sbc[:, 0, :], ALU.mult, ALU.mult)
                    empties(last, item)
                elif kind == "x7":
                    b, = a
                    dve.wait_ge(sg["exp_gate"], b + 1)
                    link(v.tensor_scalar(gu[:, 2, :], gu[:, 2, :], 1.0, None, ALU.add))
                    v.tensor_tensor(gu[:, 3, :], gu[:, 0, :], gu[:, 1, :], ALU.mult)
                    link(v.reciprocal(gu[:, 2, :], gu[:, 2, :]))
                    v.tensor_tensor(gu[:, 3, :], gu[:, 3, :], gu[:, 2, :], ALU.mult).then_inc(sg["act_ready"], 1)
                elif kind == "x8":
                    b, = a
                    dve.wait_ge(sg["act_ready"], b + 1)
                    link(v.tensor_reduce(sm[:, b, 18:19], gu[:, 3, :], AX.X, ALU.max, apply_absolute_value=True))
                    v.scalar_tensor_tensor(sm[:, b, 19:20], sm[:, b, 18:19], EPS_Q, rden[:, b, 2:3], ALU.max,
                                           ALU.mult).then_inc(sg["ratio2_ready"], 1)
                    dve.wait_ge(sg["smooth_root2"], b + 1)
                    link(v.tensor_scalar(sm[:, b, 21:22], sm[:, b, 20:21], EPS_Q, None, ALU.max))
                    v.reciprocal(sm[:, b, 22:23], sm[:, b, 21:22]).then_inc(sg["smooth_ready2"], 1)
                elif kind == "x9":
                    b, = a
                    item = ("as", b)
                    wait_filled(dve, item)
                    link(v.tensor_reduce(sm[:, b, 23:27], bank(item).rearrange("p (i m) -> p i m", i=4), AX.X, ALU.max,
                                         apply_absolute_value=True))
                    link(v.tensor_scalar(sm[:, b, 23:27], sm[:, b, 23:27], EPS_Q, 1.0 / QMAX, ALU.max, ALU.mult))
                    v.reciprocal(sm[:, b, 27:31], sm[:, b, 23:27]).then_inc(sg["inv2_ready"], 1)
                elif kind == "x10":
                    b, = a
                    wait_emptied(dve, ("as", b))
                    fa = reg_r[:, 0:1024][:, 0:512]
                    fb = qb[:].rearrange("p a d -> p (a d)")[:, 0:512]
                    link(v.tensor_scalar(fa, fa, QMAX, -QMAX, ALU.min, ALU.max))
                    wait_filled(dve, ("xqT", b))
                    v.tensor_scalar(fb, fa, ROUND, ROUND, ALU.add, ALU.subtract).then_inc(sg["q2_ready"], 1)
                elif kind == "x12":
                    b, = a
                    item = ("h2", b)
                    wait_filled(dve, item)
                    wait_emptied(dve, ("wb", b))
                    for j in range(NJ):
                        last = v.scalar_tensor_tensor(gu[:, j, :], bank(item)[:, j * 256:(j + 1) * 256],
                                                      sm[:, b, 23 + j:24 + j], sbc[:, 1, :], ALU.mult, ALU.mult)
                    empties(last, item)
                    wait_emptied(dve, item)
                    xb = xres[:, NJ * b:NJ * (b + 1), :]
                    link(v.tensor_tensor(xb, xb, gu[:, 0:2, :], ALU.add))
                elif kind == "r0":
                    b, = a

                    def free():
                        if b >= 2:
                            dve.wait_ge(scattered[b - 2], 16 * NJ * TOPK)
                            wait_filled(dve, ("h3T", b - 2))
                    layernorm(2, b, step, lambda j: h3[:, b % 2, j, :], free)
                elif kind == "r3":
                    b, = a
                    wait_emptied(dve, ("logit", b))
                    if b == 0:
                        dve.wait_ge(ld["bias"], 16)
                    link(v.tensor_scalar(sc[:, 0, :], sc[:, 0, :], 1.0, None, ALU.add))
                    link(v.reciprocal(sc[:, 1, :], sc[:, 0, :]))
                    link(v.tensor_tensor(
                        sc[:, 2, :].rearrange("p (j e) -> p j e", j=NJ), sc[:, 1, :].rearrange("p (j e) -> p j e", j=NJ),
                        bias_e[:].rearrange("p (o e) -> p o e", o=1).broadcast_to([P, NJ, E]), ALU.add))
                    n2 = NJ * NG
                    quad = sc[:, 2, :].rearrange("p (g two x) -> p g two x", two=2, x=2)
                    hi = rt[:, 0, 0:2 * n2].rearrange("p (g two) -> p g two", two=2)
                    lo = rt[:, 1, 0:2 * n2].rearrange("p (g two) -> p g two", two=2)
                    v.tensor_tensor(hi, quad[:, :, :, 0], quad[:, :, :, 1], ALU.max)
                    link(v.tensor_tensor(lo, quad[:, :, :, 0], quad[:, :, :, 1], ALU.min))
                    v.tensor_tensor(rt[:, 2, 0:n2], hi[:, :, 0], hi[:, :, 1], ALU.max)
                    v.tensor_tensor(rt[:, 3, 0:n2], hi[:, :, 0], hi[:, :, 1], ALU.min)
                    link(v.tensor_tensor(rt[:, 4, 0:n2], lo[:, :, 0], lo[:, :, 1], ALU.max))
                    link(v.tensor_tensor(rt[:, 5, 0:n2], rt[:, 3, 0:n2], rt[:, 4, 0:n2], ALU.max))
                    gs = rt[:, 6, 0:n2]
                    link(v.tensor_tensor(gs, rt[:, 2, 0:n2], rt[:, 5, 0:n2], ALU.add))
                    for j in range(NJ):
                        last = v.max(top[:, j, :], gs[:, j * NG:(j + 1) * NG])
                    link(last)
                    for j in range(NJ):
                        last = v.max_index(topi[:, j, :], top[:, j, :], gs[:, j * NG:(j + 1) * NG])
                    link(last)
                    link(v.tensor_copy(tif[:, :, 0:TKG], topi[:, :, 0:TKG]))
                    eqg = rt[:, 7, 0:NJ * TKG * NG].rearrange("p (j k g) -> p j k g", j=NJ, k=TKG)
                    link(v.tensor_tensor(
                        eqg, c_(C_I8, NG).rearrange("p (a o g) -> p a o g", a=1, o=1).broadcast_to([P, NJ, TKG, NG]),
                        tif[:, :, 0:TKG].rearrange("p j (k o) -> p j k o", o=1).broadcast_to([P, NJ, TKG, NG]),
                        ALU.is_equal))
                    gm = rt[:, 8, 0:n2]
                    link(v.tensor_reduce(gm.rearrange("p (j g) -> p j g", j=NJ),
                                         eqg.rearrange("p j k g -> p j g k"), AX.X, ALU.add))
                    mk = rt[:, 9, :]
                    link(v.tensor_tensor(mk.rearrange("p (g x) -> p g x", x=EG),
                                         sc[:, 2, :].rearrange("p (g x) -> p g x", x=EG),
                                         gm.rearrange("p (g o) -> p g o", o=1).broadcast_to([P, n2, EG]), ALU.mult))
                    link(v.tensor_scalar(mk, mk, 0.0, None, ALU.add))
                    for j in range(NJ):
                        last = v.max(top[:, j, :], mk[:, j * E:(j + 1) * E])
                    link(last)
                    for j in range(NJ):
                        last = v.max_index(topi[:, j, :], top[:, j, :], mk[:, j * E:(j + 1) * E])
                    link(last)
                    link(v.tensor_copy(tif[:], topi[:, :, 0:TOPK]))
                    oh4 = oh.rearrange("p (j k e) -> p j k e", j=NJ, k=TOPK)
                    ohp4 = ohp.rearrange("p (j k e) -> p j k e", j=NJ, k=TOPK)
                    link(v.tensor_tensor(
                        oh4, c_(C_I32, E).rearrange("p (a o g) -> p a o g", a=1, o=1).broadcast_to([P, NJ, TOPK, E]),
                        tif[:].rearrange("p j (k o) -> p j k o", o=1).broadcast_to([P, NJ, TOPK, E]), ALU.is_equal))
                    with nc.allow_low_precision("zeros and ones"):
                        v.tensor_reduce(chosen[:, NJ * b:NJ * (b + 1), :], oh4.rearrange("p j k e -> p j e k"), AX.X,
                                        ALU.add).then_inc(sg["chosen_ready"], 1)
                    link(v.tensor_tensor(
                        ohp4, oh4, sc[:, 1, :].rearrange("p (j o e) -> p j o e", j=NJ, o=1
                                                         ).broadcast_to([P, NJ, TOPK, E]), ALU.mult))
                    wk = slotf[:, 0, :].rearrange("p (j k) -> p j k", j=NJ)
                    link(v.tensor_reduce(wk, ohp4, AX.X, ALU.add))
                    ws_ = rt[:, 10, 0:NJ]
                    link(v.tensor_reduce(ws_, wk, AX.X, ALU.add))
                    link(v.tensor_scalar(ws_, ws_, 1e-20, None, ALU.add))
                    link(v.reciprocal(ws_, ws_))
                    link(v.tensor_scalar(ws_, ws_, 2.5, None, ALU.mult))
                    link(v.tensor_tensor(wk, wk, ws_.rearrange("p (j o) -> p j o", o=1).broadcast_to([P, NJ, TOPK]),
                                         ALU.mult))
                elif kind == "r4":
                    b, = a
                    item = ("pos", b)
                    wait_filled(dve, item)
                    pos = bank(item)[:, 0:NJ * E]
                    oh4 = oh.rearrange("p (j k e) -> p j k e", j=NJ, k=TOPK)
                    ohp4 = ohp.rearrange("p (j k e) -> p j k e", j=NJ, k=TOPK)
                    v.tensor_scalar(rt[:, 0, :], pos, float(CAP), NOSLOT, ALU.is_ge, ALU.mult)
                    empties(v.tensor_tensor(
                        rt[:, 1, :].rearrange("p (j e) -> p j e", j=NJ), pos.rearrange("p (j e) -> p j e", j=NJ),
                        c_(C_SLOT0, E).rearrange("p (o e) -> p o e", o=1).broadcast_to([P, NJ, E]), ALU.add), item)
                    wait_emptied(dve, item)
                    link(v.tensor_tensor(rt[:, 2, :], rt[:, 0, :], rt[:, 1, :], ALU.add))
                    link(v.tensor_tensor(
                        ohp4, oh4, rt[:, 2, :].rearrange("p (j o e) -> p j o e", j=NJ, o=1
                                                         ).broadcast_to([P, NJ, TOPK, E]), ALU.mult))
                    sl = slotf[:, 1, :]
                    link(v.tensor_reduce(sl.rearrange("p (j k) -> p j k", j=NJ), ohp4, AX.X, ALU.add))
                    tt = slice(NJ * b, NJ * (b + 1))
                    v.tensor_copy(scat[:, tt, :].rearrange("p j k -> p (j k)"), sl)
                    v.tensor_scalar(gath[:, tt, :].rearrange("p j k -> p (j k)"), sl, float(SLOTS - 1), None, ALU.min)
                    link(v.tensor_scalar(slotf[:, 2, :], sl, float(SLOTS), None, ALU.is_lt))
                    v.tensor_tensor(wtok[:, tt, :].rearrange("p j k -> p (j k)"), slotf[:, 0, :], slotf[:, 2, :],
                                    ALU.mult).then_inc(sg["slots_ready"], 1)
                elif kind == "s1":
                    b, = a
                    dve.wait_ge(sg["shared_exp"], b + 1)
                    link(v.tensor_scalar(es[:, 0, :], es[:, 0, :], 1.0, None, ALU.add))
                    link(v.reciprocal(es[:, 0, :], es[:, 0, :]))
                    empties(v.tensor_tensor(es[:, 1, :], bank(("sg", b)), es[:, 0, :], ALU.mult), ("sg", b))
                    wait_emptied(dve, ("sg", b))
                    wait_filled(dve, ("su", b))
                    if b >= 1:
                        wait_filled(dve, ("sd", b - 1))
                    empties(v.tensor_tensor(reg_t[:, 1024:1536], bank(("su", b)), es[:, 1, :],
                                            ALU.mult), ("su", b))
                elif kind == "s2":
                    b, = a
                    item = ("sd", b)
                    wait_filled(dve, item)
                    xb = xres[:, NJ * b:NJ * (b + 1), :].rearrange("p j d -> p (j d)")
                    empties(v.tensor_tensor(xb, bank(item), xb, ALU.add), item)
                elif kind == "xpT" and a[0] % 2 == 1:
                    i, = a
                    wait_filled(dve, step)
                    empties(v.tensor_copy(xpT[:, :, i * 256:(i + 1) * 256],
                                          bank(step).rearrange("p (k s) -> p k s", k=KD)), step)
                elif kind == "gate_up":
                    g, = a
                    item = ("gu", g)
                    n = XG * CAP
                    dve.wait_ge(sg["expert_exp"], g + 1)
                    eg = ee[:, g % 2, :]
                    link(v.tensor_scalar(eg, eg, 1.0, None, ALU.add))
                    link(v.reciprocal(eg, eg))
                    link(v.tensor_tensor(eg, bank(item)[:, 0:n], eg, ALU.mult))
                    if g >= 2:
                        wait_filled(dve, ("dn", g - 2))
                    empties(v.tensor_tensor(hE[:, g % 2, :], bank(item)[:, n:2 * n], eg, ALU.mult), item)
                elif kind == "yT":
                    i, = a
                    wait_filled(dve, step)
                    empties(v.tensor_copy(rows[:, 2 * i:2 * i + 2, :].rearrange("p s d -> p (s d)"), bank(step)),
                            step)
                elif kind == "combine":
                    t, = a
                    if t == 0:
                        for b in range(B):
                            wait_emptied(dve, ("sd", b))
                    for k in range(TOPK):
                        n = (t % 2) * TOPK + k
                        dve.wait_ge(gathered[n], 16 * (t // 2 + 1))
                        ins = v.scalar_tensor_tensor(xres[:, t, :], gbuf[:, n, :], wtok[:, t, k:k + 1],
                                                     xres[:, t, :], ALU.mult, ALU.add)
                        if k < TOPK - 1:
                            link(ins)
                    ins.then_inc(sg["combined"], 1)

        @block.gpsimd
        def _(pool):
            g = nc.gpsimd
            chain = [0]

            def link(ins):
                chain[0] += 1
                ins.then_inc(sg["pool_chain"], 1)
                pool.wait_ge(sg["pool_chain"], chain[0])

            for step in steps:
                kind, a = step[0], step[1:]
                if kind == "setup":
                    g.memset(neg_half[:], -0.5).then_inc(sg["halves_ready"], 1)
                    g.memset(pos_half[:], 0.5).then_inc(sg["halves_ready"], 1)
                    pool.wait_ge(sg["halves_ready"], 2)
                elif kind in ("ln1", "x0", "r0"):
                    b, = a
                    tag = ("ln1", "x0", "r0").index(kind)
                    tt = slice(NJ * b, NJ * (b + 1))
                    pool.wait_ge(sg["ln_stats"], nth(*step) + 1)
                    link(g.tensor_scalar(vtmp[:, tag, tt], mv[:, tag, tt, 1], EPS_LN, None, ALU.add))
                    g.tensor_tensor(rstd[:, tag, tt], vtmp[:, tag, tt], neg_half[:].broadcast_to([P, NJ]), ALU.pow
                                    ).then_inc(sg["ln_rstd"], 1)
                elif kind == "fused":
                    t, = a
                    pool.wait_ge(sg["squares_ready"], t + 1)
                    link(g.tensor_scalar(weps[:, t, :], ssq[:, t, :], EPS_RMS, None, ALU.add))
                    g.tensor_tensor(rrms[:, t, :], weps[:, t, :], neg_half[:].broadcast_to([P, 2]), ALU.pow
                                    ).then_inc(sg["rms_ready"], 1)
                elif kind == "q":
                    u = nth(*step)
                    pool.wait_ge(sg["rope_parts"], u + 1)
                    qp = qs[:, u % 2].rearrange("p (h m) -> p h m", h=HC)[:, :, KL:]
                    g.tensor_tensor(qp, qp, qr[:, u % 2].rearrange("p (h x) -> p h x", h=HC), ALU.add
                                    ).then_inc(sg["rope_added"], 1)
                elif kind == "x1":
                    b, = a
                    pool.wait_ge(sg["ratio_ready"], b + 1)
                    g.tensor_tensor(sm[:, b, 4:6], sm[:, b, 2:4], pos_half[:].broadcast_to([P, 2]), ALU.pow
                                    ).then_inc(sg["smooth_root"], 1)
                elif kind == "x2":
                    b, = a
                    pool.wait_ge(sg["smooth_ready"], b + 1)
                    wait_emptied(pool, ("fsT", b))
                    if b >= 1:
                        wait_filled(pool, ("as", b - 1))
                    for k in range(KD):
                        last = g.tensor_scalar(wsT[:, k * 256:(k + 1) * 256], fsT[:, k * 256:(k + 1) * 256],
                                               sm[:, b, 6 + k:7 + k], None, ALU.mult)
                    last.then_inc(sg["scaledT_w"], 1)
                elif kind == "x8":
                    b, = a
                    pool.wait_ge(sg["ratio2_ready"], b + 1)
                    g.tensor_tensor(sm[:, b, 20:21], sm[:, b, 19:20], pos_half[:], ALU.pow
                                    ).then_inc(sg["smooth_root2"], 1)
                    pool.wait_ge(sg["smooth_ready2"], b + 1)
                    wait_filled(pool, ("ws", b))
                    wait_emptied(pool, ("cxT", b))
                    g.tensor_scalar(wsT[:, 0:256], cxT[:], sm[:, b, 21:22], None, ALU.mult
                                    ).then_inc(sg["scaledT_c"], 1)
                elif kind == "scatter":
                    b, i = a
                    if i == 0:
                        pool.wait_ge(sg["slots_ready"], b + 1)
                        if b == 0:
                            pool.wait_ge(sg["xp_zeroed"], 16 * (NS // 2))
                    for m in range(2):
                        j, k = (2 * i + m) // TOPK, (2 * i + m) % TOPK
                        g.indirect_dma_start(
                            out=xp_dram, out_offset=bass.IndirectOffsetOnAxis(ap=scat[:, NJ * b + j, k:k + 1], axis=0),
                            in_=h3[:, b % 2, j, :], in_offset=None, bounds_check=SLOTS - 1, oob_is_err=False
                        ).then_inc(scattered[b], 16)
                elif kind == "combine":
                    t, = a
                    if t == 0:
                        pool.wait_ge(sg["y_stored"], 16 * (NS // 2))
                    if t >= 2:
                        pool.wait_ge(sg["combined"], t - 1)
                    for k in range(TOPK):
                        n = (t % 2) * TOPK + k
                        g.indirect_dma_start(
                            out=gbuf[:, n, :], out_offset=None, in_=y_dram,
                            in_offset=bass.IndirectOffsetOnAxis(ap=gath[:, t, k:k + 1], axis=0),
                            bounds_check=SLOTS - 1, oob_is_err=False).then_inc(gathered[n], 16)


def shape_constants():
    import numpy as np

    c = np.zeros((P, NCONST), np.float32)
    i = np.arange(P)
    c[:, C_ID:C_ID + P] = np.eye(P)
    c[:, C_MASK:C_MASK + P] = np.where(i[None, :] > i[:, None], -1e30, 0.0)
    c[:, C_TRI:C_TRI + P] = i[:, None] < i[None, :]
    freq = (1.0 / np.float32(10000.0) ** (np.arange(0, DR, 2, dtype=np.float32) / np.float32(DR))).astype(np.float32)
    for j in range(NJ):
        angle = (np.arange(P, dtype=np.float32) + np.float32(j * P))[:, None] * freq[None, :]
        cos, sin = np.cos(angle).astype(np.float32), np.sin(angle).astype(np.float32)
        o = j * DR
        c[:, C_COS + o:C_COS + o + DR] = np.concatenate([cos, cos], 1)
        c[:, C_SIN + o:C_SIN + o + DR] = np.concatenate([sin, -sin], 1)
    c[:, C_I32:C_I32 + E] = np.arange(E)
    c[:, C_I8:C_I8 + NG] = np.arange(NG)
    c[:, C_SLOT0:C_SLOT0 + E] = np.arange(E) * CAP
    return c


_INS = ['x', 'fside_BxS2xS2_0', 'ctx_1024', 'L0_attn_w_kv_a', 'L0_attn_q_a_gamma', 'L0_attn_w_qb',
        'L0_attn_kv_a_gamma', 'L0_attn_w_kvb', 'L0_attn_w_o', 'L0_ffn_router_w', 'L0_ffn_e_bias', 'L0_ffn_W_gate',
        'L0_ffn_W_up', 'L0_ffn_W_down', 'L0_ffn_shared_gate', 'L0_ffn_shared_up', 'L0_ffn_shared_down']


def kernel(**inputs):
    import numpy as _np
    import concourse.bacc as _bacc
    from concourse import mybir as _mybir
    from concourse.bass_utils import run_bass_kernel_spmd as _run

    nc = _bacc.Bacc("TRN2", target_bir_lowering=False, num_devices=1)
    arrays, args = {}, []
    given = {name: _np.ascontiguousarray(inputs[name]) for name in _INS}
    given["shape_constants"] = shape_constants()
    for name, a in given.items():
        arrays[f"in_{name}_dram"] = a
        args.append(nc.dram_tensor(f"in_{name}_dram", a.shape, _mybir.dt.from_np(a.dtype), kind="ExternalInput").ap())
    args.append(nc.dram_tensor("out_0_dram", (B, S, D), F32, kind="ExternalOutput").ap())
    decoder_layer(nc, *args)
    r = _run(nc, [arrays], core_ids=[0])
    return r.results[0]["out_0_dram"]
```

```python
from contextlib import ExitStack

import concourse.bass as bass
from concourse import mybir

ALU = mybir.AluOpType
ACT = mybir.ActivationFunctionType
AX = mybir.AxisListType
F32 = mybir.dt.float32
BF16 = mybir.dt.bfloat16
U32 = mybir.dt.uint32

P = 128
B, S, D = 4, 256, 256
NT = B * S // P
NJ = S // P
KD = D // P
NH, DN, DR, DV, QL, KL = 16, 128, 64, 128, 192, 64
DQK = KL + DR
HC = 4
GH = 4
NHU = B * NH
E, TOPK, NG, TKG = 32, 4, 8, 3
EG = E // NG
CAP = 40
SLOTS = E * CAP
NS = SLOTS // P
XG = 4
NG_E = E // XG
XR = 64
I = 128
WE = 2 * KD * I + D
SM_SCALE = 1.0 / float(DN + DR) ** 0.5
EPS_LN, EPS_RMS, EPS_Q, QMAX = 1e-5, 1e-6, 1e-6, 127.0
ROUND = 12582912.0
NOSLOT = 4096.0
BANK_S, BANK_PT, BANK_O, BANK_Q, BANK_W = 0, 2, 3, 4, 5
NBANK = 8
NW = NBANK - BANK_W

C_ID, C_MASK, C_TRI, C_COS, C_SIN, C_I32, C_I8, C_SLOT0 = 0, 128, 256, 384, 512, 640, 672, 680
NCONST = 712

SLOTS_A, SLOTS_B, SLOTS_C = 9, 10, 5
NHOME = SLOTS_A + SLOTS_B + SLOTS_C


CROSS_AND_ROUTE = (
    ("x_stats", 0), ("x_norm", 2), ("x_T", 4), ("x_smooth", 2), ("x_scale", 1), ("x_back", 4), ("x_qscale", 1),
    ("x_round", 2), ("x_qT", 4), ("x_mm", 3), ("x_tanh", 1), ("x_gate", 1), ("x_smooth2", 2), ("x_scale2", 1),
    ("x_back2", 4), ("x_qscale2", 1), ("x_round2", 2), ("x_qT2", 4), ("x_mm2", 3), ("r_stats", 0), ("r_norm", 2),
    ("r_T", 4), ("r_logit", 3), ("r_groups", 1), ("r_best", 1), ("r_choose", 1), ("r_weights", 1), ("r_pos", 4),
    ("r_slots", 1)) + tuple((f"scatter{i}", 4) for i in range(NJ * TOPK))


def plan():
    places = [[] for _ in range(4 * NHU + 200)]

    steps = [("setup",), ("ln1_stats", 0), ("ln1_norm", 0), ("hT", 0), ("hT", 1), ("fused", 0), ("fused", 1),
             ("prepT", 0), ("latents", 0), ("prepT", 1), ("latents", 1), ("latT", 0), ("prepM", 0),
             ("prepT", 2), ("latT", 1), ("prepT", 3), ("prepT", 4), ("prepM", 1), ("prepT", 5), ("prepT", 6),
             ("prepM", 2), ("prepT", 7), ("ln1_stats", 1), ("ln1_norm", 1), ("prepM", 3)]
    for p, at in ((4, 0), (5, 3), (6, 9), (7, 13)):
        places[at].append(("prepT", 2 * p))
        places[at + 1].append(("prepT", 2 * p + 1))
        places[at + 3].append(("prepM", p))
    for b, at in ((1, 6), (2, 36), (3, 50)):
        if b > 1:
            places[at - 4].append(("ln1_stats", b))
            places[at - 2].append(("ln1_norm", b))
        for t in (2 * b, 2 * b + 1):
            for kind, gap in (("hT", 0), ("fused", 2), ("latents", 5), ("latT", 8)):
                places[at + gap].append((kind, t))
            at += 5

    units = [(NJ * b + j, c) for b in range(B) for c in range(NH // HC) for j in range(NJ)]
    ahead = 3
    for u in units[:ahead]:
        steps += [("q",) + u, ("rope",) + u, ("qT",) + u]

    for b in range(B):
        at = 4 * (NH * (b + 1) + 3) + 2 if b < B - 1 else 4 * NHU
        places[at].append(("y", 2 * b))
        places[at + 2].append(("y_add", 2 * b))
        places[at + 4].append(("y", 2 * b + 1))
        places[at + 5].append(("y_add", 2 * b + 1))
        at += 2
        at += 4
        for kind, gap in CROSS_AND_ROUTE:
            at += gap if b < B - 1 else min(gap, 2)
            places[at].append(("scatter", b, int(kind[-1])) if kind[:-1] == "scatter" else (kind, b))
        places[4 * (NH * b + (15 if b else 2)) + 3].append(("wx", b))
    places[4 * 5 + 1].append(("rwT",))
    for i in range(3):
        places[4 * (6 + i) + 1].append(("shT", i))

    steps += [("attention",)]
    for hn in range(NHU):
        steps.append(("scores", hn))
        steps += places[4 * hn]
        if hn >= 2:
            steps.append(("probsT", hn - 2))
        steps += places[4 * hn + 1]
        u = hn // 2 + ahead
        if u < len(units) and hn % 2 == 0:
            steps.append(("q",) + units[u])
        steps += places[4 * hn + 2]
        if u < len(units) and hn % 2 == 0:
            steps.append(("rope",) + units[u])
        if hn >= 4 and hn % 2 == 0:
            steps.append(("pv", hn // 2 - 2))
        steps += places[4 * hn + 3]
        if u < len(units) and hn % 2 == 1:
            steps.append(("qT",) + units[u])
    steps += [("probsT", NHU - 2), ("pv", NHU // 2 - 2), ("probsT", NHU - 1), ("pv", NHU // 2 - 1), ("tail",)]
    fill = [(f"s{i}", bb) for bb in range(B - 1) for i in range(2)]
    at = 0
    for i, place in enumerate(places[4 * NHU:]):
        steps += place
        at += 1
        if i > 20 and i % 7 == 0 and fill:
            steps.append(fill.pop(0))
    assert not fill
    steps += [("s0", B - 1), ("s1", B - 1)]
    steps += [("xpT", i) for i in range(NS // 2)]
    for g in range(NG_E + 2):
        if g < NG_E:
            steps.append(("gate_up", g))
        if 0 < g <= NG_E:
            steps.append(("hidT", g - 1))
        if g > 1:
            steps.append(("down", g - 2))
    for t in range(NT):
        steps.append(("combine", t))
    return steps


ITEMS = {
    "hT": [("hT", 1)], "fused": [("fused", 1)], "latT": [("latT", 1)],
    "prepT": [("prepT", 1)], "prepM": [("prepM", 1)],
    "q": [("q", 1)], "qT": [("qT", 1)], "y": [("y", 1)],
    "wx": [("fsT", 1), ("cxT", 1)], "rwT": [("rwT", 1)], "shT": [("shT", 1)],
    "x_T": [("xT", 1)], "x_back": [("xs", 1), ("ws", 1)], "x_qT": [("xqT", 1), ("xb", 1)],
    "x_mm": [("h1", 1)], "x_back2": [("as", 1)], "x_qT2": [("aqT", 1), ("wb", 1)], "x_mm2": [("h2", 1)],
    "r_T": [("h3T", 1)], "r_logit": [("logit", 1)], "r_pos": [("pos", 1)],
    "s0": [("sg", 1), ("su", 1)], "s1": [("sd", 1)],
    "xpT": [("xpT", 1)], "gate_up": [("gu", 1)], "hidT": [("hidT", 1)], "down": [("dn", 1)],
}


class Ring:

    def __init__(self, steps):
        self.at = {}
        filled, emptied, n = [0] * NBANK, [0] * NBANK, 0
        ring = list(range(NBANK))
        self.before_attention = None
        for step in steps:
            if step[0] == "attention":
                self.before_attention = list(emptied)
                ring = list(range(BANK_W, NBANK))
            elif step[0] == "tail":
                ring = list(range(NBANK))
            for name, empties in ITEMS.get(step[0], []):
                if name in ("q", "qT"):
                    k = BANK_Q
                else:
                    k = ring[n % len(ring)]
                    n += 1
                self.at[(name,) + step[1:]] = (k, emptied[k], filled[k] + 1, emptied[k] + empties)
                filled[k] += 1
                emptied[k] += empties


def decoder_layer(nc, x, fside, ctx_w, w_kv_a, q_gamma, w_qb, kv_gamma, w_kvb, w_o, router_w, e_bias,
                  w_gate, w_up, w_down, sh_gate, sh_up, sh_down, consts, out):
    steps = plan()
    ring = Ring(steps)
    xp_dram = nc.dram_tensor("expert_rows", (SLOTS, D), F32, kind="Internal").ap()
    y_dram = nc.dram_tensor("expert_out", (E * XR, D), F32, kind="Internal").ap()

    with ExitStack() as stack:
        def sb(name, shape, dt=F32):
            return stack.enter_context(nc.sbuf_tensor(name, shape, dt))

        def sem(name):
            return stack.enter_context(nc.semaphore(name))

        psum = stack.enter_context(nc.psum_tensor("psum", [P, NBANK, 512], F32))
        ps_pt = psum[:, BANK_PT, :]
        ps_o = psum[:, BANK_O, :]

        cst = sb("consts", [P, NCONST])
        id_bf = sb("ident_bf16", [P, P], BF16)
        mask_bf = sb("mask_bf16", [P, P], BF16)
        tri_bf = sb("tri_bf16", [P, P], BF16)
        ones_bf = sb("ones_bf16", [P, P], BF16)
        xres = sb("x_residual", [P, NT, D])
        neg_half = sb("neg_half", [P, 1])
        pos_half = sb("pos_half", [P, 1])
        gam_q = sb("gamma_q", [P, QL])
        gam_kv = sb("gamma_kv", [P, KL])
        bias_e = sb("e_bias", [P, E])
        w_mo = sb("w_folded_out", [P, NH // 2, D])
        fs = sb("fside", [P, B, 2, D])
        cx = sb("ctx", [P, B, 2, I])
        rwT = sb("router_wT", [P, KD, E])
        shT = sb("shared_wT", [P, 3, KD, D])
        reg_a = sb("region_a", [P, 6912])
        reg_b = sb("region_b", [P, 8192])
        reg_c = sb("region_c", [P, 4096])
        reg_g = sb("region_g", [P, 4096])
        reg_h = sb("region_h", [P, 4096])
        wq0 = reg_a[:, 0:NH * DN].rearrange("p (h m) -> p h m", h=NH)
        wkq = reg_a[:, 2048:6144].rearrange("p (h m) -> p h m", h=NH)
        wo = reg_b[:, 0:4096].rearrange("p (h d) -> p h d", h=NH)
        qT = reg_b[:, 4096:6144].rearrange("p (c h t) -> p c h t", c=2, h=HC)
        wf0 = reg_c[:, 0:2048].rearrange("p (h m) -> p h m", h=NH)
        wf1 = reg_c[0:64, 2048:4096].rearrange("p (h m) -> p h m", h=NH)
        oT = reg_g[:, :].rearrange("p (b i t) -> p b i t", b=2, i=NH // 2)
        xpT = reg_g[:, 0:KD * (SLOTS + XR - CAP)].rearrange("p (k s) -> p k s", k=KD)
        kv = reg_h[:, 0:1024].rearrange("p (t m) -> p t m", t=NT)
        kT = reg_h[:, 1024:2048].rearrange("p (b m) -> p b m", b=B)
        qn0 = reg_h[:, 2048:3072].rearrange("p (t m) -> p t m", t=NT)
        qn1 = reg_h[0:64, 3072:4096].rearrange("p (t m) -> p t m", t=NT)
        rows = reg_h[:, 0:NS * D].rearrange("p (i d) -> p i d", i=NS)
        ybuf = reg_h[:, NS * D:NS * D + 1536].rearrange("p (u d) -> p u d", u=3)

        def home(e):
            s = e % NHOME
            if s < SLOTS_A:
                r, o = reg_a, s * WE
            elif s < SLOTS_A + SLOTS_B:
                r, o = reg_b, (s - SLOTS_A) * WE
            else:
                r, o = reg_c, (s - SLOTS_A - SLOTS_B) * WE
            return r[:, o:o + WE]

        def gate_up_of(e):
            return home(e)[:, 0:2 * KD * I].rearrange("p (k m) -> p k m", k=KD)

        def down_of(e):
            return home(e)[:, 2 * KD * I:WE]

        reg_t = sb("region_t", [P, 3072])
        reg_r = sb("region_r", [P, 2048])
        wkva = reg_b[:, 6144:6784].rearrange("p (k n) -> p k n", k=KD)
        probs = reg_t[:, 0:1152].rearrange("p (u q) -> p u q", u=3)
        probsT = reg_t[:, 1152:2688].rearrange("p (u q) -> p u q", u=4)
        es = reg_t[:, 0:1024].rearrange("p (u q) -> p u q", u=2)
        act_s = reg_t[:, 1024:2048].rearrange("p (u k t) -> p u k t", u=2, k=2)
        th = reg_t[:, 2048:3072].rearrange("p (u q) -> p u q", u=4)
        hE = reg_r[:, 0:512].rearrange("p (u q) -> p u q", u=2)
        hET = reg_r[:, 512:1024].rearrange("p (u q) -> p u q", u=2)
        hn_f = reg_r[:, 0:512].rearrange("p (j d) -> p j d", j=NJ)
        hT_f = reg_r[:, 512:1024].rearrange("p (i m) -> p i m", i=2)
        wT = reg_g[:, 2048:3328].rearrange("p (i m) -> p i m", i=4)
        fused_s = reg_r[:, 1024:1344]
        sq = reg_r[:, 1408:1664]
        qn = reg_r[:, 1664:1664 + 2 * QL].rearrange("p (i m) -> p i m", i=2)
        qa = reg_r[:, 0:1024].rearrange("p (i d) -> p i d", i=4)
        gu = reg_r[:, 1024:2048].rearrange("p (i d) -> p i d", i=4)
        zeros = reg_g[:, 3584:4096]
        rw = reg_g[:, 3328:3584]

        ssq = sb("sum_squares", [P, NT, 2])
        rrms = sb("rrms", [P, NT, 2])
        weps = sb("rms_eps", [P, NT, 2])
        kr = sb("k_rope_tmp", [P, 2, DR])
        qs = sb("q_chunk", [P, 2, HC * DQK])
        qr = sb("q_rope_tmp", [P, 2, HC * DR])
        nmax = sb("neg_max", [P, NHU, 2])
        sums = sb("prob_sums", [P, NHU, NJ])
        rsum = sb("prob_rsums", [P, NHU, NJ])
        stats = sb("bn_stats", [P, 2, 6])
        mv = sb("mean_var", [P, 3, NT, 2])
        rstd = sb("rstd", [P, 3, NT])
        vtmp = sb("var_eps", [P, 3, NT])
        h2 = sb("h_cross", [P, NJ, D])
        fsT = sb("fsideT", [P, 512])
        cxT = sb("ctxT", [P, 256])
        xsT = sb("x_scaledT", [P, 512])
        wsT = sb("w_scaledT", [P, 512])
        rden = sb("rden", [P, B, 3])
        sm = sb("smooth", [P, B, 36])
        qb = sb("q_bf16", [P, 4, D], BF16)
        qTs = sb("qT_bf16", [P, 4, D], BF16)
        sbc = sb("scale_rows", [P, 2, D])
        h3 = sb("h_moe", [P, 2, NJ, D])
        h3T = sb("h_moeT", [P, B, KD, S])
        sc = sb("scores", [P, 3, NJ * E])
        reg_rt = sb("route", [P, 12 * NJ * E])
        rt = reg_rt[:, :].rearrange("p (i m) -> p i m", i=12)
        top = sb("top", [P, NJ, 8])
        topi = sb("top_index", [P, NJ, 8], U32)
        tif = sb("top_index_f32", [P, NJ, TOPK])
        oh = reg_t[:, 2688:2944]
        ohp = reg_rt[:, 3 * NJ * E:3 * NJ * E + 256]
        chosen = sb("chosen", [P, NT, E], BF16)
        slotf = sb("slot_f32", [P, 4, NJ * TOPK])
        scat = sb("slot_scatter", [P, NT, TOPK], U32)
        gath = sb("slot_gather", [P, NT, TOPK], U32)
        wtok = sb("token_weights", [P, NT, TOPK])
        h3T_flat = h3T[:].rearrange("p b k t -> p (b k t)")
        shw = h3T_flat[:, 0:1536].rearrange("p (i o d) -> p i o d", i=3, o=2)
        gbuf = reg_b[:, 0:2048].rearrange("p (n d) -> p n d", n=8)

        ld = {k: sem("ld_" + k) for k in ("consts", "x0", "x1", "x2", "x3", "wkva", "gam", "rope_cols", "fs", "cx", "rw", "sh", "bias")}
        ld_fold = [sem(f"ld_fold{i}") for i in range(2)]
        ld_experts = [sem(f"ld_experts{g}") for g in range(E // XG)]
        ld_rows = [sem(f"ld_rows{i}") for i in range(NS // 2)]
        bank_filled = [sem(f"bank_filled{k}") for k in range(NBANK)]
        bank_emptied = [sem(f"bank_emptied{k}") for k in range(NBANK)]
        names = """consts_ready halves_ready zeros_ready padding_ready ln_stats ln_rstd h_ready squares_ready
            rms_ready lat_ready scores_ready max_ready exp_done probs_normed probsT_done
            probsT_copied heads_done heads_copied
            rope_parts rope_added ratio_ready smooth_root smooth_ready scaledT_w inv_ready q_ready gate_tanh
            ratio2_ready smooth_root2 smooth_ready2 scaledT_a scaledT_c inv2_ready q2_ready
            chosen_ready weights_ready slots_ready shared_tanh xp_zeroed expert_tanh combined out_stored
            dve_chain act_chain pool_chain""".split()
        sg = {n: sem(n) for n in names}
        scattered = [sem(f"scattered{b}") for b in range(B)]
        y_stored = [sem(f"y_stored{g}") for g in range(NG_E)]
        gathered = [sem(f"gathered{i}") for i in range(8)]
        block = stack.enter_context(nc.Block())

        def c_(o, n):
            return cst[:, o:o + n]

        ident = c_(C_ID, P)

        def bank(item):
            return psum[:, ring.at[item][0], :]

        def wait_empty(eng, item):
            k, before, _, _ = ring.at[item]
            if before:
                eng.wait_ge(bank_emptied[k], before)

        def wait_filled(eng, item):
            k, _, filled, _ = ring.at[item]
            eng.wait_ge(bank_filled[k], filled)

        def wait_emptied(eng, item):
            k, _, _, after = ring.at[item]
            eng.wait_ge(bank_emptied[k], after)

        def fills(ins, item):
            ins.then_inc(bank_filled[ring.at[item][0]], 1)

        def empties(ins, item):
            ins.then_inc(bank_emptied[ring.at[item][0]], 1)

        step_no = {}
        for step in steps:
            kind = "ln" if step[0] in ("ln1_stats", "x_stats", "r_stats") else step[0]
            step_no[step] = sum(1 for k in step_no.values() if k[0] == kind), kind
            step_no[step] = (kind, step_no[step][0])

        def nth(*step):
            return step_no[step][1]

        q_order = [step for step in steps if step[0] == "qT"]

        @block.sync
        def _(sp):
            def load_expert(e):
                s = ld_experts[e // XG]
                w = gate_up_of(e)
                sp.dma_start(w[:, :, 0:I], w_gate[e].rearrange("(k p) i -> p k i", p=P)).then_inc(s, 16)
                sp.dma_start(w[:, :, I:], w_up[e].rearrange("(k p) i -> p k i", p=P)).then_inc(s, 16)
                sp.dma_start(down_of(e), w_down[e]).then_inc(s, 16)

            xt = x.rearrange("b (j p) d -> b p j d", p=P)
            sp.dma_start(xres[:, 0:2, :], xt[0]).then_inc(ld["x0"], 16)
            sp.dma_start(cst[:], consts).then_inc(ld["consts"], 16)
            sp.dma_start(wkva[:], w_kv_a.rearrange("(k p) n -> p k n", p=P)).then_inc(ld["wkva"], 16)
            sp.dma_start(gam_q[:], q_gamma.partition_broadcast(P)).then_inc(ld["gam"], 16)
            sp.dma_start(gam_kv[:], kv_gamma.partition_broadcast(P)).then_inc(ld["gam"], 16)
            sp.dma_start(xres[:, 2:4, :], xt[1]).then_inc(ld["x1"], 16)
            wqh = w_qb.rearrange("p (h m) -> p h m", h=NH)
            kvh = w_kvb.rearrange("p (h m) -> p h m", h=NH)
            woh = w_o.rearrange("(h p) d -> p h d", p=P)
            for i in range(2):
                hs = slice(i * NH // 2, (i + 1) * NH // 2)
                sp.dma_start(wkq[0:KL, hs], kvh[:, hs]).then_inc(ld_fold[i], 16)
                sp.dma_start(wq0[:, hs], wqh[0:P, hs, 0:DN]).then_inc(ld_fold[i], 16)
                sp.dma_start(wkq[KL:P, hs, 0:DN], wqh[P:QL, hs, 0:DN]).then_inc(ld_fold[i], 16)
                sp.dma_start(wo[:, hs], woh[:, hs]).then_inc(ld_fold[i], 16)
            sp.dma_start(wf0[:, :, KL:], wqh[0:P, :, DN:]).then_inc(ld["rope_cols"], 16)
            sp.dma_start(wf1[:, :, KL:], wqh[P:QL, :, DN:]).then_inc(ld["rope_cols"], 16)
            sp.dma_start(xres[:, 4:6, :], xt[2]).then_inc(ld["x2"], 16)
            sp.dma_start(xres[:, 6:8, :], xt[3]).then_inc(ld["x3"], 16)
            sp.dma_start(fs[:], fside.rearrange("b (o p) d -> p b o d", p=P)).then_inc(ld["fs"], 16)
            sp.dma_start(cx[:], ctx_w.rearrange("b (o p) i -> p b o i", p=P)).then_inc(ld["cx"], 16)
            sp.dma_start(rw[0:E, :], router_w).then_inc(ld["rw"], 16)
            sp.dma_start(bias_e[:], e_bias.partition_broadcast(P)).then_inc(ld["bias"], 16)
            for i, w in enumerate((sh_gate, sh_up, sh_down)):
                sp.dma_start(shw[:, i], w.rearrange("(o p) d -> p o d", p=P)).then_inc(ld["sh"], 16)
            sp.wait_ge(sg["zeros_ready"], 1)
            xz = xp_dram.rearrange("(p a) d -> p (a d)", p=P)
            for i in range(NS // 2):
                sp.dma_start(xz[:, 512 * i:512 * i + 512], zeros).then_inc(sg["xp_zeroed"], 16)
            for p in range(NH // 2):
                wait_emptied(sp, ("prepM", p))
            for e in range(SLOTS_A + 5):
                load_expert(e)
            wait_filled(sp, ("fused", NT - 1))
            for e in range(SLOTS_A + 8, SLOTS_A + SLOTS_B):
                load_expert(e)
            wait_filled(sp, q_order[-1])
            for e in range(SLOTS_A + SLOTS_B, NHOME):
                load_expert(e)
            sp.wait_ge(sg["scores_ready"], NHU)
            for e in range(SLOTS_A + 5, SLOTS_A + 8):
                load_expert(e)
            for b in range(B):
                sp.wait_ge(scattered[b], 16 * NJ * TOPK)
            for i in range(NS // 2):
                sp.dma_start(rows[:, 2 * i:2 * i + 2, :],
                             xp_dram.rearrange("(i p) d -> p i d", p=P)[:, 2 * i:2 * i + 2, :]
                             ).then_inc(ld_rows[i], 16)
            yv = y_dram.rearrange("(i p) d -> p i d", p=P)

            def store_outputs(i):
                wait_emptied(sp, ("dn", i))
                sp.dma_start(yv[:, 2 * i:2 * i + 2, :], ybuf[:, i % 3, :].rearrange("p (i d) -> p i d", i=2)
                             ).then_inc(y_stored[i], 16)

            for e in range(NHOME, E):
                if (e - NHOME) % XG == 0:
                    wait_filled(sp, ("dn", (e - NHOME) // XG))
                load_expert(e)
                if (e - NHOME) % XG == XG - 1:
                    store_outputs((e - NHOME) // XG)
            for i in range(2, NG_E):
                store_outputs(i)
            ov = out.rearrange("b (j p) d -> p (b j) d", p=P)
            for t in range(NT):
                sp.wait_ge(sg["combined"], t + 1)
                sp.dma_start(ov[:, t, :], xres[:, t, :]).then_inc(sg["out_stored"], 16)
            sp.wait_ge(sg["out_stored"], 16 * NT)

        @block.tensor
        def _(pe):
            def mm(out_, lhsT, rhs, first=True, last=True):
                return nc.tensor.matmul(out_, lhsT, rhs, start=first, stop=last)

            def mm_halves(out_, lhsT, rhs, first=True, last=True):
                h = P // 2
                mm(out_[0:h], lhsT[:, 0:h], rhs, first, last)
                return mm(out_[h:P], lhsT[:, h:P], rhs, first, last)

            def turn(out_, in_, idn=None):
                return nc.tensor.transpose(out_, in_, ident if idn is None else idn)

            def bf(item):
                return bank(item).bitcast(BF16)

            for step in steps:
                kind, a = step[0], step[1:]
                if kind == "setup":
                    pe.wait_ge(ld["consts"], 16)
                elif kind == "hT":
                    t, = a
                    pe.wait_ge(sg["h_ready"], nth("ln1_stats", t // NJ) + 1)
                    wait_empty(pe, step)
                    for k in range(KD):
                        last = turn(bank(step)[:, k * P:(k + 1) * P], hn_f[:, t % 2, k * P:(k + 1) * P])
                    fills(last, step)
                elif kind == "fused":
                    t, = a
                    if t == 0:
                        pe.wait_ge(ld["wkva"], 16)
                    wait_emptied(pe, ("hT", t))
                    wait_empty(pe, step)
                    for k in range(KD):
                        last = mm(bank(step)[:, 0:QL + KL + DR], hT_f[:, t % 2, k * P:(k + 1) * P], wkva[:, k, :],
                                  k == 0, k == KD - 1)
                    fills(last, step)
                elif kind == "latT":
                    t, = a
                    pe.wait_ge(sg["lat_ready"], t + 1)
                    wait_empty(pe, step)
                    turn(bank(step)[:, 0:P], qn[:, t % 2, 0:P])
                    turn(bank(step)[:, P:2 * P], kv[:, t, :])
                    fills(turn(bank(step)[0:64, 2 * P:3 * P], qn[:, t % 2, P:QL]), step)
                elif kind == "prepT":
                    h, = a
                    if h % (NH // 2) == 0:
                        pe.wait_ge(ld_fold[h // (NH // 2)], 16 * 4)
                    wait_empty(pe, step)
                    turn(bank(step)[:, 0:P], wq0[:, h, :])
                    turn(bank(step)[:, P:2 * P], wkq[:, h, 0:DN])
                    fills(turn(bank(step)[:, 256:320], wkq[0:KL, h, DN:], ident[0:KL, 0:KL]), step)
                elif kind == "prepM":
                    p, = a
                    wait_emptied(pe, ("prepT", 2 * p))
                    wait_emptied(pe, ("prepT", 2 * p + 1))
                    wait_empty(pe, step)
                    for i in range(2):
                        w = wT[:, (2 * p + i) % 4, :]
                        wkT = w[:, P:P + KL]
                        mm_halves(bank(step)[:, i * KL:(i + 1) * KL], w[:, 0:P], wkT)
                        mm(bank(step)[0:64, 128 + i * KL:128 + (i + 1) * KL], w[:, P + KL:2 * P], wkT)
                    for i in range(2):
                        last = mm(bank(step)[i * KL:(i + 1) * KL, 256:512], wT[:, (2 * p + i) % 4, 256:320], wo[:, 2 * p + i, :])
                    fills(last, step)
                elif kind == "q":
                    t, c = a
                    if t < NJ:
                        for p in range(HC * c // 2, HC * (c + 1) // 2):
                            wait_emptied(pe, ("prepM", p))
                    if nth(*step) == 0:
                        pe.wait_ge(ld["rope_cols"], 32)
                    wait_emptied(pe, ("latT", t))
                    wait_empty(pe, step)
                    mm(bank(step), qn0[:, t, :], wf0[:, HC * c:HC * (c + 1), :], True, False)
                    fills(mm(bank(step), qn1[:, t, :], wf1[:, HC * c:HC * (c + 1), :], False, True), step)
                elif kind == "qT":
                    u = nth(*step)
                    pe.wait_ge(sg["rope_added"], u + 1)
                    wait_empty(pe, step)
                    for i in range(HC):
                        last = turn(bank(step)[:, i * P:(i + 1) * P], qs[:, u % 2, i * P:(i + 1) * P])
                    fills(last, step)
                elif kind == "attention":
                    for k in range(BANK_Q):
                        pe.wait_ge(bank_emptied[k], ring.before_attention[k])
                    pe.wait_ge(sg["consts_ready"], 1)
                elif kind == "scores":
                    hn, = a
                    b, n = hn // NH, hn % NH
                    if n == 0:
                        for j in range(NJ):
                            wait_emptied(pe, ("latT", NJ * b + j))
                    if n % HC == 0:
                        for j in range(NJ):
                            wait_emptied(pe, ("qT", NJ * b + j, n // HC))
                    if hn >= 2:
                        pe.wait_ge(sg["exp_done"], hn - 1)
                    o = psum[:, BANK_S + hn % 2, :]
                    q = qT[:, (hn // HC) % 2, n % HC, :]
                    mm(o[:, 0:P], id_bf[:], mask_bf[:], True, False)
                    mm(o[0:64, 0:64], q[:, 0:64], kT[:, b, 0:64], False, True)
                    mm(o[64:P, 0:P], q[:, 64:P], kT[:, b, 0:P], False, True)
                    mm(o[:, P:3 * P], q[:, P:2 * P], kT[:, b, :], True, False)
                    mm(o[:, 2 * P:3 * P], id_bf[:], mask_bf[:], False, True).then_inc(sg["scores_ready"], 1)
                elif kind == "probsT":
                    hn, = a
                    pe.wait_ge(sg["probs_normed"], hn + 1)
                    if hn >= 1:
                        pe.wait_ge(sg["probsT_copied"], hn)
                    for i in range(3):
                        last = turn(ps_pt[:, i * P:(i + 1) * P], probs[:, hn % 3, i * P:(i + 1) * P])
                    last.then_inc(sg["probsT_done"], 1)
                elif kind == "pv":
                    pr, = a
                    b = pr // (NH // 2)
                    pe.wait_ge(sg["probsT_copied"], 2 * pr + 2)
                    if pr % 2 == 0 and pr:
                        pe.wait_ge(sg["heads_copied"], pr // 2)
                    c0 = (pr % 2) * S
                    for i in range(2):
                        mm(ps_o[i * KL:(i + 1) * KL, c0:c0 + S], kv[:, 2 * b, 0:KL],
                           probsT[:, (2 * pr + i) % 4, 0:2 * P], True, False)
                    for i in range(2):
                        last = mm(ps_o[i * KL:(i + 1) * KL, c0 + P:c0 + S], kv[:, 2 * b + 1, 0:KL],
                                  probsT[:, (2 * pr + i) % 4, 2 * P:3 * P], False, True)
                    last.then_inc(sg["heads_done"], 1)
                elif kind == "tail":
                    pe.wait_ge(sg["exp_done"], NHU)
                    pe.wait_ge(sg["probsT_copied"], NHU)
                    pe.wait_ge(sg["heads_copied"], NHU // GH)
                elif kind == "y":
                    t, = a
                    pe.wait_ge(sg["heads_copied"], (NH // GH) * (t // NJ + 1))
                    wait_empty(pe, step)
                    for i in range(NH // 2):
                        last = mm(bank(step)[:, 0:D], oT[:, (t // NJ) % 2, i, (t % 2) * P:(t % 2 + 1) * P], w_mo[:, i, :], i == 0, i == NH // 2 - 1)
                    fills(last, step)
                elif kind == "wx":
                    b, = a
                    item = ("fsT", b)
                    if b == 0:
                        pe.wait_ge(ld["fs"], 16)
                        pe.wait_ge(ld["cx"], 16)
                    wait_empty(pe, item)
                    for k in range(KD):
                        for o in range(2):
                            last = turn(bank(item)[:, k * 256 + o * P:k * 256 + (o + 1) * P],
                                        fs[:, b, o, k * P:(k + 1) * P])
                    fills(last, item)
                    item = ("cxT", b)
                    wait_empty(pe, item)
                    for o in range(2):
                        last = turn(bank(item)[:, o * P:(o + 1) * P], cx[:, b, o, :])
                    fills(last, item)
                elif kind == "rwT":
                    pe.wait_ge(ld["rw"], 16)
                    wait_empty(pe, step)
                    for k in range(KD):
                        last = turn(bank(step)[:, k * E:(k + 1) * E], rw[0:E, k * P:(k + 1) * P], ident[0:E, 0:E])
                    fills(last, step)
                elif kind == "shT":
                    i, = a
                    if i == 0:
                        pe.wait_ge(ld["sh"], 48)
                    wait_empty(pe, step)
                    for k in range(KD):
                        for o in range(2):
                            last = turn(bank(step)[:, k * 256 + o * P:k * 256 + (o + 1) * P],
                                        shw[:, i, o, k * P:(k + 1) * P])
                    fills(last, step)
                elif kind == "x_T":
                    b, = a
                    item = ("xT", b)
                    pe.wait_ge(sg["h_ready"], nth("x_stats", b) + 1)
                    wait_empty(pe, item)
                    for k in range(KD):
                        for j in range(NJ):
                            last = turn(bank(item)[:, k * 256 + j * P:k * 256 + (j + 1) * P],
                                        h2[:, j, k * P:(k + 1) * P])
                    fills(last, item)
                elif kind == "x_back":
                    b, = a
                    for item, src in ((("xs", b), xsT), (("ws", b), wsT)):
                        if item[0] == "xs":
                            wait_emptied(pe, ("xT", b))
                        else:
                            pe.wait_ge(sg["scaledT_w"], b + 1)
                        wait_empty(pe, item)
                        for j in range(NJ):
                            for k in range(KD):
                                last = turn(bank(item)[:, j * 256 + k * P:j * 256 + (k + 1) * P],
                                            src[:, k * 256 + j * P:k * 256 + (j + 1) * P])
                        fills(last, item)
                elif kind == "x_qT":
                    b, = a
                    item = ("xqT", b)
                    pe.wait_ge(sg["q_ready"], b + 1)
                    wait_empty(pe, item)
                    for i in range(4):
                        for k in range(KD):
                            o = (i // 2) * 512 + k * 256 + (i % 2) * P
                            last = turn(bf(item)[:, o:o + P], qb[:, i, k * P:(k + 1) * P], id_bf[:])
                    fills(last, item)
                    item = ("xb", b)
                    wait_empty(pe, item)
                    for j in range(NJ):
                        last = mm_halves(bank(item)[:, j * P:(j + 1) * P],
                                         sm[:, b, 10 + j:11 + j].broadcast_to([P, P]), ident)
                    fills(last, item)
                elif kind == "x_mm":
                    b, = a
                    item = ("h1", b)
                    wait_emptied(pe, ("xqT", b))
                    wait_empty(pe, item)
                    f = qTs[:].rearrange("p a d -> p (a d)")
                    for oh_ in range(2):
                        for k in range(KD):
                            w0 = 512 + k * 256 + oh_ * P
                            last = mm(bank(item)[:, oh_ * 256:(oh_ + 1) * 256], f[:, w0:w0 + P],
                                      f[:, k * 256:(k + 1) * 256], k == 0, k == KD - 1)
                    fills(last, item)
                elif kind == "x_back2":
                    b, = a
                    item = ("as", b)
                    pe.wait_ge(sg["scaledT_a"], b + 1)
                    pe.wait_ge(sg["scaledT_c"], b + 1)
                    wait_empty(pe, item)
                    for i in range(4):
                        src = xsT if i < 2 else wsT
                        last = turn(bank(item)[:, i * P:(i + 1) * P], src[:, (i % 2) * P:(i % 2 + 1) * P])
                    fills(last, item)
                elif kind == "x_qT2":
                    b, = a
                    item = ("aqT", b)
                    pe.wait_ge(sg["q2_ready"], b + 1)
                    wait_empty(pe, item)
                    f = qb[:].rearrange("p a d -> p (a d)")
                    for i in range(4):
                        last = turn(bf(item)[:, i * P:(i + 1) * P], f[:, i * P:(i + 1) * P], id_bf[:])
                    fills(last, item)
                    item = ("wb", b)
                    wait_empty(pe, item)
                    for o in range(2):
                        last = mm_halves(bank(item)[:, o * P:(o + 1) * P],
                                         sm[:, b, 25 + o:26 + o].broadcast_to([P, P]), ident)
                    fills(last, item)
                elif kind == "x_mm2":
                    b, = a
                    item = ("h2", b)
                    wait_emptied(pe, ("aqT", b))
                    wait_empty(pe, item)
                    f = qTs[:].rearrange("p a d -> p (a d)")
                    for j in range(NJ):
                        last = mm(bank(item)[:, j * 256:(j + 1) * 256], f[:, j * P:(j + 1) * P], f[:, 256:512])
                    fills(last, item)
                elif kind == "r_T":
                    b, = a
                    item = ("h3T", b)
                    pe.wait_ge(sg["h_ready"], nth("r_stats", b) + 1)
                    wait_empty(pe, item)
                    for k in range(KD):
                        for j in range(NJ):
                            last = turn(bank(item)[:, k * 256 + j * P:k * 256 + (j + 1) * P],
                                        h3[:, b % 2, j, k * P:(k + 1) * P])
                    fills(last, item)
                elif kind == "r_logit":
                    b, = a
                    item = ("logit", b)
                    wait_emptied(pe, ("rwT",))
                    wait_emptied(pe, ("h3T", b))
                    wait_empty(pe, item)
                    for j in range(NJ):
                        for k in range(KD):
                            last = mm_halves(bank(item)[:, j * E:(j + 1) * E], h3T[:, b, k, j * P:(j + 1) * P],
                                      rwT[:, k, :], k == 0, k == KD - 1)
                    fills(last, item)
                elif kind == "r_pos":
                    b, = a
                    item = ("pos", b)
                    pe.wait_ge(sg["chosen_ready"], b + 1)
                    wait_empty(pe, item)
                    for j in range(NJ):
                        t = NJ * b + j
                        last = mm(bank(item)[:, j * E:(j + 1) * E], tri_bf[:], chosen[:, t, :], True, t == 0)
                        for tt in range(t):
                            last = mm(bank(item)[:, j * E:(j + 1) * E], ones_bf[:], chosen[:, tt, :],
                                      False, tt == t - 1)
                    fills(last, item)
                elif kind == "s0":
                    b, = a
                    for i, name in enumerate(("sg", "su")):
                        item = (name, b)
                        wait_emptied(pe, ("shT", i))
                        wait_emptied(pe, ("h3T", b))
                        wait_empty(pe, item)
                        for oh_ in range(2):
                            for k in range(KD):
                                last = mm(bank(item)[:, oh_ * 256:(oh_ + 1) * 256],
                                          shT[:, i, k, oh_ * P:(oh_ + 1) * P], h3T[:, b, k, :], k == 0, k == KD - 1)
                        fills(last, item)
                elif kind == "s1":
                    b, = a
                    item = ("sd", b)
                    wait_emptied(pe, ("shT", 2))
                    wait_emptied(pe, ("su", b))
                    wait_empty(pe, item)
                    for j in range(NJ):
                        for k in range(2):
                            last = mm(bank(item)[:, j * 256:(j + 1) * 256], act_s[:, b % 2, k, j * P:(j + 1) * P],
                                      shT[:, 2, k, :], k == 0, k == 1)
                    fills(last, item)
                elif kind == "xpT":
                    i, = a
                    pe.wait_ge(ld_rows[i], 16)
                    wait_empty(pe, step)
                    for k in range(KD):
                        for s in range(2):
                            last = turn(bank(step)[:, k * 256 + s * P:k * 256 + (s + 1) * P],
                                        rows[:, 2 * i + s, k * P:(k + 1) * P])
                    fills(last, step)
                elif kind == "gate_up":
                    g, = a
                    item = ("gu", g)
                    pe.wait_ge(ld_experts[g], 16 * 3 * XG)
                    for i in range((g * XG * CAP) // 256, min(-(-((g + 1) * XG * CAP + XR - CAP) // 256), NS // 2)):
                        wait_emptied(pe, ("xpT", i))
                    if g == 0:
                        pe.wait_ge(sg["padding_ready"], 1)
                    wait_empty(pe, item)
                    for pair in range(XG // 2):
                        for k in range(KD):
                            for side in range(2):
                                e = g * XG + 2 * pair + side
                                last = mm(bank(item)[side * XR:(side + 1) * XR, pair * 256:(pair + 1) * 256],
                                          xpT[:, k, e * CAP:e * CAP + XR], gate_up_of(e)[:, k, :],
                                          k == 0, k == KD - 1)
                    fills(last, item)
                elif kind == "hidT":
                    g, = a
                    wait_emptied(pe, ("gu", g))
                    wait_empty(pe, step)
                    for pair in range(XG // 2):
                        last = turn(bank(step)[:, pair * P:(pair + 1) * P], hE[:, g % 2, pair * P:(pair + 1) * P])
                    fills(last, step)
                elif kind == "down":
                    g, = a
                    item = ("dn", g)
                    wait_emptied(pe, ("hidT", g))
                    wait_empty(pe, item)
                    for pair in range(XG // 2):
                        for side in range(2):
                            e = g * XG + 2 * pair + side
                            c0 = pair * P + side * XR
                            last = mm(bank(item)[side * XR:(side + 1) * XR, pair * 256:(pair + 1) * 256],
                                      hET[:, g % 2, c0:c0 + XR], down_of(e))
                    fills(last, item)

        @block.scalar
        def _(act):
            def copy(out_, in_, scale=1.0):
                return nc.scalar.activation(out_, in_, ACT.Copy, scale=scale)

            for step in steps:
                kind, a = step[0], step[1:]
                if kind == "hT":
                    t, = a
                    wait_filled(act, step)
                    if t >= 2:
                        wait_filled(act, ("fused", t - 2))
                    empties(copy(hT_f[:, t % 2, :], bank(step)[:, 0:256]), step)
                elif kind == "fused":
                    t, = a
                    wait_filled(act, step)
                    if t >= 1:
                        act.wait_ge(sg["squares_ready"], t)
                        act.wait_ge(sg["lat_ready"], t)
                    nc.scalar.activation(sq[:, 0:QL], bank(step)[:, 0:QL], ACT.Square, scale=float(QL) ** -0.5,
                                         accum_out=ssq[:, t, 0:1])
                    nc.scalar.activation(sq[:, QL:QL + KL], bank(step)[:, QL:QL + KL], ACT.Square,
                                         scale=float(KL) ** -0.5, accum_out=ssq[:, t, 1:2]
                                         ).then_inc(sg["squares_ready"], 1)
                    empties(copy(fused_s, bank(step)[:, 0:QL + KL + DR]), step)
                elif kind == "latT":
                    t, = a
                    wait_filled(act, step)
                    copy(qn0[:, t, :], bank(step)[:, 0:P])
                    copy(kT[:, t // 2, (t % 2) * P:(t % 2 + 1) * P], bank(step)[:, P:2 * P])
                    empties(copy(qn1[:, t, :], bank(step)[0:64, 2 * P:3 * P]), step)
                elif kind == "prepT" and a[0] % 2 == 0:
                    h, = a
                    wait_filled(act, step)
                    if h >= 4:
                        wait_filled(act, ("prepM", h // 2 - 2))
                    empties(copy(wT[:, h % 4, :], bank(step)[:, 0:320]), step)
                elif kind == "q":
                    t, c = a
                    u = nth(*step)
                    wait_filled(act, step)
                    if u >= 2:
                        wait_filled(act, q_order[u - 2])
                    if u >= 2:
                        act.wait_ge(sg["rope_added"], u - 1)
                    empties(copy(qs[:, u % 2], bank(step), SM_SCALE), step)
                elif kind == "qT":
                    t, c = a
                    b = t // NJ
                    wait_filled(act, step)
                    C = (NH // HC) * b + c
                    if C >= 2:
                        act.wait_ge(sg["scores_ready"], HC * (C - 1))
                    empties(copy(qT[:, C % 2, :, (t % 2) * P:(t % 2 + 1) * P],
                                 bank(step).rearrange("p (h m) -> p h m", h=HC)), step)
                elif kind == "scores":
                    hn, = a
                    act.wait_ge(sg["max_ready"], hn + 1)
                    if hn >= 3:
                        act.wait_ge(sg["probsT_done"], hn - 2)
                    s = psum[:, BANK_S + hn % 2, :]
                    nc.scalar.activation(probs[:, hn % 3, 0:P], s[:, 0:P], ACT.Exp, bias=nmax[:, hn, 0:1],
                                         accum_out=sums[:, hn, 0:1])
                    nc.scalar.activation(probs[:, hn % 3, P:3 * P], s[:, P:3 * P], ACT.Exp, bias=nmax[:, hn, 1:2],
                                         accum_out=sums[:, hn, 1:2]).then_inc(sg["exp_done"], 1)
                elif kind == "pv" and a[0] % 2 == 1:
                    pr, = a
                    b, i0 = pr // (NH // 2), (pr % (NH // 2)) - 1
                    act.wait_ge(sg["heads_done"], pr + 1)
                    if b >= 2 and i0 == 0:
                        for j in range(NJ):
                            wait_filled(act, ("y", NJ * (b - 2) + j))
                    if b == 1 and i0 == 0:
                        act.wait_ge(sg["xp_zeroed"], 16 * (NS // 2))
                    copy(oT[:, b % 2, i0:i0 + 2, :].rearrange("p i t -> p (i t)"), ps_o
                         ).then_inc(sg["heads_copied"], 1)
                elif kind == "wx":
                    b, = a
                    if b >= 1:
                        act.wait_ge(sg["scaledT_w"], b)
                        act.wait_ge(sg["scaledT_c"], b)
                    wait_filled(act, ("fsT", b))
                    empties(copy(fsT[:], bank(("fsT", b))), ("fsT", b))
                    wait_filled(act, ("cxT", b))
                    empties(copy(cxT[:], bank(("cxT", b))[:, 0:256]), ("cxT", b))
                elif kind == "rwT":
                    wait_filled(act, step)
                    empties(copy(rwT[:].rearrange("p k e -> p (k e)"), bank(step)[:, 0:KD * E]), step)
                elif kind == "shT":
                    i, = a
                    wait_filled(act, step)
                    empties(copy(shT[:, i].rearrange("p k d -> p (k d)"), bank(step)), step)
                elif kind == "x_scale":
                    b, = a
                    act.wait_ge(sg["smooth_ready"], b + 1)
                    if b >= 1:
                        wait_filled(act, ("as", b - 1))
                    for k in range(KD):
                        last = copy(xsT[:, k * 256:(k + 1) * 256], bank(("xT", b))[:, k * 256:(k + 1) * 256],
                                    sm[:, b, 8 + k:9 + k])
                    empties(last, ("xT", b))
                elif kind == "x_qscale":
                    b, = a
                    act.wait_ge(sg["inv_ready"], b + 1)
                    if b >= 1:
                        act.wait_ge(sg["q2_ready"], b)
                    for i, item in enumerate((("xs", b), ("ws", b))):
                        for j in range(2):
                            last = copy(qa[:, 2 * i + j, :], bank(item)[:, j * 256:(j + 1) * 256],
                                        sm[:, b, 14 + 2 * i + j:15 + 2 * i + j])
                        empties(last, item)
                elif kind == "x_qT":
                    b, = a
                    wait_filled(act, ("xqT", b))
                    if b >= 1:
                        wait_filled(act, ("h2", b - 1))
                    empties(copy(qTs[:].rearrange("p a d -> p (a d)"), bank(("xqT", b)).bitcast(BF16)), ("xqT", b))
                    wait_filled(act, ("xb", b))
                    if b >= 1:
                        wait_emptied(act, ("h1", b - 1))
                    empties(copy(sbc[:, 0, :], bank(("xb", b))[:, 0:256]), ("xb", b))
                elif kind == "x_tanh":
                    b, = a
                    wait_emptied(act, ("h1", b))
                    nc.scalar.activation(gu[:, 2, :], gu[:, 0, :], ACT.Tanh, scale=0.5).then_inc(sg["gate_tanh"], 1)
                elif kind == "x_scale2":
                    b, = a
                    act.wait_ge(sg["smooth_ready2"], b + 1)
                    wait_filled(act, ("xs", b))
                    copy(xsT[:, 0:256], gu[:, 3, :], sm[:, b, 22:23]).then_inc(sg["scaledT_a"], 1)
                elif kind == "x_qscale2":
                    b, = a
                    act.wait_ge(sg["inv2_ready"], b + 1)
                    act.wait_ge(sg["q_ready"], b + 1)
                    f = reg_r[:, 0:1024]
                    for i in range(4):
                        last = copy(f[:, i * P:(i + 1) * P], bank(("as", b))[:, i * P:(i + 1) * P],
                                    sm[:, b, 27 + i:28 + i])
                    empties(last, ("as", b))
                elif kind == "x_qT2":
                    b, = a
                    wait_filled(act, ("aqT", b))
                    wait_filled(act, ("h1", b))
                    empties(copy(qTs[:].rearrange("p a d -> p (a d)")[:, 0:512],
                                 bank(("aqT", b)).bitcast(BF16)[:, 0:512]), ("aqT", b))
                    wait_filled(act, ("wb", b))
                    empties(copy(sbc[:, 1, :], bank(("wb", b))[:, 0:256]), ("wb", b))
                elif kind == "r_T":
                    b, = a
                    wait_filled(act, ("h3T", b))
                    empties(copy(h3T[:, b].rearrange("p k t -> p (k t)"), bank(("h3T", b))), ("h3T", b))
                elif kind == "r_logit":
                    b, = a
                    wait_filled(act, ("logit", b))
                    if b >= 1:
                        act.wait_ge(sg["weights_ready"], b)
                    empties(nc.scalar.activation(sc[:, 0, :], bank(("logit", b))[:, 0:NJ * E], ACT.Exp, scale=-1.0),
                            ("logit", b))
                elif kind == "s0":
                    b, = a
                    wait_filled(act, ("sg", b))
                    if b >= 1:
                        wait_emptied(act, ("su", b - 1))
                    nc.scalar.activation(es[:, 0, :], bank(("sg", b)), ACT.Tanh, scale=0.5
                                         ).then_inc(sg["shared_tanh"], 1)
                elif kind == "xpT" and a[0] % 2 == 0:
                    i, = a
                    wait_filled(act, step)
                    empties(copy(xpT[:, :, i * 256:(i + 1) * 256],
                                 bank(step).rearrange("p (k s) -> p k s", k=KD)), step)
                elif kind == "gate_up":
                    g, = a
                    wait_filled(act, ("gu", g))
                    if g >= 2:
                        wait_emptied(act, ("gu", g - 2))
                    nc.scalar.activation(
                        th[:, g % 2, :].rearrange("p (i m) -> p i m", i=2),
                        bank(("gu", g)).rearrange("p (i two m) -> p i two m", i=2, two=2)[:, :, 0, :],
                        ACT.Tanh, scale=0.5).then_inc(sg["expert_tanh"], 1)
                elif kind == "hidT":
                    g, = a
                    wait_filled(act, step)
                    if g >= 2:
                        wait_filled(act, ("dn", g - 2))
                    empties(copy(hET[:, g % 2, :], bank(step)[:, 0:256]), step)
                elif kind == "down":
                    g, = a
                    wait_filled(act, ("dn", g))
                    if g >= 3:
                        act.wait_ge(y_stored[g - 3], 16)
                    empties(copy(ybuf[:, g % 3, :], bank(("dn", g))), ("dn", g))

        @block.vector
        def _(dve):
            v = nc.vector
            chain = [0]

            def link(ins):
                chain[0] += 1
                ins.then_inc(sg["dve_chain"], 1)
                dve.wait_ge(sg["dve_chain"], chain[0])

            def normalise(hn):
                dve.wait_ge(sg["exp_done"], hn + 1)
                link(v.reciprocal(rsum[:, hn, :], sums[:, hn, :]))
                pr = probs[:, hn % 3, :]
                v.tensor_scalar(pr[:, 0:P], pr[:, 0:P], rsum[:, hn, 0:1], None, ALU.mult)
                v.tensor_scalar(pr[:, P:3 * P], pr[:, P:3 * P], rsum[:, hn, 1:2], None, ALU.mult
                                ).then_inc(sg["probs_normed"], 1)

            def ln_stats(tag, b):
                for j in range(NJ):
                    link(v.bn_stats(stats[:, j, :], xres[:, NJ * b + j, :]))
                for j in range(NJ):
                    last = v.bn_aggr(mv[:, tag, NJ * b + j, :], stats[:, j, :])
                last.then_inc(sg["ln_stats"], 1)

            def ln_normalise(tag, b, i, dst):
                dve.wait_ge(sg["ln_rstd"], i + 1)
                for j in range(NJ):
                    t = NJ * b + j
                    last = v.tensor_scalar(dst(j), xres[:, t, :], mv[:, tag, t, 0:1], rstd[:, tag, t:t + 1],
                                           ALU.subtract, ALU.mult)
                last.then_inc(sg["h_ready"], 1)

            for step in steps:
                kind, a = step[0], step[1:]
                if kind == "setup":
                    v.memset(zeros, 0.0).then_inc(sg["zeros_ready"], 1)
                    link(v.memset(ones_bf[:], 1.0))
                elif kind == "ln1_stats":
                    b, = a
                    dve.wait_ge(ld[f"x{b}"], 16)
                    ln_stats(0, b)
                elif kind == "ln1_norm":
                    b, = a
                    if b >= 1:
                        for j in range(NJ):
                            wait_filled(dve, ("hT", NJ * (b - 1) + j))
                    ln_normalise(0, b, nth("ln1_stats", b), lambda j: hn_f[:, j, :])
                    if b == 0:
                        dve.wait_ge(ld["consts"], 16)
                        v.tensor_copy(id_bf[:], ident)
                        v.tensor_copy(mask_bf[:], c_(C_MASK, P))
                        v.tensor_copy(tri_bf[:], c_(C_TRI, P)).then_inc(sg["consts_ready"], 1)
                elif kind == "latents":
                    t, = a
                    if t == 0:
                        dve.wait_ge(ld["gam"], 32)
                    dve.wait_ge(sg["rms_ready"], t + 1)
                    wait_emptied(dve, ("fused", t))
                    if t >= 2:
                        wait_filled(dve, ("latT", t - 2))
                    v.scalar_tensor_tensor(qn[:, t % 2, :], fused_s[:, 0:QL], rrms[:, t, 0:1], gam_q[:],
                                           ALU.mult, ALU.mult)
                    v.scalar_tensor_tensor(kv[:, t, 0:KL], fused_s[:, QL:QL + KL], rrms[:, t, 1:2], gam_kv[:],
                                           ALU.mult, ALU.mult)
                    if t >= 1:
                        dve.wait_ge(sg["lat_ready"], t)
                    kp = fused_s[:, QL + KL:QL + KL + DR]
                    o = (t % NJ) * DR
                    v.tensor_tensor(kr[:, 0, :], kp, c_(C_COS + o, DR), ALU.mult)
                    link(v.tensor_tensor(kr[:, 1, :].rearrange("p (two x) -> p two x", two=2)[:, ::-1, :],
                                         kp.rearrange("p (two x) -> p two x", two=2),
                                         c_(C_SIN + o, DR).rearrange("p (two x) -> p two x", two=2), ALU.mult))
                    v.tensor_tensor(kv[:, t, KL:], kr[:, 0, :], kr[:, 1, :], ALU.add).then_inc(sg["lat_ready"], 1)
                elif kind == "prepT" and a[0] % 2 == 1:
                    h, = a
                    wait_filled(dve, step)
                    if h >= 4:
                        wait_filled(dve, ("prepM", h // 2 - 2))
                    empties(v.tensor_copy(wT[:, h % 4, :], bank(step)[:, 0:320]), step)
                elif kind == "prepM":
                    p, = a
                    wait_filled(dve, step)
                    pb = bank(step)
                    v.tensor_copy(wf0[:, 2 * p:2 * p + 2, 0:KL], pb[:, 0:128].rearrange("p (h m) -> p h m", h=2))
                    v.tensor_copy(wf1[:, 2 * p:2 * p + 2, 0:KL],
                                  pb[0:64, 128:256].rearrange("p (h m) -> p h m", h=2))
                    empties(v.tensor_copy(w_mo[:, p, :], pb[:, 256:512]), step)
                elif kind == "rope":
                    t, c = a
                    u = nth(*step)
                    wait_emptied(dve, ("q",) + a)
                    if u >= 2:
                        dve.wait_ge(sg["rope_added"], u - 1)
                    o = (t % NJ) * DR
                    qp = qs[:, u % 2].rearrange("p (h m) -> p h m", h=HC)[:, :, KL:]
                    v.tensor_tensor(
                        qr[:, u % 2].rearrange("p (h two x) -> p h two x", h=HC, two=2)[:, :, ::-1, :],
                        qp.rearrange("p h (two x) -> p h two x", two=2),
                        c_(C_SIN + o, DR).rearrange("p (o two x) -> p o two x", o=1, two=2
                                                    ).broadcast_to([P, HC, 2, DR // 2]), ALU.mult)
                    v.tensor_tensor(qp, qp,
                                    c_(C_COS + o, DR).rearrange("p (o x) -> p o x", o=1).broadcast_to([P, HC, DR]),
                                    ALU.mult).then_inc(sg["rope_parts"], 1)
                elif kind == "scores":
                    hn, = a
                    if hn >= 1:
                        normalise(hn - 1)
                    dve.wait_ge(sg["scores_ready"], hn + 1)
                    s = psum[:, BANK_S + hn % 2, :]
                    v.tensor_reduce(nmax[:, hn, 0:1], s[:, 0:P], AX.X, ALU.max, negate=True)
                    v.tensor_reduce(nmax[:, hn, 1:2], s[:, P:3 * P], AX.X, ALU.max, negate=True
                                    ).then_inc(sg["max_ready"], 1)
                elif kind == "probsT":
                    hn, = a
                    if hn == NHU - 2:
                        normalise(NHU - 1)
                    dve.wait_ge(sg["probsT_done"], hn + 1)
                    if hn >= 4:
                        dve.wait_ge(sg["heads_done"], hn // 2 - 1)
                    v.tensor_copy(probsT[:, hn % 4, :], ps_pt[:, 0:384]).then_inc(sg["probsT_copied"], 1)
                elif kind == "y_add":
                    t, = a
                    item = ("y", t)
                    wait_filled(dve, item)
                    empties(v.tensor_tensor(xres[:, t, :], bank(item)[:, 0:D], xres[:, t, :], ALU.add), item)
                    if t == NT - 1:
                        v.memset(xpT[:, :, SLOTS:], 0.0).then_inc(sg["padding_ready"], 1)
                elif kind == "wx":
                    b, = a
                    wait_emptied(dve, ("fsT", b))
                    v.tensor_reduce(rden[:, b, 0:2], fsT[:].rearrange("p (k o) -> p k o", k=KD), AX.X, ALU.max,
                                    apply_absolute_value=True)
                    wait_emptied(dve, ("cxT", b))
                    link(v.tensor_reduce(rden[:, b, 2:3], cxT[:], AX.X, ALU.max, apply_absolute_value=True))
                    link(v.tensor_scalar(rden[:, b, :], rden[:, b, :], EPS_Q, None, ALU.max))
                    link(v.reciprocal(rden[:, b, :], rden[:, b, :]))
                elif kind == "x_stats":
                    b, = a
                    for j in range(NJ):
                        wait_emptied(dve, ("y", NJ * b + j))
                    ln_stats(1, b)
                elif kind == "x_norm":
                    b, = a
                    if b >= 1:
                        wait_filled(dve, ("xT", b - 1))
                    ln_normalise(1, b, nth("x_stats", b), lambda j: h2[:, j, :])
                elif kind == "x_T":
                    b, = a
                    item = ("xT", b)
                    wait_filled(dve, item)
                    link(v.tensor_reduce(sm[:, b, 0:2], bank(item).rearrange("p (k t) -> p k t", k=KD), AX.X, ALU.max,
                                         apply_absolute_value=True))
                    v.scalar_tensor_tensor(sm[:, b, 2:4], sm[:, b, 0:2], EPS_Q, rden[:, b, 0:2], ALU.max, ALU.mult
                                           ).then_inc(sg["ratio_ready"], 1)
                elif kind == "x_smooth":
                    b, = a
                    dve.wait_ge(sg["smooth_root"], b + 1)
                    link(v.tensor_scalar(sm[:, b, 6:8], sm[:, b, 4:6], EPS_Q, None, ALU.max))
                    v.reciprocal(sm[:, b, 8:10], sm[:, b, 6:8]).then_inc(sg["smooth_ready"], 1)
                    wait_emptied(dve, ("fsT", b))
                    if b >= 1:
                        wait_filled(dve, ("as", b - 1))
                    for k in range(KD):
                        last = v.tensor_scalar(wsT[:, k * 256:(k + 1) * 256], fsT[:, k * 256:(k + 1) * 256],
                                               sm[:, b, 6 + k:7 + k], None, ALU.mult)
                    last.then_inc(sg["scaledT_w"], 1)
                elif kind == "x_back":
                    b, = a
                    for i, item in enumerate((("xs", b), ("ws", b))):
                        wait_filled(dve, item)
                        last = v.tensor_reduce(sm[:, b, 10 + 2 * i:12 + 2 * i],
                                               bank(item).rearrange("p (j d) -> p j d", j=2), AX.X, ALU.max,
                                               apply_absolute_value=True)
                    link(last)
                    link(v.tensor_scalar(sm[:, b, 10:14], sm[:, b, 10:14], EPS_Q, 1.0 / QMAX, ALU.max, ALU.mult))
                    v.reciprocal(sm[:, b, 14:18], sm[:, b, 10:14]).then_inc(sg["inv_ready"], 1)
                elif kind == "x_round":
                    b, = a
                    for item in (("xs", b), ("ws", b)):
                        wait_emptied(dve, item)
                    link(v.tensor_scalar(qa, qa, QMAX, -QMAX, ALU.min, ALU.max))
                    if b >= 1:
                        wait_filled(dve, ("aqT", b - 1))
                    v.tensor_scalar(qb[:], qa, ROUND, ROUND, ALU.add, ALU.subtract).then_inc(sg["q_ready"], 1)
                elif kind == "x_mm":
                    b, = a
                    item = ("h1", b)
                    wait_filled(dve, item)
                    wait_emptied(dve, ("xb", b))
                    for i in range(2):
                        last = v.scalar_tensor_tensor(gu[:, i, :], bank(item)[:, i * 256:(i + 1) * 256],
                                                      sm[:, b, 12 + i:13 + i], sbc[:, 0, :], ALU.mult, ALU.mult)
                    empties(last, item)
                elif kind == "x_gate":
                    b, = a
                    dve.wait_ge(sg["gate_tanh"], b + 1)
                    link(v.scalar_tensor_tensor(gu[:, 2, :], gu[:, 2, :], 1.0, gu[:, 0, :], ALU.add, ALU.mult))
                    link(v.scalar_tensor_tensor(gu[:, 3, :], gu[:, 2, :], 0.5, gu[:, 1, :], ALU.mult, ALU.mult))
                    link(v.tensor_reduce(sm[:, b, 18:19], gu[:, 3, :], AX.X, ALU.max, apply_absolute_value=True))
                    v.scalar_tensor_tensor(sm[:, b, 19:20], sm[:, b, 18:19], EPS_Q, rden[:, b, 2:3], ALU.max,
                                           ALU.mult).then_inc(sg["ratio2_ready"], 1)
                elif kind == "x_smooth2":
                    b, = a
                    dve.wait_ge(sg["smooth_root2"], b + 1)
                    link(v.tensor_scalar(sm[:, b, 21:22], sm[:, b, 20:21], EPS_Q, None, ALU.max))
                    v.reciprocal(sm[:, b, 22:23], sm[:, b, 21:22]).then_inc(sg["smooth_ready2"], 1)
                    wait_filled(dve, ("ws", b))
                    v.tensor_scalar(wsT[:, 0:256], cxT[:], sm[:, b, 21:22], None, ALU.mult
                                    ).then_inc(sg["scaledT_c"], 1)
                elif kind == "x_back2":
                    b, = a
                    item = ("as", b)
                    wait_filled(dve, item)
                    link(v.tensor_reduce(sm[:, b, 23:27], bank(item).rearrange("p (i m) -> p i m", i=4), AX.X, ALU.max,
                                         apply_absolute_value=True))
                    link(v.tensor_scalar(sm[:, b, 23:27], sm[:, b, 23:27], EPS_Q, 1.0 / QMAX, ALU.max, ALU.mult))
                    v.reciprocal(sm[:, b, 27:31], sm[:, b, 23:27]).then_inc(sg["inv2_ready"], 1)
                elif kind == "x_round2":
                    b, = a
                    wait_emptied(dve, ("as", b))
                    fa = reg_r[:, 0:1024][:, 0:512]
                    fb = qb[:].rearrange("p a d -> p (a d)")[:, 0:512]
                    link(v.tensor_scalar(fa, fa, QMAX, -QMAX, ALU.min, ALU.max))
                    wait_filled(dve, ("xqT", b))
                    v.tensor_scalar(fb, fa, ROUND, ROUND, ALU.add, ALU.subtract).then_inc(sg["q2_ready"], 1)
                elif kind == "x_mm2":
                    b, = a
                    item = ("h2", b)
                    wait_filled(dve, item)
                    wait_emptied(dve, ("wb", b))
                    for j in range(NJ):
                        last = v.scalar_tensor_tensor(gu[:, j, :], bank(item)[:, j * 256:(j + 1) * 256],
                                                      sm[:, b, 23 + j:24 + j], sbc[:, 1, :], ALU.mult, ALU.mult)
                    empties(last, item)
                    wait_emptied(dve, item)
                    xb = xres[:, NJ * b:NJ * (b + 1), :]
                    link(v.tensor_tensor(xb, xb, gu[:, 0:2, :], ALU.add))
                elif kind == "r_stats":
                    b, = a
                    ln_stats(2, b)
                elif kind == "r_norm":
                    b, = a
                    if b >= 2:
                        dve.wait_ge(scattered[b - 2], 16 * NJ * TOPK)
                        wait_filled(dve, ("h3T", b - 2))
                    ln_normalise(2, b, nth("r_stats", b), lambda j: h3[:, b % 2, j, :])
                elif kind == "r_groups":
                    b, = a
                    wait_emptied(dve, ("logit", b))
                    if b == 0:
                        dve.wait_ge(ld["bias"], 16)
                    link(v.tensor_scalar(sc[:, 0, :], sc[:, 0, :], 1.0, None, ALU.add))
                    link(v.reciprocal(sc[:, 1, :], sc[:, 0, :]))
                    link(v.tensor_tensor(
                        sc[:, 2, :].rearrange("p (j e) -> p j e", j=NJ), sc[:, 1, :].rearrange("p (j e) -> p j e", j=NJ),
                        bias_e[:].rearrange("p (o e) -> p o e", o=1).broadcast_to([P, NJ, E]), ALU.add))
                    n2 = NJ * NG
                    quad = sc[:, 2, :].rearrange("p (g two x) -> p g two x", two=2, x=2)
                    hi = rt[:, 0, 0:2 * n2].rearrange("p (g two) -> p g two", two=2)
                    lo = rt[:, 1, 0:2 * n2].rearrange("p (g two) -> p g two", two=2)
                    v.tensor_tensor(hi, quad[:, :, :, 0], quad[:, :, :, 1], ALU.max)
                    link(v.tensor_tensor(lo, quad[:, :, :, 0], quad[:, :, :, 1], ALU.min))
                    v.tensor_tensor(rt[:, 2, 0:n2], hi[:, :, 0], hi[:, :, 1], ALU.max)
                    v.tensor_tensor(rt[:, 3, 0:n2], hi[:, :, 0], hi[:, :, 1], ALU.min)
                    link(v.tensor_tensor(rt[:, 4, 0:n2], lo[:, :, 0], lo[:, :, 1], ALU.max))
                    link(v.tensor_tensor(rt[:, 5, 0:n2], rt[:, 3, 0:n2], rt[:, 4, 0:n2], ALU.max))
                    gs = rt[:, 6, 0:n2]
                    link(v.tensor_tensor(gs, rt[:, 2, 0:n2], rt[:, 5, 0:n2], ALU.add))
                elif kind == "r_best":
                    n2 = NJ * NG
                    gs = rt[:, 6, 0:n2]
                    for j in range(NJ):
                        last = v.max(top[:, j, :], gs[:, j * NG:(j + 1) * NG])
                    link(last)
                    for j in range(NJ):
                        last = v.max_index(topi[:, j, :], top[:, j, :], gs[:, j * NG:(j + 1) * NG])
                    link(last)
                    link(v.tensor_copy(tif[:, :, 0:TKG], topi[:, :, 0:TKG]))
                    eqg = rt[:, 7, 0:NJ * TKG * NG].rearrange("p (j k g) -> p j k g", j=NJ, k=TKG)
                    link(v.tensor_tensor(
                        eqg, c_(C_I8, NG).rearrange("p (a o g) -> p a o g", a=1, o=1).broadcast_to([P, NJ, TKG, NG]),
                        tif[:, :, 0:TKG].rearrange("p j (k o) -> p j k o", o=1).broadcast_to([P, NJ, TKG, NG]),
                        ALU.is_equal))
                    gm = rt[:, 8, 0:n2]
                    link(v.tensor_reduce(gm.rearrange("p (j g) -> p j g", j=NJ),
                                         eqg.rearrange("p j k g -> p j g k"), AX.X, ALU.add))
                    mk = rt[:, 9, :]
                    link(v.tensor_tensor(mk.rearrange("p (g x) -> p g x", x=EG),
                                         sc[:, 2, :].rearrange("p (g x) -> p g x", x=EG),
                                         gm.rearrange("p (g o) -> p g o", o=1).broadcast_to([P, n2, EG]), ALU.mult))
                    link(v.tensor_scalar(mk, mk, 0.0, None, ALU.add))
                elif kind == "r_choose":
                    b, = a
                    mk = rt[:, 9, :]
                    for j in range(NJ):
                        last = v.max(top[:, j, :], mk[:, j * E:(j + 1) * E])
                    link(last)
                    for j in range(NJ):
                        last = v.max_index(topi[:, j, :], top[:, j, :], mk[:, j * E:(j + 1) * E])
                    link(last)
                    link(v.tensor_copy(tif[:], topi[:, :, 0:TOPK]))
                    oh4 = oh.rearrange("p (j k e) -> p j k e", j=NJ, k=TOPK)
                    ohp4 = ohp.rearrange("p (j k e) -> p j k e", j=NJ, k=TOPK)
                    link(v.tensor_tensor(
                        oh4, c_(C_I32, E).rearrange("p (a o g) -> p a o g", a=1, o=1).broadcast_to([P, NJ, TOPK, E]),
                        tif[:].rearrange("p j (k o) -> p j k o", o=1).broadcast_to([P, NJ, TOPK, E]), ALU.is_equal))
                    with nc.allow_low_precision("zeros and ones"):
                        v.tensor_reduce(chosen[:, NJ * b:NJ * (b + 1), :], oh4.rearrange("p j k e -> p j e k"), AX.X,
                                        ALU.add).then_inc(sg["chosen_ready"], 1)
                elif kind == "r_weights":
                    b, = a
                    oh4 = oh.rearrange("p (j k e) -> p j k e", j=NJ, k=TOPK)
                    ohp4 = ohp.rearrange("p (j k e) -> p j k e", j=NJ, k=TOPK)
                    link(v.tensor_tensor(
                        ohp4, oh4, sc[:, 1, :].rearrange("p (j o e) -> p j o e", j=NJ, o=1
                                                         ).broadcast_to([P, NJ, TOPK, E]), ALU.mult))
                    wk = slotf[:, 0, :].rearrange("p (j k) -> p j k", j=NJ)
                    link(v.tensor_reduce(wk, ohp4, AX.X, ALU.add))
                    ws_ = rt[:, 10, 0:NJ]
                    link(v.tensor_reduce(ws_, wk, AX.X, ALU.add))
                    link(v.tensor_scalar(ws_, ws_, 1e-20, None, ALU.add))
                    link(v.reciprocal(ws_, ws_))
                    link(v.tensor_scalar(ws_, ws_, 2.5, None, ALU.mult))
                    v.tensor_tensor(wk, wk, ws_.rearrange("p (j o) -> p j o", o=1).broadcast_to([P, NJ, TOPK]),
                                    ALU.mult).then_inc(sg["weights_ready"], 1)
                elif kind == "r_slots":
                    b, = a
                    item = ("pos", b)
                    wait_filled(dve, item)
                    pos = bank(item)[:, 0:NJ * E]
                    oh4 = oh.rearrange("p (j k e) -> p j k e", j=NJ, k=TOPK)
                    ohp4 = ohp.rearrange("p (j k e) -> p j k e", j=NJ, k=TOPK)
                    v.tensor_scalar(rt[:, 0, :], pos, float(CAP), NOSLOT, ALU.is_ge, ALU.mult)
                    empties(v.tensor_tensor(
                        rt[:, 1, :].rearrange("p (j e) -> p j e", j=NJ), pos.rearrange("p (j e) -> p j e", j=NJ),
                        c_(C_SLOT0, E).rearrange("p (o e) -> p o e", o=1).broadcast_to([P, NJ, E]), ALU.add), item)
                    wait_emptied(dve, item)
                    link(v.tensor_tensor(rt[:, 2, :], rt[:, 0, :], rt[:, 1, :], ALU.add))
                    link(v.tensor_tensor(
                        ohp4, oh4, rt[:, 2, :].rearrange("p (j o e) -> p j o e", j=NJ, o=1
                                                         ).broadcast_to([P, NJ, TOPK, E]), ALU.mult))
                    sl = slotf[:, 1, :]
                    link(v.tensor_reduce(sl.rearrange("p (j k) -> p j k", j=NJ), ohp4, AX.X, ALU.add))
                    tt = slice(NJ * b, NJ * (b + 1))
                    v.tensor_copy(scat[:, tt, :].rearrange("p j k -> p (j k)"), sl)
                    link(v.tensor_scalar(slotf[:, 3, :], sl, float(SLOTS - 1), None, ALU.min))
                    v.scalar_tensor_tensor(gath[:, tt, :].rearrange("p j k -> p (j k)"),
                                           tif[:].rearrange("p j k -> p (j k)"), float(XR - CAP), slotf[:, 3, :],
                                           ALU.mult, ALU.add)
                    link(v.tensor_scalar(slotf[:, 2, :], sl, float(SLOTS), None, ALU.is_lt))
                    dve.wait_ge(sg["weights_ready"], b + 1)
                    v.tensor_tensor(wtok[:, tt, :].rearrange("p j k -> p (j k)"), slotf[:, 0, :], slotf[:, 2, :],
                                    ALU.mult).then_inc(sg["slots_ready"], 1)
                elif kind == "s0":
                    b, = a
                    dve.wait_ge(sg["shared_tanh"], b + 1)
                    empties(v.scalar_tensor_tensor(es[:, 1, :], es[:, 0, :], 1.0, bank(("sg", b)),
                                                   ALU.add, ALU.mult), ("sg", b))
                    wait_emptied(dve, ("sg", b))
                    wait_filled(dve, ("su", b))
                    if b >= 2:
                        wait_filled(dve, ("sd", b - 2))
                    empties(v.scalar_tensor_tensor(act_s[:, b % 2].rearrange("p k t -> p (k t)"), es[:, 1, :], 0.5,
                                                   bank(("su", b)), ALU.mult, ALU.mult), ("su", b))
                elif kind == "s1":
                    b, = a
                    item = ("sd", b)
                    wait_filled(dve, item)
                    xb = xres[:, NJ * b:NJ * (b + 1), :].rearrange("p j d -> p (j d)")
                    empties(v.tensor_tensor(xb, bank(item), xb, ALU.add), item)
                elif kind == "xpT" and a[0] % 2 == 1:
                    i, = a
                    wait_filled(dve, step)
                    empties(v.tensor_copy(xpT[:, :, i * 256:(i + 1) * 256],
                                          bank(step).rearrange("p (k s) -> p k s", k=KD)), step)
                elif kind == "gate_up":
                    g, = a
                    item = ("gu", g)
                    dve.wait_ge(sg["expert_tanh"], g + 1)
                    gu4 = bank(item).rearrange("p (i two m) -> p i two m", i=2, two=2)
                    tg = th[:, g % 2, :].rearrange("p (i m) -> p i m", i=2)
                    gg = th[:, 2 + g % 2, :].rearrange("p (i m) -> p i m", i=2)
                    link(v.scalar_tensor_tensor(gg, tg, 1.0, gu4[:, :, 0, :], ALU.add, ALU.mult))
                    if g >= 2:
                        wait_filled(dve, ("hidT", g - 2))
                    empties(v.scalar_tensor_tensor(hE[:, g % 2, :].rearrange("p (i m) -> p i m", i=2), gg, 0.5,
                                                   gu4[:, :, 1, :], ALU.mult, ALU.mult), item)
                elif kind == "combine":
                    t, = a
                    if t == 0:
                        for b in range(B):
                            wait_emptied(dve, ("sd", b))
                    for k in range(TOPK):
                        n = (t % 2) * TOPK + k
                        dve.wait_ge(gathered[n], 16 * (t // 2 + 1))
                        ins = v.scalar_tensor_tensor(xres[:, t, :], gbuf[:, n, :], wtok[:, t, k:k + 1],
                                                     xres[:, t, :], ALU.mult, ALU.add)
                        if k < TOPK - 1:
                            link(ins)
                    ins.then_inc(sg["combined"], 1)

        @block.gpsimd
        def _(pool):
            g = nc.gpsimd
            chain = [0]

            def link(ins):
                chain[0] += 1
                ins.then_inc(sg["pool_chain"], 1)
                pool.wait_ge(sg["pool_chain"], chain[0])

            for step in steps:
                kind, a = step[0], step[1:]
                if kind == "setup":
                    g.memset(neg_half[:], -0.5).then_inc(sg["halves_ready"], 1)
                    g.memset(pos_half[:], 0.5).then_inc(sg["halves_ready"], 1)
                    pool.wait_ge(sg["halves_ready"], 2)
                elif kind in ("ln1_stats", "x_stats", "r_stats"):
                    b, = a
                    tag = ("ln1_stats", "x_stats", "r_stats").index(kind)
                    tt = slice(NJ * b, NJ * (b + 1))
                    pool.wait_ge(sg["ln_stats"], nth(*step) + 1)
                    link(g.tensor_scalar(vtmp[:, tag, tt], mv[:, tag, tt, 1], EPS_LN, None, ALU.add))
                    g.tensor_tensor(rstd[:, tag, tt], vtmp[:, tag, tt], neg_half[:].broadcast_to([P, NJ]), ALU.pow
                                    ).then_inc(sg["ln_rstd"], 1)
                elif kind == "fused":
                    t, = a
                    pool.wait_ge(sg["squares_ready"], t + 1)
                    link(g.tensor_scalar(weps[:, t, :], ssq[:, t, :], EPS_RMS, None, ALU.add))
                    g.tensor_tensor(rrms[:, t, :], weps[:, t, :], neg_half[:].broadcast_to([P, 2]), ALU.pow
                                    ).then_inc(sg["rms_ready"], 1)
                elif kind == "rope":
                    u = nth(*step)
                    pool.wait_ge(sg["rope_parts"], u + 1)
                    qp = qs[:, u % 2].rearrange("p (h m) -> p h m", h=HC)[:, :, KL:]
                    g.tensor_tensor(qp, qp, qr[:, u % 2].rearrange("p (h x) -> p h x", h=HC), ALU.add
                                    ).then_inc(sg["rope_added"], 1)
                elif kind == "x_T":
                    b, = a
                    pool.wait_ge(sg["ratio_ready"], b + 1)
                    g.tensor_tensor(sm[:, b, 4:6], sm[:, b, 2:4], pos_half[:].broadcast_to([P, 2]), ALU.pow
                                    ).then_inc(sg["smooth_root"], 1)
                elif kind == "x_gate":
                    b, = a
                    pool.wait_ge(sg["ratio2_ready"], b + 1)
                    g.tensor_tensor(sm[:, b, 20:21], sm[:, b, 19:20], pos_half[:], ALU.pow
                                    ).then_inc(sg["smooth_root2"], 1)
                elif kind == "scatter":
                    b, i = a
                    if i == 0:
                        pool.wait_ge(sg["slots_ready"], b + 1)
                        if b == 0:
                            pool.wait_ge(sg["xp_zeroed"], 16 * (NS // 2))
                    j, k = i // TOPK, i % TOPK
                    g.indirect_dma_start(
                        out=xp_dram, out_offset=bass.IndirectOffsetOnAxis(ap=scat[:, NJ * b + j, k:k + 1], axis=0),
                        in_=h3[:, b % 2, j, :], in_offset=None, bounds_check=SLOTS - 1, oob_is_err=False
                    ).then_inc(scattered[b], 16)
                elif kind == "combine":
                    t, = a
                    if t == 0:
                        for i in range(NG_E):
                            pool.wait_ge(y_stored[i], 16)
                    if t >= 2:
                        pool.wait_ge(sg["combined"], t - 1)
                    for k in range(TOPK):
                        n = (t % 2) * TOPK + k
                        g.indirect_dma_start(
                            out=gbuf[:, n, :], out_offset=None, in_=y_dram,
                            in_offset=bass.IndirectOffsetOnAxis(ap=gath[:, t, k:k + 1], axis=0),
                            bounds_check=E * XR - 1, oob_is_err=False).then_inc(gathered[n], 16)


def shape_constants():
    import numpy as np

    c = np.zeros((P, NCONST), np.float32)
    i = np.arange(P)
    c[:, C_ID:C_ID + P] = np.eye(P)
    c[:, C_MASK:C_MASK + P] = np.where(i[None, :] > i[:, None], -1e30, 0.0)
    c[:, C_TRI:C_TRI + P] = i[:, None] < i[None, :]
    freq = (1.0 / np.float32(10000.0) ** (np.arange(0, DR, 2, dtype=np.float32) / np.float32(DR))).astype(np.float32)
    for j in range(NJ):
        angle = (np.arange(P, dtype=np.float32) + np.float32(j * P))[:, None] * freq[None, :]
        cos, sin = np.cos(angle).astype(np.float32), np.sin(angle).astype(np.float32)
        o = j * DR
        c[:, C_COS + o:C_COS + o + DR] = np.concatenate([cos, cos], 1)
        c[:, C_SIN + o:C_SIN + o + DR] = np.concatenate([sin, -sin], 1)
    c[:, C_I32:C_I32 + E] = np.arange(E)
    c[:, C_I8:C_I8 + NG] = np.arange(NG)
    c[:, C_SLOT0:C_SLOT0 + E] = np.arange(E) * CAP
    return c


_INS = ['x', 'fside_BxS2xS2_0', 'ctx_1024', 'L0_attn_w_kv_a', 'L0_attn_q_a_gamma', 'L0_attn_w_qb',
        'L0_attn_kv_a_gamma', 'L0_attn_w_kvb', 'L0_attn_w_o', 'L0_ffn_router_w', 'L0_ffn_e_bias', 'L0_ffn_W_gate',
        'L0_ffn_W_up', 'L0_ffn_W_down', 'L0_ffn_shared_gate', 'L0_ffn_shared_up', 'L0_ffn_shared_down']


def kernel(**inputs):
    import numpy as _np
    import concourse.bacc as _bacc
    from concourse import mybir as _mybir
    from concourse.bass_utils import run_bass_kernel_spmd as _run

    nc = _bacc.Bacc("TRN2", target_bir_lowering=False, num_devices=1)
    arrays, args = {}, []
    given = {name: _np.ascontiguousarray(inputs[name]) for name in _INS}
    given["shape_constants"] = shape_constants()
    for name, a in given.items():
        arrays[f"in_{name}_dram"] = a
        args.append(nc.dram_tensor(f"in_{name}_dram", a.shape, _mybir.dt.from_np(a.dtype), kind="ExternalInput").ap())
    args.append(nc.dram_tensor("out_0_dram", (B, S, D), F32, kind="ExternalOutput").ap())
    decoder_layer(nc, *args)
    r = _run(nc, [arrays], core_ids=[0])
    return r.results[0]["out_0_dram"]
```

```python
from contextlib import ExitStack

import concourse.bass as bass
from concourse import mybir

ALU = mybir.AluOpType
ACT = mybir.ActivationFunctionType
AX = mybir.AxisListType
F32 = mybir.dt.float32
BF16 = mybir.dt.bfloat16
U32 = mybir.dt.uint32

P = 128
B, S, D = 4, 256, 256
NT = B * S // P
NJ = S // P
KD = D // P
NH, DN, DR, DV, QL, KL = 16, 128, 64, 128, 192, 64
DQK = KL + DR
HC = 4
GH = 4
NHU = B * NH
E, TOPK, NG, TKG = 32, 4, 8, 3
EG = E // NG
CAP = 40
SLOTS = E * CAP
NS = SLOTS // P
XG = 4
NG_E = E // XG
XR = 64
NPAIR = E // 2
W_TOK, W_WT, W_EX = D, D + 1, D + 1 + TOPK
XW = D + 1 + 2 * TOPK
NZ = 10
MIXED = (5, 6, 7)
FINISH = ("combine", 0), ("mix", 5), ("combine", 1), ("mix", 6), ("combine", 2), ("combine", 3), ("mix", 7), (
    "combine", 4)
I = 128
WE = 2 * KD * I + D
SM_SCALE = 1.0 / float(DN + DR) ** 0.5
EPS_LN, EPS_RMS, EPS_Q, QMAX = 1e-5, 1e-6, 1e-6, 127.0
ROUND = 12582912.0
NOSLOT = 4096.0
BANK_S, BANK_PT, BANK_O, BANK_Q, BANK_W = 0, 2, 3, 4, 5
NBANK = 8
PT_DVE = 0

C_ID, C_MASK, C_TRI, C_COS, C_SIN, C_I32, C_I8, C_SLOT0 = 0, 128, 256, 384, 512, 640, 672, 680
C_TOKEN = 712
NCONST = C_TOKEN + NT
C_EXPERT, C_MIXED = NCONST, NCONST + NPAIR
NLATE = NPAIR + len(MIXED) * P

SLOTS_A, SLOTS_B, SLOTS_C = 9, 10, 5
NHOME = SLOTS_A + SLOTS_B + SLOTS_C


CROSS_AND_ROUTE = (
    ("x_stats", 0), ("x_norm", 2), ("x_T", 4), ("x_smooth", 2), ("x_scale", 1), ("x_back", 4),
    ("x_qscale", 1), ("x_round", 2), ("x_qT", 4), ("x_mm", 3), ("x_tanh", 1), ("x_gate", 1), ("x_smooth2", 2),
    ("x_scale2", 1), ("x_back2", 4), ("x_qscale2", 1), ("x_round2", 2), ("x_qT2", 4), ("x_mm2", 3),
    ("r_stats", 1), ("r_norm", 2), ("r_T", 4), ("r_logit", 3), ("r_groups", 1), ("r_best", 0),
    ("r_choose", 1), ("r_weights", 2), ("r_pos", 4), ("r_slots", 1)) + tuple((f"scatter{i}", 4) for i in range(NJ * TOPK))


EVEN_SLOT = ("scores", 0, "norm", 1, "q", "probsT", 2, "qT", 3)
ODD_SLOT = ("norm", "scores", "rope", 0, "probsT", 1, "pv", 2, 3)
Y_AT, WX_AT, WX_FIRST = 19, 55, 11
PREP_AT = (5, 12)
FRONT_AT, FRONT_GAPS, FRONT_NEXT = (6, 36, 50), (0, 2, 5, 8), 4


FILL = (
    ("x_stats", ("r_groups", 2)), ("x_norm", ("r_best", 2)), ("x_T", ("r_choose", 2)),
    ("x_scale", ("s_gate", 0)), ("x_scale", ("s_up", 0)), ("x_scale", ("r_weights", 2)),
    ("x_back", ("s_silu", 0)), ("x_back", ("s_mul", 0)), ("x_back", ("r_pos", 2)), ("x_qscale", ("s_down", 0)),
    ("x_qscale", ("s_gate", 1)), ("x_qscale", ("r_slots", 2)), ("x_round", ("s_silu", 1)),
    ("x_tanh", ("s_up", 1)), ("x_tanh", ("s_gate", 2)), ("x_smooth2", ("s_add", 0)), ("x_scale2", ("s_mul", 1)),
    ("x_back2", ("s_down", 1)), ("x_round2", ("s_silu", 2)), ("x_round2", ("s_add", 1)), ("x_mm2", ("s_up", 2)),
    ("r_norm", ("s_mul", 2)), ("r_logit", ("s_down", 2)), ("r_logit", ("s_gate", 3)), ("r_pos", ("s_up", 3)),
    ("r_slots", ("s_add", 2)), ("r_slots", ("s_silu", 3)), ("r_slots", ("s_down", 3)),
    ("r_slots", ("s_mul", 3)), ("r_slots", ("s_add", 3)))
SCATTER_AFTER = ("x_qscale", "x_round", "x_qT", "x_mm", "x_smooth2", "x_scale2", "x_back2", "x_qscale2")


def plan():
    places = [[] for _ in range(4 * NHU + 200)]

    steps = [("setup",), ("ln1_stats", 0), ("ln1_norm", 0), ("hT", 0), ("hT", 1), ("fused", 0), ("fused", 1),
             ("prepT", 0), ("latents", 0), ("prepT", 1), ("latents", 1), ("latT", 0), ("prepM", 0),
             ("prepT", 2), ("latT", 1), ("prepT", 3), ("prepM", 1), ("prepT", 4), ("prepT", 5), ("q", 0, 0),
             ("rope", 0, 0), ("q", 1, 0), ("prepM", 2), ("rope", 1, 0), ("prepT", 6), ("prepT", 7), ("qT", 0, 0),
             ("prepM", 3), ("prepT", 8), ("ln1_stats", 1), ("prepT", 9), ("qT", 1, 0), ("q", 0, 1), ("ln1_norm", 1),
             ("prepM", 4), ("prepT", 10), ("rope", 0, 1), ("prepT", 11)]
    places[0] += [("prepM", 5)]
    for p, at in zip((6, 7), PREP_AT):
        places[at].append(("prepT", 2 * p))
        places[at + 1].append(("prepT", 2 * p + 1))
        places[at + 3].append(("prepM", p))
    for b, at in zip((1, 2, 3), FRONT_AT):
        if b > 1:
            places[at - 4].append(("ln1_stats", b))
            places[at - 2].append(("ln1_norm", b))
        for t in (2 * b, 2 * b + 1):
            for kind, gap in zip(("hT", "fused", "latents", "latT"), FRONT_GAPS):
                places[at + gap].append((kind, t))
            at += FRONT_NEXT

    units = [(NJ * b + j, c) for b in range(B) for c in range(NH // HC) for j in range(NJ)]
    ahead = 3

    def late(kind, b):
        return ("scatter", b, int(kind[7:])) if kind.startswith("scatter") else (kind, b)

    for b in range(B):
        places[4 * NH * b + (WX_AT if b else WX_FIRST)].append(("wx", b))
        if b == B - 1:
            break
        at = 4 * NH * (b + 1) + Y_AT
        places[at].append(("y_first", 2 * b))
        places[at].append(("y_last", 2 * b))
        places[at + 2].append(("y_add", 2 * b))
        places[at + 4].append(("y_first", 2 * b + 1))
        places[at + 4].append(("y_last", 2 * b + 1))
        places[at + 5].append(("y_add", 2 * b + 1))
        at += 6
        for kind, gap in CROSS_AND_ROUTE:
            at += gap if b < B - 2 else min(gap, 3)
            if b == B - 2 and kind.startswith("scatter"):
                break
            places[at].append(late(kind, b))
    places[4 * 5 + 1].append(("rwT",))
    for i in range(3):
        places[4 * (6 + i) + 1].append(("shT", i))

    steps += [("attention",)]
    for hn in range(NHU):
        u = hn // 2 + ahead
        for what in ODD_SLOT if hn % 2 else EVEN_SLOT:
            if what in (0, 1, 2, 3):
                steps += places[4 * hn + what]
            elif what == "scores":
                steps.append(("scores", hn))
            elif what == "norm" and hn >= 1:
                steps.append(("norm", hn - 1))
            elif what == "probsT" and hn >= 3:
                steps.append(("probsT", hn - 3))
            elif what == "pv" and hn >= 5:
                steps.append(("pv", (hn - 5) // 2))
            elif what in ("q", "rope") and u < len(units):
                steps.append((what,) + units[u])
            elif what == "qT" and u <= len(units):
                steps.append(("qT",) + units[u - 1])
    b = B - 1
    left = [step for place in places[4 * NHU:] for step in place]
    n = left.index(("r_groups", b - 1)) if ("r_groups", b - 1) in left else 0
    steps += [("norm", NHU - 1), ("probsT", NHU - 3), ("y_first", 2 * b), ("probsT", NHU - 2),
              ("pv", NHU // 2 - 2), ("y_first", 2 * b + 1), ("probsT", NHU - 1)]
    steps += [step for step in left[:n] if step[0] != "r_logit"] + [("pv", NHU // 2 - 1), ("tail",)]
    steps += [step for step in left[:n] if step[0] == "r_logit"]
    steps += [("y_last", 2 * b), ("y_last", 2 * b + 1),
              ("y_add", 2 * b), ("y_add", 2 * b + 1)]
    left = left[n:]
    scatters = [("scatter", b - 1, i) for i in range(NJ * TOPK)]
    for kind, _ in CROSS_AND_ROUTE:
        steps.append(late(kind, b))
        n = SCATTER_AFTER.count(kind)
        steps += scatters[:n]
        scatters = scatters[n:]
        steps += [step for after, step in FILL if after == kind and (step[0][0] == "s" or step in left)]
        left = [step for step in left if (kind, step) not in FILL]
    assert not scatters and not left
    turned = 0
    for g in range(NG_E + 2):
        while turned < min(-(-((g + 2) * XG * CAP + XR - CAP) // (2 * P)), NS // 2):
            steps.append(("xpT", turned))
            turned += 1
        if g < NG_E:
            steps.append(("gate_up", g))
        if 0 < g <= NG_E:
            steps.append(("hidT", g - 1))
        if g > 1:
            steps.append(("down", g - 2))
        if g == 2:
            steps.append(("slot_weights",))
        if g >= 6:
            steps += [("onehot", i) for i in range((g - 6) * 4, NPAIR if g == NG_E + 1 else (g - 5) * 4)]
    steps += [("gather", t) for t in range(NT) if t not in MIXED]
    steps += FINISH
    return steps


ITEMS = {
    "hT": [("hT", 1)], "fused": [("fused", 1)], "latT": [("latT", 1)],
    "prepT": [("prepT", 1)], "prepM": [("prepM", 1)],
    "q": [("q", 1)], "qT": [("qT", 1)], "y_first": [("y", 1)],
    "wx": [("fsT", 1), ("cxT", 1)], "rwT": [("rwT", 1)], "shT": [("shT", 1)],
    "x_T": [("xT", 1)], "x_back": [("xs", 1), ("ws", 1)], "x_qT": [("xqT", 1), ("xb", 1)],
    "x_mm": [("h1", 1)], "x_back2": [("as", 1)], "x_qT2": [("aqT", 1), ("wb", 1)], "x_mm2": [("h2", 1)],
    "r_T": [("h3T", 1)], "r_logit": [("logit", 1)], "r_pos": [("pos", 1)],
    "s_gate": [("sg", 1)], "s_up": [("su", 1)], "s_down": [("sd", 1)],
    "xpT": [("xpT", 1)], "gate_up": [("gu", 1)], "hidT": [("hidT", 1)], "down": [("dn", 1)],
    "mix": [("mix", 1)],
}


class Ring:

    def __init__(self, steps):
        self.at = {}
        filled, emptied, n = [0] * NBANK, [0] * NBANK, 0
        ring = list(range(NBANK))
        self.before_attention = None
        for step in steps:
            if step[0] == "attention":
                self.before_attention = list(emptied)
                ring = list(range(BANK_W, NBANK))
            elif step[0] == "tail":
                ring = list(range(NBANK))
            for name, empties in ITEMS.get(step[0], []):
                if name == "q" and self.before_attention:
                    k = BANK_Q
                else:
                    k = ring[n % len(ring)]
                    n += 1
                self.at[(name,) + step[1:]] = (k, emptied[k], filled[k] + 1, emptied[k] + empties)
                filled[k] += 1
                emptied[k] += empties


def decoder_layer(nc, x, fside, ctx_w, w_kv_a, q_gamma, w_qb, kv_gamma, w_kvb, w_o, router_w, e_bias,
                  w_gate, w_up, w_down, sh_gate, sh_up, sh_down, consts, out):
    steps = plan()
    ring = Ring(steps)
    xp_dram = nc.dram_tensor("expert_rows", (SLOTS, XW), F32, kind="Internal").ap()
    y_dram = nc.dram_tensor("expert_out", (E * XR, D), F32, kind="Internal").ap()

    with ExitStack() as stack:
        def sb(name, shape, dt=F32):
            return stack.enter_context(nc.sbuf_tensor(name, shape, dt))

        def sem(name):
            return stack.enter_context(nc.semaphore(name))

        psum = stack.enter_context(nc.psum_tensor("psum", [P, NBANK, 512], F32))
        ps_pt = psum[:, BANK_PT, :]
        ps_o = psum[:, BANK_O, :]

        cst = sb("consts", [P, NCONST])
        id_bf = sb("ident_bf16", [P, P], BF16)
        mask_bf = sb("mask_bf16", [P, P], BF16)
        tri_bf = sb("tri_bf16", [P, P], BF16)
        ones_bf = sb("ones_bf16", [P, P], BF16)
        xres = sb("x_residual", [P, NT, D])
        neg_half = sb("neg_half", [P, 1])
        pos_half = sb("pos_half", [P, 1])
        gam_q = sb("gamma_q", [P, QL])
        gam_kv = sb("gamma_kv", [P, KL])
        bias_e = sb("e_bias", [P, E])
        w_mo = sb("w_folded_out", [P, NH // 2, D])
        fs = sb("fside", [P, B, 2, D])
        cx = sb("ctx", [P, B, 2, I])
        rwT = sb("router_wT", [P, KD, E])
        shT = sb("shared_wT", [P, 3, KD, D])
        reg_a = sb("region_a", [P, 6912])
        reg_b = sb("region_b", [P, 8192])
        reg_c = sb("region_c", [P, 4096])
        reg_g = sb("region_g", [P, 4096])
        reg_h = sb("region_h", [P, 4096])
        wq0 = reg_a[:, 0:NH * DN].rearrange("p (h m) -> p h m", h=NH)
        wkq = reg_a[:, 2048:6144].rearrange("p (h m) -> p h m", h=NH)
        wo = reg_b[:, 0:4096].rearrange("p (h d) -> p h d", h=NH)
        qT = reg_b[:, 4096:6144].rearrange("p (c h t) -> p c h t", c=2, h=HC)
        wf0 = reg_c[:, 0:2048].rearrange("p (h m) -> p h m", h=NH)
        wf1 = reg_c[0:64, 2048:4096].rearrange("p (h m) -> p h m", h=NH)
        oT = reg_g[:, :].rearrange("p (b i t) -> p b i t", b=2, i=NH // 2)
        xpT = reg_g[:, 0:KD * (SLOTS + XR - CAP)].rearrange("p (k s) -> p k s", k=KD)
        kv = reg_h[:, 0:1024].rearrange("p (t m) -> p t m", t=NT)
        kT = reg_h[:, 1024:2048].rearrange("p (b m) -> p b m", b=B)
        qn0 = reg_h[:, 2048:3072].rearrange("p (t m) -> p t m", t=NT)
        qn1 = reg_h[0:64, 3072:4096].rearrange("p (t m) -> p t m", t=NT)
        rows = reg_h[:, 0:NS * D].rearrange("p (i d) -> p i d", i=NS)

        def ybuf(g):
            o = (NS * D + g * 2 * D) % (NG_E * 2 * D)
            return reg_h[:, o:o + 2 * D]

        def home(e):
            s = e % NHOME
            if s < SLOTS_A:
                r, o = reg_a, s * WE
            elif s < SLOTS_A + SLOTS_B:
                r, o = reg_b, (s - SLOTS_A) * WE
            else:
                r, o = reg_c, (s - SLOTS_A - SLOTS_B) * WE
            return r[:, o:o + WE]

        def gate_up_of(e):
            return home(e)[:, 0:2 * KD * I].rearrange("p (k m) -> p k m", k=KD)

        def down_of(e):
            return home(e)[:, 2 * KD * I:WE]

        reg_t = sb("region_t", [P, 3072])
        reg_r = sb("region_r", [P, 2048])
        wkva = reg_b[:, 6144:6784].rearrange("p (k n) -> p k n", k=KD)
        probs = reg_t[:, 0:1536].rearrange("p (u q) -> p u q", u=4)
        probsT = reg_t[:, 1536:3072].rearrange("p (u q) -> p u q", u=4)
        es = reg_t[:, 0:1024].rearrange("p (u q) -> p u q", u=2)
        act_s = reg_t[:, 1024:2048].rearrange("p (u k t) -> p u k t", u=2, k=2)
        th = reg_t[:, 2048:3072].rearrange("p (u q) -> p u q", u=4)
        hE = reg_r[:, 0:512].rearrange("p (u q) -> p u q", u=2)
        hET = reg_r[:, 512:1024].rearrange("p (u q) -> p u q", u=2)
        hn_f = reg_r[:, 0:512].rearrange("p (j d) -> p j d", j=NJ)
        hT_f = reg_r[:, 512:1024].rearrange("p (i m) -> p i m", i=2)
        wT = reg_g[:, 2048:3328].rearrange("p (i m) -> p i m", i=4)
        fused_s = reg_r[:, 1024:1344]
        sq = reg_r[:, 1408:1664]
        qn = reg_r[:, 1664:1664 + 2 * QL].rearrange("p (i m) -> p i m", i=2)
        qa = reg_r[:, 0:1024].rearrange("p (i d) -> p i d", i=4)
        gu = reg_r[:, 1024:2048].rearrange("p (i d) -> p i d", i=4)
        late = reg_r[:, 1024:1024 + NLATE]
        meta = reg_r[:, 1024 + NLATE:1024 + NLATE + 9 * NPAIR].rearrange("p (i m) -> p i m", i=NPAIR)
        wsel = reg_r[:, 1600:1600 + 5 * NPAIR].rearrange("p (m i) -> p m i", m=5)
        onehot = reg_b[:, 2048:8192].rearrange("p (i t) -> p i t", i=NPAIR)
        zeros = reg_g[:, 3584:4096]
        rw = reg_g[:, 3328:3584]

        ssq = sb("sum_squares", [P, NT, 2])
        rrms = sb("rrms", [P, NT, 2])
        weps = sb("rms_eps", [P, NT, 2])
        kr = sb("k_rope_tmp", [P, 2, DR])
        qs = sb("q_chunk", [P, 2, HC * DQK])
        qr = sb("q_rope_tmp", [P, 2, HC * DR])
        nmax = sb("neg_max", [P, NHU, 2])
        sums = sb("prob_sums", [P, NHU, NJ])
        rsum = sb("prob_rsums", [P, NHU, NJ])
        stats = sb("bn_stats", [P, 2, 6])
        mv = sb("mean_var", [P, 3, NT, 2])
        rstd = sb("rstd", [P, 3, NT])
        vtmp = sb("var_eps", [P, 3, NT])
        h2 = sb("h_cross", [P, NJ, D])
        fsT = sb("fsideT", [P, 512])
        cxT = sb("ctxT", [P, 256])
        xsT = sb("x_scaledT", [P, 512])
        wsT = sb("w_scaledT", [P, 512])
        rden = sb("rden", [P, B, 3])
        sm = sb("smooth", [P, B, 36])
        qb = sb("q_bf16", [P, 4, D], BF16)
        qTs = sb("qT_bf16", [P, 4, D], BF16)
        sbc = sb("scale_rows", [P, 2, D])
        h3 = sb("h_moe", [P, 2, NJ, XW])
        h3T = sb("h_moeT", [P, B, KD, S])
        sc = sb("scores", [P, 3, NJ * E])
        reg_rt = sb("route", [P, 12 * NJ * E])
        rt = reg_rt[:, :].rearrange("p (i m) -> p i m", i=12)
        top = sb("top", [P, NJ, 8])
        topi = sb("top_index", [P, NJ, 8], U32)
        tif = sb("top_index_f32", [P, NJ, TOPK])
        oh = reg_rt[:, 6 * NJ * E:6 * NJ * E + 256]
        ohp = reg_rt[:, 2 * NJ * E:2 * NJ * E + 256]
        chosen = sb("chosen", [P, NT, E], BF16)
        slotf = sb("slot_f32", [P, 4, NJ * TOPK])
        scat = sb("slot_scatter", [P, NT, TOPK], U32)
        gath = sb("slot_gather", [P, NT, TOPK], U32)
        wtok = sb("token_weights", [P, NT, TOPK])
        h3T_flat = h3T[:].rearrange("p b k t -> p (b k t)")
        shw = h3T_flat[:, 0:1536].rearrange("p (i o d) -> p i o d", i=3, o=2)
        gbuf = reg_b[:, 0:2048].rearrange("p (n d) -> p n d", n=8)

        ld = {k: sem("ld_" + k) for k in ("consts", "x0", "x1", "x2", "x3", "wkva", "gam", "fs", "cx", "rw", "sh", "bias", "late", "meta")}
        ld_fold = [sem(f"ld_fold{i}") for i in range(2)]
        ld_rope_cols = [sem(f"ld_rope_cols{i}") for i in range(2)]
        ld_experts = [sem(f"ld_experts{g}") for g in range(E // XG)]
        ld_rows = [sem(f"ld_rows{i}") for i in range(NS // 2)]
        bank_filled = [sem(f"bank_filled{k}") for k in range(NBANK)]
        bank_emptied = [sem(f"bank_emptied{k}") for k in range(NBANK)]
        names = """consts_ready halves_ready zeros_ready padding_ready meta_zeroed onehot_ready
            ln_stats ln_rstd h_ready squares_ready rms_ready lat_ready
            scores_ready max_ready exp_done probs_normed probsT_done probsT_copied heads_done heads_copied
            rope_parts rope_added ratio_ready smooth_root smooth_ready scaledT_w inv_ready q_ready gate_tanh
            ratio2_ready smooth_root2 smooth_ready2 scaledT_a scaledT_c inv2_ready q2_ready
            chosen_ready weights_ready slots_ready gather_ready shared_tanh xp_zeroed expert_tanh combined out_stored
            dve_chain pool_chain""".split()
        sg = {n: sem(n) for n in names}
        scattered = [sem(f"scattered{b}") for b in range(B)]
        y_stored = [sem(f"y_stored{g}") for g in range(NG_E)]
        gathered = [sem(f"gathered{i}") for i in range(8)]
        block = stack.enter_context(nc.Block())

        def c_(o, n):
            return cst[:, o:o + n]

        ident = c_(C_ID, P)

        def bank(item):
            return psum[:, ring.at[item][0], :]

        def wait_empty(eng, item):
            k, before, _, _ = ring.at[item]
            if before:
                eng.wait_ge(bank_emptied[k], before)

        def wait_filled(eng, item):
            k, _, filled, _ = ring.at[item]
            eng.wait_ge(bank_filled[k], filled)

        def wait_emptied(eng, item):
            k, _, _, after = ring.at[item]
            eng.wait_ge(bank_emptied[k], after)

        def fills(ins, item):
            ins.then_inc(bank_filled[ring.at[item][0]], 1)

        def empties(ins, item):
            ins.then_inc(bank_emptied[ring.at[item][0]], 1)

        step_no = {}
        for step in steps:
            kind = "ln" if step[0] in ("ln1_stats", "x_stats", "r_stats") else step[0]
            step_no[step] = sum(1 for k in step_no.values() if k[0] == kind), kind
            step_no[step] = (kind, step_no[step][0])

        def nth(*step):
            return step_no[step][1]

        q_order = [step for step in steps if step[0] == "qT"]

        @block.sync
        def _(sp):
            def load_expert(e):
                s = ld_experts[e // XG]
                w = gate_up_of(e)
                sp.dma_start(w[:, :, 0:I], w_gate[e].rearrange("(k p) i -> p k i", p=P)).then_inc(s, 16)
                sp.dma_start(w[:, :, I:], w_up[e].rearrange("(k p) i -> p k i", p=P)).then_inc(s, 16)
                sp.dma_start(down_of(e), w_down[e]).then_inc(s, 16)

            xt = x.rearrange("b (j p) d -> b p j d", p=P)
            sp.dma_start(xres[:, 0:2, :], xt[0]).then_inc(ld["x0"], 16)
            sp.dma_start(cst[:], consts[:, 0:NCONST]).then_inc(ld["consts"], 16)
            sp.dma_start(wkva[:], w_kv_a.rearrange("(k p) n -> p k n", p=P)).then_inc(ld["wkva"], 16)
            sp.dma_start(gam_q[:], q_gamma.partition_broadcast(P)).then_inc(ld["gam"], 16)
            sp.dma_start(gam_kv[:], kv_gamma.partition_broadcast(P)).then_inc(ld["gam"], 16)
            wqh = w_qb.rearrange("p (h m) -> p h m", h=NH)
            kvh = w_kvb.rearrange("p (h m) -> p h m", h=NH)
            woh = w_o.rearrange("(h p) d -> p h d", p=P)
            for i in range(2):
                hs = slice(i * NH // 2, (i + 1) * NH // 2)
                sp.dma_start(wkq[0:KL, hs], kvh[:, hs]).then_inc(ld_fold[i], 16)
                sp.dma_start(wq0[:, hs], wqh[0:P, hs, 0:DN]).then_inc(ld_fold[i], 16)
                sp.dma_start(wkq[KL:P, hs, 0:DN], wqh[P:QL, hs, 0:DN]).then_inc(ld_fold[i], 16)
                sp.dma_start(wo[:, hs], woh[:, hs]).then_inc(ld_fold[i], 16)
                sp.dma_start(wf0[:, hs, KL:], wqh[0:P, hs, DN:]).then_inc(ld_rope_cols[i], 16)
                sp.dma_start(wf1[:, hs, KL:], wqh[P:QL, hs, DN:]).then_inc(ld_rope_cols[i], 16)
            sp.dma_start(xres[:, 2:4, :], xt[1]).then_inc(ld["x1"], 16)
            sp.dma_start(xres[:, 4:6, :], xt[2]).then_inc(ld["x2"], 16)
            sp.dma_start(xres[:, 6:8, :], xt[3]).then_inc(ld["x3"], 16)
            sp.dma_start(fs[:], fside.rearrange("b (o p) d -> p b o d", p=P)).then_inc(ld["fs"], 16)
            sp.dma_start(cx[:], ctx_w.rearrange("b (o p) i -> p b o i", p=P)).then_inc(ld["cx"], 16)
            sp.dma_start(rw[0:E, :], router_w).then_inc(ld["rw"], 16)
            sp.dma_start(bias_e[:], e_bias.partition_broadcast(P)).then_inc(ld["bias"], 16)
            for i, w in enumerate((sh_gate, sh_up, sh_down)):
                sp.dma_start(shw[:, i], w.rearrange("(o p) d -> p o d", p=P)).then_inc(ld["sh"], 16)
            sp.wait_ge(sg["zeros_ready"], 1)
            xz = xp_dram.rearrange("(p a) d -> p (a d)", p=P)
            n = SLOTS * XW // P // NZ
            for i in range(NZ):
                sp.dma_start(xz[:, n * i:n * (i + 1)], zeros[:, 0:n]).then_inc(sg["xp_zeroed"], 16)
            for p in range(NH // 2):
                wait_emptied(sp, ("prepM", p))
            for e in range(SLOTS_A + 5):
                load_expert(e)
            wait_filled(sp, ("fused", NT - 1))
            for e in range(SLOTS_A + 8, SLOTS_A + SLOTS_B):
                load_expert(e)
            wait_filled(sp, q_order[-1])
            for e in range(SLOTS_A + SLOTS_B, NHOME):
                load_expert(e)
            sp.wait_ge(sg["scores_ready"], NHU)
            for e in range(SLOTS_A + 5, SLOTS_A + 8):
                load_expert(e)
            wait_emptied(sp, ("h2", B - 1))
            sp.wait_ge(sg["meta_zeroed"], 1)
            sp.dma_start(late, consts[:, NCONST:NCONST + NLATE]).then_inc(ld["late"], 16)
            for b in range(B):
                sp.wait_ge(scattered[b], 16 * NJ * TOPK)
            for i in range(NS // 2):
                sp.dma_start(rows[:, 2 * i:2 * i + 2, :],
                             xp_dram.rearrange("(i p) d -> p i d", p=P)[:, 2 * i:2 * i + 2, 0:D]
                             ).then_inc(ld_rows[i], 16)
            slots = xp_dram.rearrange("(i two p) d -> two p i d", two=2, p=CAP)
            for side in range(2):
                sp.dma_start(meta[side * XR:side * XR + CAP], slots[side, :, :, W_TOK:]).then_inc(ld["meta"], 16)
            yv = y_dram.rearrange("(i p) d -> p i d", p=P)

            def store_outputs(i):
                wait_emptied(sp, ("dn", i))
                sp.dma_start(yv[:, 2 * i:2 * i + 2, :], ybuf(i).rearrange("p (i d) -> p i d", i=2)
                             ).then_inc(y_stored[i], 16)

            for e in range(NHOME, E):
                if (e - NHOME) % XG == 0:
                    wait_filled(sp, ("dn", (e - NHOME) // XG))
                load_expert(e)
                if (e - NHOME) % XG == XG - 1:
                    store_outputs((e - NHOME) // XG)
            for i in range(2, NG_E):
                store_outputs(i)
            ov = out.rearrange("b (j p) d -> p (b j) d", p=P)
            for i, (_, t) in enumerate(FINISH):
                sp.wait_ge(sg["combined"], i + 1)
                sp.dma_start(ov[:, t, :], xres[:, t, :]).then_inc(sg["out_stored"], 16)
            sp.wait_ge(sg["out_stored"], 16 * NT)

        @block.tensor
        def _(pe):
            def mm(out_, lhsT, rhs, first=True, last=True):
                return nc.tensor.matmul(out_, lhsT, rhs, start=first, stop=last)

            def mm_halves(out_, lhsT, rhs, first=True, last=True):
                h = P // 2
                mm(out_[0:h], lhsT[:, 0:h], rhs, first, last)
                return mm(out_[h:P], lhsT[:, h:P], rhs, first, last)

            def turn(out_, in_, idn=None):
                return nc.tensor.transpose(out_, in_, ident if idn is None else idn)

            def bf(item):
                return bank(item).bitcast(BF16)

            for step in steps:
                kind, a = step[0], step[1:]
                if kind == "setup":
                    pe.wait_ge(ld["consts"], 16)
                elif kind == "hT":
                    t, = a
                    pe.wait_ge(sg["h_ready"], nth("ln1_stats", t // NJ) + 1)
                    wait_empty(pe, step)
                    for k in range(KD):
                        last = turn(bank(step)[:, k * P:(k + 1) * P], hn_f[:, t % 2, k * P:(k + 1) * P])
                    fills(last, step)
                elif kind == "fused":
                    t, = a
                    if t == 0:
                        pe.wait_ge(ld["wkva"], 16)
                    wait_emptied(pe, ("hT", t))
                    wait_empty(pe, step)
                    for k in range(KD):
                        last = mm(bank(step)[:, 0:QL + KL + DR], hT_f[:, t % 2, k * P:(k + 1) * P], wkva[:, k, :],
                                  k == 0, k == KD - 1)
                    fills(last, step)
                elif kind == "latT":
                    t, = a
                    pe.wait_ge(sg["lat_ready"], t + 1)
                    wait_empty(pe, step)
                    turn(bank(step)[:, 0:P], qn[:, t % 2, 0:P])
                    turn(bank(step)[:, P:2 * P], kv[:, t, :])
                    fills(turn(bank(step)[0:64, 2 * P:3 * P], qn[:, t % 2, P:QL]), step)
                elif kind == "prepT":
                    h, = a
                    if h % (NH // 2) == 0:
                        pe.wait_ge(ld_fold[h // (NH // 2)], 16 * 4)
                    wait_empty(pe, step)
                    turn(bank(step)[:, 0:P], wq0[:, h, :])
                    turn(bank(step)[:, P:2 * P], wkq[:, h, 0:DN])
                    fills(turn(bank(step)[:, 256:320], wkq[0:KL, h, DN:], ident[0:KL, 0:KL]), step)
                elif kind == "prepM":
                    p, = a
                    wait_emptied(pe, ("prepT", 2 * p))
                    wait_emptied(pe, ("prepT", 2 * p + 1))
                    wait_empty(pe, step)
                    for i in range(2):
                        w = wT[:, (2 * p + i) % 4, :]
                        wkT = w[:, P:P + KL]
                        mm_halves(bank(step)[:, i * KL:(i + 1) * KL], w[:, 0:P], wkT)
                        mm(bank(step)[0:64, 128 + i * KL:128 + (i + 1) * KL], w[:, P + KL:2 * P], wkT)
                    for i in range(2):
                        last = mm(bank(step)[i * KL:(i + 1) * KL, 256:512], wT[:, (2 * p + i) % 4, 256:320], wo[:, 2 * p + i, :])
                    fills(last, step)
                elif kind == "q":
                    t, c = a
                    if t < NJ:
                        for p in range(HC * c // 2, HC * (c + 1) // 2):
                            wait_emptied(pe, ("prepM", p))
                        pe.wait_ge(ld_rope_cols[HC * c // (NH // 2)], 32)
                    wait_emptied(pe, ("latT", t))
                    wait_empty(pe, step)
                    mm(bank(step), qn0[:, t, :], wf0[:, HC * c:HC * (c + 1), :], True, False)
                    fills(mm(bank(step), qn1[:, t, :], wf1[:, HC * c:HC * (c + 1), :], False, True), step)
                elif kind == "qT":
                    u = nth(*step)
                    pe.wait_ge(sg["rope_added"], u + 1)
                    wait_empty(pe, step)
                    for i in range(HC):
                        last = turn(bank(step)[:, i * P:(i + 1) * P], qs[:, u % 2, i * P:(i + 1) * P])
                    fills(last, step)
                elif kind == "attention":
                    for k in range(BANK_Q):
                        pe.wait_ge(bank_emptied[k], ring.before_attention[k])
                    pe.wait_ge(sg["consts_ready"], 1)
                elif kind == "scores":
                    hn, = a
                    b, n = hn // NH, hn % NH
                    if n == 0:
                        for j in range(NJ):
                            wait_emptied(pe, ("latT", NJ * b + j))
                    if n % HC == 0:
                        for j in range(NJ):
                            wait_emptied(pe, ("qT", NJ * b + j, n // HC))
                    if hn >= 2:
                        pe.wait_ge(sg["exp_done"], hn - 1)
                    o = psum[:, BANK_S + hn % 2, :]
                    q = qT[:, (hn // HC) % 2, n % HC, :]
                    mm(o[:, 0:P], id_bf[:], mask_bf[:], True, False)
                    mm(o[0:64, 0:64], q[:, 0:64], kT[:, b, 0:64], False, True)
                    mm(o[64:P, 0:P], q[:, 64:P], kT[:, b, 0:P], False, True)
                    mm(o[:, P:3 * P], q[:, P:2 * P], kT[:, b, :], True, False)
                    mm(o[:, 2 * P:3 * P], id_bf[:], mask_bf[:], False, True).then_inc(sg["scores_ready"], 1)
                elif kind == "probsT":
                    hn, = a
                    pe.wait_ge(sg["probs_normed"], hn + 1)
                    if hn >= 1:
                        pe.wait_ge(sg["probsT_copied"], hn)
                    for i in range(3):
                        last = turn(ps_pt[:, i * P:(i + 1) * P], probs[:, hn % 4, i * P:(i + 1) * P])
                    last.then_inc(sg["probsT_done"], 1)
                elif kind == "pv":
                    pr, = a
                    b = pr // (NH // 2)
                    pe.wait_ge(sg["probsT_copied"], 2 * pr + 2)
                    if pr % 2 == 0 and pr:
                        pe.wait_ge(sg["heads_copied"], pr // 2)
                    c0 = (pr % 2) * S
                    for i in range(2):
                        mm(ps_o[i * KL:(i + 1) * KL, c0:c0 + S], kv[:, 2 * b, 0:KL],
                           probsT[:, (2 * pr + i) % 4, 0:2 * P], True, False)
                    for i in range(2):
                        last = mm(ps_o[i * KL:(i + 1) * KL, c0 + P:c0 + S], kv[:, 2 * b + 1, 0:KL],
                                  probsT[:, (2 * pr + i) % 4, 2 * P:3 * P], False, True)
                    last.then_inc(sg["heads_done"], 1)
                elif kind == "tail":
                    pe.wait_ge(sg["exp_done"], NHU)
                    pe.wait_ge(sg["probsT_copied"], NHU)
                    pe.wait_ge(sg["heads_copied"], NHU // GH)
                elif kind in ("y_first", "y_last"):
                    t, = a
                    item = ("y", t)
                    n = NH // 2 - 2
                    quads = (NH // GH) * (t // NJ) + (NH // GH - 1 if kind == "y_first" else NH // GH)
                    pe.wait_ge(sg["heads_copied"], quads)
                    if kind == "y_first":
                        wait_empty(pe, item)
                    for i in range(n) if kind == "y_first" else range(n, NH // 2):
                        last = mm(bank(item)[:, 0:D], oT[:, (t // NJ) % 2, i, (t % 2) * P:(t % 2 + 1) * P],
                                  w_mo[:, i, :], i == 0, i == NH // 2 - 1)
                    if kind == "y_last":
                        fills(last, item)
                elif kind == "wx":
                    b, = a
                    item = ("fsT", b)
                    if b == 0:
                        pe.wait_ge(ld["fs"], 16)
                        pe.wait_ge(ld["cx"], 16)
                    wait_empty(pe, item)
                    for k in range(KD):
                        for o in range(2):
                            last = turn(bank(item)[:, k * 256 + o * P:k * 256 + (o + 1) * P],
                                        fs[:, b, o, k * P:(k + 1) * P])
                    fills(last, item)
                    item = ("cxT", b)
                    wait_empty(pe, item)
                    for o in range(2):
                        last = turn(bank(item)[:, o * P:(o + 1) * P], cx[:, b, o, :])
                    fills(last, item)
                elif kind == "rwT":
                    pe.wait_ge(ld["rw"], 16)
                    wait_empty(pe, step)
                    for k in range(KD):
                        last = turn(bank(step)[:, k * E:(k + 1) * E], rw[0:E, k * P:(k + 1) * P], ident[0:E, 0:E])
                    fills(last, step)
                elif kind == "shT":
                    i, = a
                    if i == 0:
                        pe.wait_ge(ld["sh"], 48)
                    wait_empty(pe, step)
                    for k in range(KD):
                        for o in range(2):
                            last = turn(bank(step)[:, k * 256 + o * P:k * 256 + (o + 1) * P],
                                        shw[:, i, o, k * P:(k + 1) * P])
                    fills(last, step)
                elif kind == "x_T":
                    b, = a
                    item = ("xT", b)
                    pe.wait_ge(sg["h_ready"], nth("x_stats", b) + 1)
                    wait_empty(pe, item)
                    for k in range(KD):
                        for j in range(NJ):
                            last = turn(bank(item)[:, k * 256 + j * P:k * 256 + (j + 1) * P],
                                        h2[:, j, k * P:(k + 1) * P])
                    fills(last, item)
                elif kind == "x_back":
                    b, = a
                    for item, src in ((("xs", b), xsT), (("ws", b), wsT)):
                        if item[0] == "xs":
                            wait_emptied(pe, ("xT", b))
                        else:
                            pe.wait_ge(sg["scaledT_w"], b + 1)
                        wait_empty(pe, item)
                        for j in range(NJ):
                            for k in range(KD):
                                last = turn(bank(item)[:, j * 256 + k * P:j * 256 + (k + 1) * P],
                                            src[:, k * 256 + j * P:k * 256 + (j + 1) * P])
                        fills(last, item)
                elif kind == "x_qT":
                    b, = a
                    item = ("xqT", b)
                    pe.wait_ge(sg["q_ready"], b + 1)
                    wait_empty(pe, item)
                    for i in range(4):
                        for k in range(KD):
                            o = (i // 2) * 512 + k * 256 + (i % 2) * P
                            last = turn(bf(item)[:, o:o + P], qb[:, i, k * P:(k + 1) * P], id_bf[:])
                    fills(last, item)
                    item = ("xb", b)
                    wait_empty(pe, item)
                    for j in range(NJ):
                        last = mm_halves(bank(item)[:, j * P:(j + 1) * P],
                                         sm[:, b, 10 + j:11 + j].broadcast_to([P, P]), ident)
                    fills(last, item)
                elif kind == "x_mm":
                    b, = a
                    item = ("h1", b)
                    wait_emptied(pe, ("xqT", b))
                    wait_empty(pe, item)
                    f = qTs[:].rearrange("p a d -> p (a d)")
                    for oh_ in range(2):
                        for k in range(KD):
                            w0 = 512 + k * 256 + oh_ * P
                            last = mm(bank(item)[:, oh_ * 256:(oh_ + 1) * 256], f[:, w0:w0 + P],
                                      f[:, k * 256:(k + 1) * 256], k == 0, k == KD - 1)
                    fills(last, item)
                elif kind == "x_back2":
                    b, = a
                    item = ("as", b)
                    pe.wait_ge(sg["scaledT_a"], b + 1)
                    pe.wait_ge(sg["scaledT_c"], b + 1)
                    wait_empty(pe, item)
                    for i in range(4):
                        src = xsT if i < 2 else wsT
                        last = turn(bank(item)[:, i * P:(i + 1) * P], src[:, (i % 2) * P:(i % 2 + 1) * P])
                    fills(last, item)
                elif kind == "x_qT2":
                    b, = a
                    item = ("aqT", b)
                    pe.wait_ge(sg["q2_ready"], b + 1)
                    wait_empty(pe, item)
                    f = qb[:].rearrange("p a d -> p (a d)")
                    for i in range(4):
                        last = turn(bf(item)[:, i * P:(i + 1) * P], f[:, i * P:(i + 1) * P], id_bf[:])
                    fills(last, item)
                    item = ("wb", b)
                    wait_empty(pe, item)
                    for o in range(2):
                        last = mm_halves(bank(item)[:, o * P:(o + 1) * P],
                                         sm[:, b, 25 + o:26 + o].broadcast_to([P, P]), ident)
                    fills(last, item)
                elif kind == "x_mm2":
                    b, = a
                    item = ("h2", b)
                    wait_emptied(pe, ("aqT", b))
                    wait_empty(pe, item)
                    f = qTs[:].rearrange("p a d -> p (a d)")
                    for j in range(NJ):
                        last = mm(bank(item)[:, j * 256:(j + 1) * 256], f[:, j * P:(j + 1) * P], f[:, 256:512])
                    fills(last, item)
                elif kind == "r_T":
                    b, = a
                    item = ("h3T", b)
                    pe.wait_ge(sg["h_ready"], nth("r_stats", b) + 1)
                    wait_empty(pe, item)
                    for k in range(KD):
                        for j in range(NJ):
                            last = turn(bank(item)[:, k * 256 + j * P:k * 256 + (j + 1) * P],
                                        h3[:, b % 2, j, k * P:(k + 1) * P])
                    fills(last, item)
                elif kind == "r_logit":
                    b, = a
                    item = ("logit", b)
                    wait_emptied(pe, ("rwT",))
                    wait_emptied(pe, ("h3T", b))
                    wait_empty(pe, item)
                    for j in range(NJ):
                        for k in range(KD):
                            last = mm_halves(bank(item)[:, j * E:(j + 1) * E], h3T[:, b, k, j * P:(j + 1) * P],
                                      rwT[:, k, :], k == 0, k == KD - 1)
                    fills(last, item)
                elif kind == "r_pos":
                    b, = a
                    item = ("pos", b)
                    pe.wait_ge(sg["chosen_ready"], b + 1)
                    wait_empty(pe, item)
                    for j in range(NJ):
                        t = NJ * b + j
                        last = mm(bank(item)[:, j * E:(j + 1) * E], tri_bf[:], chosen[:, t, :], True, t == 0)
                        for tt in range(t):
                            last = mm(bank(item)[:, j * E:(j + 1) * E], ones_bf[:], chosen[:, tt, :],
                                      False, tt == t - 1)
                    fills(last, item)
                elif kind in ("s_gate", "s_up"):
                    b, = a
                    i = ("s_gate", "s_up").index(kind)
                    item = (("sg", "su")[i], b)
                    wait_emptied(pe, ("shT", i))
                    wait_emptied(pe, ("h3T", b))
                    wait_empty(pe, item)
                    for oh_ in range(2):
                        for k in range(KD):
                            last = mm(bank(item)[:, oh_ * 256:(oh_ + 1) * 256],
                                      shT[:, i, k, oh_ * P:(oh_ + 1) * P], h3T[:, b, k, :], k == 0, k == KD - 1)
                    fills(last, item)
                elif kind == "s_down":
                    b, = a
                    item = ("sd", b)
                    wait_emptied(pe, ("shT", 2))
                    wait_emptied(pe, ("su", b))
                    wait_empty(pe, item)
                    for j in range(NJ):
                        for k in range(2):
                            last = mm(bank(item)[:, j * 256:(j + 1) * 256], act_s[:, b % 2, k, j * P:(j + 1) * P],
                                      shT[:, 2, k, :], k == 0, k == 1)
                    fills(last, item)
                elif kind == "xpT":
                    i, = a
                    pe.wait_ge(ld_rows[i], 16)
                    wait_empty(pe, step)
                    for k in range(KD):
                        for s in range(2):
                            last = turn(bank(step)[:, k * 256 + s * P:k * 256 + (s + 1) * P],
                                        rows[:, 2 * i + s, k * P:(k + 1) * P])
                    fills(last, step)
                elif kind == "gate_up":
                    g, = a
                    item = ("gu", g)
                    pe.wait_ge(ld_experts[g], 16 * 3 * XG)
                    for i in range((g * XG * CAP) // 256, min(-(-((g + 1) * XG * CAP + XR - CAP) // 256), NS // 2)):
                        wait_emptied(pe, ("xpT", i))
                    if g == 0:
                        pe.wait_ge(sg["padding_ready"], 1)
                    wait_empty(pe, item)
                    for pair in range(XG // 2):
                        for k in range(KD):
                            for side in range(2):
                                e = g * XG + 2 * pair + side
                                last = mm(bank(item)[side * XR:(side + 1) * XR, pair * 256:(pair + 1) * 256],
                                          xpT[:, k, e * CAP:e * CAP + XR], gate_up_of(e)[:, k, :],
                                          k == 0, k == KD - 1)
                    fills(last, item)
                elif kind == "mix":
                    t, = a
                    pe.wait_ge(sg["onehot_ready"], NPAIR)
                    wait_emptied(pe, ("dn", NG_E - 1))
                    wait_empty(pe, step)
                    c0 = MIXED.index(t) * P
                    for i in range(NPAIR):
                        last = mm(bank(step)[:, 0:D], onehot[:, i, c0:c0 + P],
                                  ybuf(i // 2)[:, (i % 2) * D:(i % 2 + 1) * D], i == 0, i == NPAIR - 1)
                    fills(last, step)
                elif kind == "hidT":
                    g, = a
                    wait_emptied(pe, ("gu", g))
                    wait_empty(pe, step)
                    for pair in range(XG // 2):
                        last = turn(bank(step)[:, pair * P:(pair + 1) * P], hE[:, g % 2, pair * P:(pair + 1) * P])
                    fills(last, step)
                elif kind == "down":
                    g, = a
                    item = ("dn", g)
                    wait_emptied(pe, ("hidT", g))
                    wait_empty(pe, item)
                    for pair in range(XG // 2):
                        for side in range(2):
                            e = g * XG + 2 * pair + side
                            c0 = pair * P + side * XR
                            last = mm(bank(item)[side * XR:(side + 1) * XR, pair * 256:(pair + 1) * 256],
                                      hET[:, g % 2, c0:c0 + XR], down_of(e))
                    fills(last, item)

        @block.scalar
        def _(act):
            def copy(out_, in_, scale=1.0):
                return nc.scalar.activation(out_, in_, ACT.Copy, scale=scale)

            for step in steps:
                kind, a = step[0], step[1:]
                if kind == "hT":
                    t, = a
                    wait_filled(act, step)
                    if t >= 2:
                        wait_filled(act, ("fused", t - 2))
                    empties(copy(hT_f[:, t % 2, :], bank(step)[:, 0:256]), step)
                elif kind == "fused":
                    t, = a
                    wait_filled(act, step)
                    if t >= 1:
                        act.wait_ge(sg["squares_ready"], t)
                        act.wait_ge(sg["lat_ready"], t)
                    nc.scalar.activation(sq[:, 0:QL], bank(step)[:, 0:QL], ACT.Square, scale=float(QL) ** -0.5,
                                         accum_out=ssq[:, t, 0:1])
                    nc.scalar.activation(sq[:, QL:QL + KL], bank(step)[:, QL:QL + KL], ACT.Square,
                                         scale=float(KL) ** -0.5, accum_out=ssq[:, t, 1:2]
                                         ).then_inc(sg["squares_ready"], 1)
                    empties(copy(fused_s, bank(step)[:, 0:QL + KL + DR]), step)
                elif kind == "latT":
                    t, = a
                    wait_filled(act, step)
                    copy(qn0[:, t, :], bank(step)[:, 0:P])
                    copy(kT[:, t // 2, (t % 2) * P:(t % 2 + 1) * P], bank(step)[:, P:2 * P])
                    empties(copy(qn1[:, t, :], bank(step)[0:64, 2 * P:3 * P]), step)
                elif kind == "prepT" and a[0] % 2 == 0:
                    h, = a
                    wait_filled(act, step)
                    if h >= 4:
                        wait_filled(act, ("prepM", h // 2 - 2))
                    empties(copy(wT[:, h % 4, :], bank(step)[:, 0:320]), step)
                elif kind == "q":
                    t, c = a
                    u = nth(*step)
                    wait_filled(act, step)
                    if u >= 2:
                        wait_filled(act, q_order[u - 2])
                    if u >= 2:
                        act.wait_ge(sg["rope_added"], u - 1)
                    empties(copy(qs[:, u % 2], bank(step), SM_SCALE), step)
                elif kind == "qT":
                    t, c = a
                    b = t // NJ
                    wait_filled(act, step)
                    C = (NH // HC) * b + c
                    if C >= 2:
                        act.wait_ge(sg["scores_ready"], HC * (C - 1))
                    empties(copy(qT[:, C % 2, :, (t % 2) * P:(t % 2 + 1) * P],
                                 bank(step).rearrange("p (h m) -> p h m", h=HC)), step)
                elif kind == "scores":
                    hn, = a
                    act.wait_ge(sg["max_ready"], hn + 1)
                    if hn >= 4:
                        act.wait_ge(sg["probsT_done"], hn - 3)
                    s = psum[:, BANK_S + hn % 2, :]
                    nc.scalar.activation(probs[:, hn % 4, 0:P], s[:, 0:P], ACT.Exp, bias=nmax[:, hn, 0:1],
                                         accum_out=sums[:, hn, 0:1])
                    nc.scalar.activation(probs[:, hn % 4, P:3 * P], s[:, P:3 * P], ACT.Exp, bias=nmax[:, hn, 1:2],
                                         accum_out=sums[:, hn, 1:2]).then_inc(sg["exp_done"], 1)
                elif kind == "probsT" and a[0] % 2 != PT_DVE:
                    hn, = a
                    act.wait_ge(sg["probsT_done"], hn + 1)
                    if hn >= 4:
                        act.wait_ge(sg["heads_done"], hn // 2 - 1)
                    copy(probsT[:, hn % 4, :], ps_pt[:, 0:384]).then_inc(sg["probsT_copied"], 1)
                elif kind == "pv" and a[0] % 2 == 1:
                    pr, = a
                    b, i0 = pr // (NH // 2), (pr % (NH // 2)) - 1
                    act.wait_ge(sg["heads_done"], pr + 1)
                    if b >= 2 and i0 == 0:
                        for j in range(NJ):
                            wait_filled(act, ("y", NJ * (b - 2) + j))
                    if b == 1 and i0 == 0:
                        act.wait_ge(sg["xp_zeroed"], 16 * NZ)
                    copy(oT[:, b % 2, i0:i0 + 2, :].rearrange("p i t -> p (i t)"), ps_o
                         ).then_inc(sg["heads_copied"], 1)
                elif kind == "wx":
                    b, = a
                    if b >= 1:
                        act.wait_ge(sg["scaledT_w"], b)
                        act.wait_ge(sg["scaledT_c"], b)
                    wait_filled(act, ("fsT", b))
                    empties(copy(fsT[:], bank(("fsT", b))), ("fsT", b))
                    wait_filled(act, ("cxT", b))
                    empties(copy(cxT[:], bank(("cxT", b))[:, 0:256]), ("cxT", b))
                elif kind == "rwT":
                    wait_filled(act, step)
                    empties(copy(rwT[:].rearrange("p k e -> p (k e)"), bank(step)[:, 0:KD * E]), step)
                elif kind == "shT":
                    i, = a
                    wait_filled(act, step)
                    empties(copy(shT[:, i].rearrange("p k d -> p (k d)"), bank(step)), step)
                elif kind == "x_scale":
                    b, = a
                    act.wait_ge(sg["smooth_ready"], b + 1)
                    if b >= 1:
                        wait_filled(act, ("as", b - 1))
                    for k in range(KD):
                        last = copy(xsT[:, k * 256:(k + 1) * 256], bank(("xT", b))[:, k * 256:(k + 1) * 256],
                                    sm[:, b, 8 + k:9 + k])
                    empties(last, ("xT", b))
                elif kind == "x_qscale":
                    b, = a
                    act.wait_ge(sg["inv_ready"], b + 1)
                    if b >= 1:
                        act.wait_ge(sg["q2_ready"], b)
                    for i, item in enumerate((("xs", b), ("ws", b))):
                        for j in range(2):
                            last = copy(qa[:, 2 * i + j, :], bank(item)[:, j * 256:(j + 1) * 256],
                                        sm[:, b, 14 + 2 * i + j:15 + 2 * i + j])
                        empties(last, item)
                elif kind == "x_qT":
                    b, = a
                    wait_filled(act, ("xqT", b))
                    if b >= 1:
                        wait_filled(act, ("h2", b - 1))
                    empties(copy(qTs[:].rearrange("p a d -> p (a d)"), bank(("xqT", b)).bitcast(BF16)), ("xqT", b))
                    wait_filled(act, ("xb", b))
                    if b >= 1:
                        wait_emptied(act, ("h1", b - 1))
                    empties(copy(sbc[:, 0, :], bank(("xb", b))[:, 0:256]), ("xb", b))
                elif kind == "x_tanh":
                    b, = a
                    wait_emptied(act, ("h1", b))
                    nc.scalar.activation(gu[:, 2, :], gu[:, 0, :], ACT.Tanh, scale=0.5).then_inc(sg["gate_tanh"], 1)
                elif kind == "x_scale2":
                    b, = a
                    act.wait_ge(sg["smooth_ready2"], b + 1)
                    wait_filled(act, ("xs", b))
                    copy(xsT[:, 0:256], gu[:, 3, :], sm[:, b, 22:23]).then_inc(sg["scaledT_a"], 1)
                elif kind == "x_qscale2":
                    b, = a
                    act.wait_ge(sg["inv2_ready"], b + 1)
                    act.wait_ge(sg["q_ready"], b + 1)
                    f = reg_r[:, 0:1024]
                    for i in range(4):
                        last = copy(f[:, i * P:(i + 1) * P], bank(("as", b))[:, i * P:(i + 1) * P],
                                    sm[:, b, 27 + i:28 + i])
                    empties(last, ("as", b))
                elif kind == "x_qT2":
                    b, = a
                    wait_filled(act, ("aqT", b))
                    wait_filled(act, ("h1", b))
                    empties(copy(qTs[:].rearrange("p a d -> p (a d)")[:, 0:512],
                                 bank(("aqT", b)).bitcast(BF16)[:, 0:512]), ("aqT", b))
                    wait_filled(act, ("wb", b))
                    empties(copy(sbc[:, 1, :], bank(("wb", b))[:, 0:256]), ("wb", b))
                elif kind == "r_T":
                    b, = a
                    wait_filled(act, ("h3T", b))
                    empties(copy(h3T[:, b].rearrange("p k t -> p (k t)"), bank(("h3T", b))), ("h3T", b))
                elif kind == "r_logit":
                    b, = a
                    wait_filled(act, ("logit", b))
                    if b >= 1:
                        act.wait_ge(sg["weights_ready"], b)
                    empties(nc.scalar.activation(sc[:, 0, :], bank(("logit", b))[:, 0:NJ * E], ACT.Exp, scale=-1.0),
                            ("logit", b))
                elif kind == "s_gate":
                    b, = a
                    wait_filled(act, ("sg", b))
                    if b >= 1:
                        wait_emptied(act, ("sg", b - 1))
                    nc.scalar.activation(es[:, 0, :], bank(("sg", b)), ACT.Tanh, scale=0.5
                                         ).then_inc(sg["shared_tanh"], 1)
                elif kind == "xpT" and a[0] % 2 == 0:
                    i, = a
                    wait_filled(act, step)
                    empties(copy(xpT[:, :, i * 256:(i + 1) * 256],
                                 bank(step).rearrange("p (k s) -> p k s", k=KD)), step)
                elif kind == "gate_up":
                    g, = a
                    wait_filled(act, ("gu", g))
                    if g >= 2:
                        wait_emptied(act, ("gu", g - 2))
                    nc.scalar.activation(
                        th[:, g % 2, :].rearrange("p (i m) -> p i m", i=2),
                        bank(("gu", g)).rearrange("p (i two m) -> p i two m", i=2, two=2)[:, :, 0, :],
                        ACT.Tanh, scale=0.5).then_inc(sg["expert_tanh"], 1)
                elif kind == "hidT":
                    g, = a
                    wait_filled(act, step)
                    if g >= 2:
                        wait_filled(act, ("dn", g - 2))
                    empties(copy(hET[:, g % 2, :], bank(step)[:, 0:256]), step)
                elif kind == "down":
                    g, = a
                    wait_filled(act, ("dn", g))
                    if g >= 3:
                        wait_filled(act, ("xpT", g - 3))
                    empties(copy(ybuf(g), bank(("dn", g))), ("dn", g))

        @block.vector
        def _(dve):
            v = nc.vector
            chain = [0]

            def link(ins):
                chain[0] += 1
                ins.then_inc(sg["dve_chain"], 1)
                dve.wait_ge(sg["dve_chain"], chain[0])

            def ln_stats(tag, b):
                for j in range(NJ):
                    link(v.bn_stats(stats[:, j, :], xres[:, NJ * b + j, :]))
                for j in range(NJ):
                    last = v.bn_aggr(mv[:, tag, NJ * b + j, :], stats[:, j, :])
                last.then_inc(sg["ln_stats"], 1)

            def ln_normalise(tag, b, i, dst):
                dve.wait_ge(sg["ln_rstd"], i + 1)
                for j in range(NJ):
                    t = NJ * b + j
                    last = v.tensor_scalar(dst(j), xres[:, t, :], mv[:, tag, t, 0:1], rstd[:, tag, t:t + 1],
                                           ALU.subtract, ALU.mult)
                last.then_inc(sg["h_ready"], 1)

            for step in steps:
                kind, a = step[0], step[1:]
                if kind == "setup":
                    v.memset(zeros, 0.0).then_inc(sg["zeros_ready"], 1)
                    link(v.memset(ones_bf[:], 1.0))
                elif kind == "ln1_stats":
                    b, = a
                    dve.wait_ge(ld[f"x{b}"], 16)
                    ln_stats(0, b)
                elif kind == "ln1_norm":
                    b, = a
                    if b >= 1:
                        for j in range(NJ):
                            wait_filled(dve, ("hT", NJ * (b - 1) + j))
                    ln_normalise(0, b, nth("ln1_stats", b), lambda j: hn_f[:, j, :])
                    if b == 0:
                        dve.wait_ge(ld["consts"], 16)
                        v.tensor_copy(id_bf[:], ident)
                        v.tensor_copy(mask_bf[:], c_(C_MASK, P))
                        v.tensor_copy(tri_bf[:], c_(C_TRI, P)).then_inc(sg["consts_ready"], 1)
                elif kind == "latents":
                    t, = a
                    if t == 0:
                        dve.wait_ge(ld["gam"], 32)
                    dve.wait_ge(sg["rms_ready"], t + 1)
                    wait_emptied(dve, ("fused", t))
                    if t >= 2:
                        wait_filled(dve, ("latT", t - 2))
                    v.scalar_tensor_tensor(qn[:, t % 2, :], fused_s[:, 0:QL], rrms[:, t, 0:1], gam_q[:],
                                           ALU.mult, ALU.mult)
                    v.scalar_tensor_tensor(kv[:, t, 0:KL], fused_s[:, QL:QL + KL], rrms[:, t, 1:2], gam_kv[:],
                                           ALU.mult, ALU.mult)
                    if t >= 1:
                        dve.wait_ge(sg["lat_ready"], t)
                    kp = fused_s[:, QL + KL:QL + KL + DR]
                    o = (t % NJ) * DR
                    v.tensor_tensor(kr[:, 0, :], kp, c_(C_COS + o, DR), ALU.mult)
                    link(v.tensor_tensor(kr[:, 1, :].rearrange("p (two x) -> p two x", two=2)[:, ::-1, :],
                                         kp.rearrange("p (two x) -> p two x", two=2),
                                         c_(C_SIN + o, DR).rearrange("p (two x) -> p two x", two=2), ALU.mult))
                    v.tensor_tensor(kv[:, t, KL:], kr[:, 0, :], kr[:, 1, :], ALU.add).then_inc(sg["lat_ready"], 1)
                elif kind == "prepT" and a[0] % 2 == 1:
                    h, = a
                    wait_filled(dve, step)
                    if h >= 4:
                        wait_filled(dve, ("prepM", h // 2 - 2))
                    empties(v.tensor_copy(wT[:, h % 4, :], bank(step)[:, 0:320]), step)
                elif kind == "prepM":
                    p, = a
                    wait_filled(dve, step)
                    pb = bank(step)
                    v.tensor_copy(wf0[:, 2 * p:2 * p + 2, 0:KL], pb[:, 0:128].rearrange("p (h m) -> p h m", h=2))
                    v.tensor_copy(wf1[:, 2 * p:2 * p + 2, 0:KL],
                                  pb[0:64, 128:256].rearrange("p (h m) -> p h m", h=2))
                    empties(v.tensor_copy(w_mo[:, p, :], pb[:, 256:512]), step)
                elif kind == "rope":
                    t, c = a
                    u = nth(*step)
                    wait_emptied(dve, ("q",) + a)
                    if u >= 2:
                        dve.wait_ge(sg["rope_added"], u - 1)
                    o = (t % NJ) * DR
                    qp = qs[:, u % 2].rearrange("p (h m) -> p h m", h=HC)[:, :, KL:]
                    v.tensor_tensor(
                        qr[:, u % 2].rearrange("p (h two x) -> p h two x", h=HC, two=2)[:, :, ::-1, :],
                        qp.rearrange("p h (two x) -> p h two x", two=2),
                        c_(C_SIN + o, DR).rearrange("p (o two x) -> p o two x", o=1, two=2
                                                    ).broadcast_to([P, HC, 2, DR // 2]), ALU.mult)
                    v.tensor_tensor(qp, qp,
                                    c_(C_COS + o, DR).rearrange("p (o x) -> p o x", o=1).broadcast_to([P, HC, DR]),
                                    ALU.mult).then_inc(sg["rope_parts"], 1)
                elif kind == "norm":
                    hn, = a
                    dve.wait_ge(sg["exp_done"], hn + 1)
                    link(v.reciprocal(rsum[:, hn, :], sums[:, hn, :]))
                    pr = probs[:, hn % 4, :]
                    v.tensor_scalar(pr[:, 0:P], pr[:, 0:P], rsum[:, hn, 0:1], None, ALU.mult)
                    v.tensor_scalar(pr[:, P:3 * P], pr[:, P:3 * P], rsum[:, hn, 1:2], None, ALU.mult
                                    ).then_inc(sg["probs_normed"], 1)
                elif kind == "scores":
                    hn, = a
                    dve.wait_ge(sg["scores_ready"], hn + 1)
                    s = psum[:, BANK_S + hn % 2, :]
                    v.tensor_reduce(nmax[:, hn, 0:1], s[:, 0:P], AX.X, ALU.max, negate=True)
                    v.tensor_reduce(nmax[:, hn, 1:2], s[:, P:3 * P], AX.X, ALU.max, negate=True
                                    ).then_inc(sg["max_ready"], 1)
                elif kind == "probsT":
                    hn, = a
                    if hn % 2 == PT_DVE:
                        dve.wait_ge(sg["probsT_done"], hn + 1)
                        if hn >= 4:
                            dve.wait_ge(sg["heads_done"], hn // 2 - 1)
                        v.tensor_copy(probsT[:, hn % 4, :], ps_pt[:, 0:384]).then_inc(sg["probsT_copied"], 1)
                elif kind == "y_add":
                    t, = a
                    item = ("y", t)
                    wait_filled(dve, item)
                    empties(v.tensor_tensor(xres[:, t, :], bank(item)[:, 0:D], xres[:, t, :], ALU.add), item)
                    if t == NT - 1:
                        v.memset(xpT[:, :, SLOTS:], 0.0).then_inc(sg["padding_ready"], 1)
                elif kind == "wx":
                    b, = a
                    wait_emptied(dve, ("fsT", b))
                    v.tensor_reduce(rden[:, b, 0:2], fsT[:].rearrange("p (k o) -> p k o", k=KD), AX.X, ALU.max,
                                    apply_absolute_value=True)
                    wait_emptied(dve, ("cxT", b))
                    link(v.tensor_reduce(rden[:, b, 2:3], cxT[:], AX.X, ALU.max, apply_absolute_value=True))
                    link(v.tensor_scalar(rden[:, b, :], rden[:, b, :], EPS_Q, None, ALU.max))
                    link(v.reciprocal(rden[:, b, :], rden[:, b, :]))
                elif kind == "x_stats":
                    b, = a
                    for j in range(NJ):
                        wait_emptied(dve, ("y", NJ * b + j))
                    ln_stats(1, b)
                elif kind == "x_norm":
                    b, = a
                    if b >= 1:
                        wait_filled(dve, ("xT", b - 1))
                    ln_normalise(1, b, nth("x_stats", b), lambda j: h2[:, j, :])
                elif kind == "x_T":
                    b, = a
                    item = ("xT", b)
                    wait_filled(dve, item)
                    link(v.tensor_reduce(sm[:, b, 0:2], bank(item).rearrange("p (k t) -> p k t", k=KD), AX.X, ALU.max,
                                         apply_absolute_value=True))
                    v.scalar_tensor_tensor(sm[:, b, 2:4], sm[:, b, 0:2], EPS_Q, rden[:, b, 0:2], ALU.max, ALU.mult
                                           ).then_inc(sg["ratio_ready"], 1)
                elif kind == "x_smooth":
                    b, = a
                    dve.wait_ge(sg["smooth_root"], b + 1)
                    link(v.tensor_scalar(sm[:, b, 6:8], sm[:, b, 4:6], EPS_Q, None, ALU.max))
                    v.reciprocal(sm[:, b, 8:10], sm[:, b, 6:8]).then_inc(sg["smooth_ready"], 1)
                    wait_emptied(dve, ("fsT", b))
                    if b >= 1:
                        wait_filled(dve, ("as", b - 1))
                    for k in range(KD):
                        last = v.tensor_scalar(wsT[:, k * 256:(k + 1) * 256], fsT[:, k * 256:(k + 1) * 256],
                                               sm[:, b, 6 + k:7 + k], None, ALU.mult)
                    last.then_inc(sg["scaledT_w"], 1)
                elif kind == "x_back":
                    b, = a
                    for i, item in enumerate((("xs", b), ("ws", b))):
                        wait_filled(dve, item)
                        last = v.tensor_reduce(sm[:, b, 10 + 2 * i:12 + 2 * i],
                                               bank(item).rearrange("p (j d) -> p j d", j=2), AX.X, ALU.max,
                                               apply_absolute_value=True)
                    link(last)
                    link(v.tensor_scalar(sm[:, b, 10:14], sm[:, b, 10:14], EPS_Q, 1.0 / QMAX, ALU.max, ALU.mult))
                    v.reciprocal(sm[:, b, 14:18], sm[:, b, 10:14]).then_inc(sg["inv_ready"], 1)
                elif kind == "x_round":
                    b, = a
                    for item in (("xs", b), ("ws", b)):
                        wait_emptied(dve, item)
                    link(v.tensor_scalar(qa, qa, QMAX, -QMAX, ALU.min, ALU.max))
                    if b >= 1:
                        wait_filled(dve, ("aqT", b - 1))
                    v.tensor_scalar(qb[:], qa, ROUND, ROUND, ALU.add, ALU.subtract).then_inc(sg["q_ready"], 1)
                elif kind == "x_mm":
                    b, = a
                    item = ("h1", b)
                    wait_filled(dve, item)
                    wait_emptied(dve, ("xb", b))
                    for i in range(2):
                        last = v.scalar_tensor_tensor(gu[:, i, :], bank(item)[:, i * 256:(i + 1) * 256],
                                                      sm[:, b, 12 + i:13 + i], sbc[:, 0, :], ALU.mult, ALU.mult)
                    empties(last, item)
                elif kind == "x_gate":
                    b, = a
                    dve.wait_ge(sg["gate_tanh"], b + 1)
                    link(v.scalar_tensor_tensor(gu[:, 2, :], gu[:, 2, :], 1.0, gu[:, 0, :], ALU.add, ALU.mult))
                    link(v.scalar_tensor_tensor(gu[:, 3, :], gu[:, 2, :], 0.5, gu[:, 1, :], ALU.mult, ALU.mult))
                    link(v.tensor_reduce(sm[:, b, 18:19], gu[:, 3, :], AX.X, ALU.max, apply_absolute_value=True))
                    v.scalar_tensor_tensor(sm[:, b, 19:20], sm[:, b, 18:19], EPS_Q, rden[:, b, 2:3], ALU.max,
                                           ALU.mult).then_inc(sg["ratio2_ready"], 1)
                elif kind == "x_smooth2":
                    b, = a
                    dve.wait_ge(sg["smooth_root2"], b + 1)
                    link(v.tensor_scalar(sm[:, b, 21:22], sm[:, b, 20:21], EPS_Q, None, ALU.max))
                    v.reciprocal(sm[:, b, 22:23], sm[:, b, 21:22]).then_inc(sg["smooth_ready2"], 1)
                    wait_filled(dve, ("ws", b))
                    v.tensor_scalar(wsT[:, 0:256], cxT[:], sm[:, b, 21:22], None, ALU.mult
                                    ).then_inc(sg["scaledT_c"], 1)
                elif kind == "x_back2":
                    b, = a
                    item = ("as", b)
                    wait_filled(dve, item)
                    link(v.tensor_reduce(sm[:, b, 23:27], bank(item).rearrange("p (i m) -> p i m", i=4), AX.X, ALU.max,
                                         apply_absolute_value=True))
                    link(v.tensor_scalar(sm[:, b, 23:27], sm[:, b, 23:27], EPS_Q, 1.0 / QMAX, ALU.max, ALU.mult))
                    v.reciprocal(sm[:, b, 27:31], sm[:, b, 23:27]).then_inc(sg["inv2_ready"], 1)
                elif kind == "x_round2":
                    b, = a
                    wait_emptied(dve, ("as", b))
                    fa = reg_r[:, 0:1024][:, 0:512]
                    fb = qb[:].rearrange("p a d -> p (a d)")[:, 0:512]
                    link(v.tensor_scalar(fa, fa, QMAX, -QMAX, ALU.min, ALU.max))
                    wait_filled(dve, ("xqT", b))
                    v.tensor_scalar(fb, fa, ROUND, ROUND, ALU.add, ALU.subtract).then_inc(sg["q2_ready"], 1)
                elif kind == "x_mm2":
                    b, = a
                    item = ("h2", b)
                    wait_filled(dve, item)
                    wait_emptied(dve, ("wb", b))
                    for j in range(NJ):
                        last = v.scalar_tensor_tensor(gu[:, j, :], bank(item)[:, j * 256:(j + 1) * 256],
                                                      sm[:, b, 23 + j:24 + j], sbc[:, 1, :], ALU.mult, ALU.mult)
                    empties(last, item)
                    wait_emptied(dve, item)
                    xb = xres[:, NJ * b:NJ * (b + 1), :]
                    link(v.tensor_tensor(xb, xb, gu[:, 0:2, :], ALU.add))
                    if b == B - 1:
                        v.memset(meta, 0.0).then_inc(sg["meta_zeroed"], 1)
                elif kind == "r_stats":
                    b, = a
                    ln_stats(2, b)
                elif kind == "r_norm":
                    b, = a
                    if b >= 2:
                        dve.wait_ge(scattered[b - 2], 16 * NJ * TOPK)
                        wait_filled(dve, ("h3T", b - 2))
                    ln_normalise(2, b, nth("r_stats", b), lambda j: h3[:, b % 2, j, 0:D])
                elif kind == "r_groups":
                    b, = a
                    wait_emptied(dve, ("logit", b))
                    if b == 0:
                        dve.wait_ge(ld["bias"], 16)
                    link(v.tensor_scalar(sc[:, 0, :], sc[:, 0, :], 1.0, None, ALU.add))
                    link(v.reciprocal(sc[:, 1, :], sc[:, 0, :]))
                    link(v.tensor_tensor(
                        sc[:, 2, :].rearrange("p (j e) -> p j e", j=NJ), sc[:, 1, :].rearrange("p (j e) -> p j e", j=NJ),
                        bias_e[:].rearrange("p (o e) -> p o e", o=1).broadcast_to([P, NJ, E]), ALU.add))
                    n2 = NJ * NG
                    quad = sc[:, 2, :].rearrange("p (g two x) -> p g two x", two=2, x=2)
                    hi = rt[:, 0, 0:2 * n2].rearrange("p (g two) -> p g two", two=2)
                    lo = rt[:, 1, 0:2 * n2].rearrange("p (g two) -> p g two", two=2)
                    v.tensor_tensor(hi, quad[:, :, :, 0], quad[:, :, :, 1], ALU.max)
                    link(v.tensor_tensor(lo, quad[:, :, :, 0], quad[:, :, :, 1], ALU.min))
                    v.tensor_tensor(rt[:, 2, 0:n2], hi[:, :, 0], hi[:, :, 1], ALU.max)
                    v.tensor_tensor(rt[:, 3, 0:n2], hi[:, :, 0], hi[:, :, 1], ALU.min)
                    link(v.tensor_tensor(rt[:, 4, 0:n2], lo[:, :, 0], lo[:, :, 1], ALU.max))
                    link(v.tensor_tensor(rt[:, 5, 0:n2], rt[:, 3, 0:n2], rt[:, 4, 0:n2], ALU.max))
                    gs = rt[:, 6, 0:n2]
                    link(v.tensor_tensor(gs, rt[:, 2, 0:n2], rt[:, 5, 0:n2], ALU.add))
                elif kind == "r_best":
                    n2 = NJ * NG
                    gs = rt[:, 6, 0:n2]
                    for j in range(NJ):
                        last = v.max(top[:, j, :], gs[:, j * NG:(j + 1) * NG])
                    link(last)
                    for j in range(NJ):
                        last = v.max_index(topi[:, j, :], top[:, j, :], gs[:, j * NG:(j + 1) * NG])
                    link(last)
                    link(v.tensor_copy(tif[:, :, 0:TKG], topi[:, :, 0:TKG]))
                    eqg = rt[:, 7, 0:NJ * TKG * NG].rearrange("p (j k g) -> p j k g", j=NJ, k=TKG)
                    link(v.tensor_tensor(
                        eqg, c_(C_I8, NG).rearrange("p (a o g) -> p a o g", a=1, o=1).broadcast_to([P, NJ, TKG, NG]),
                        tif[:, :, 0:TKG].rearrange("p j (k o) -> p j k o", o=1).broadcast_to([P, NJ, TKG, NG]),
                        ALU.is_equal))
                    gm = rt[:, 8, 0:n2]
                    link(v.tensor_reduce(gm.rearrange("p (j g) -> p j g", j=NJ),
                                         eqg.rearrange("p j k g -> p j g k"), AX.X, ALU.add))
                    mk = rt[:, 9, :]
                    link(v.tensor_tensor(mk.rearrange("p (g x) -> p g x", x=EG),
                                         sc[:, 2, :].rearrange("p (g x) -> p g x", x=EG),
                                         gm.rearrange("p (g o) -> p g o", o=1).broadcast_to([P, n2, EG]), ALU.mult))
                    link(v.tensor_scalar(mk, mk, 0.0, None, ALU.add))
                elif kind == "r_choose":
                    b, = a
                    mk = rt[:, 9, :]
                    for j in range(NJ):
                        last = v.max(top[:, j, :], mk[:, j * E:(j + 1) * E])
                    link(last)
                    for j in range(NJ):
                        last = v.max_index(topi[:, j, :], top[:, j, :], mk[:, j * E:(j + 1) * E])
                    link(last)
                    link(v.tensor_copy(tif[:], topi[:, :, 0:TOPK]))
                    oh4 = oh.rearrange("p (j k e) -> p j k e", j=NJ, k=TOPK)
                    ohp4 = ohp.rearrange("p (j k e) -> p j k e", j=NJ, k=TOPK)
                    link(v.tensor_tensor(
                        oh4, c_(C_I32, E).rearrange("p (a o g) -> p a o g", a=1, o=1).broadcast_to([P, NJ, TOPK, E]),
                        tif[:].rearrange("p j (k o) -> p j k o", o=1).broadcast_to([P, NJ, TOPK, E]), ALU.is_equal))
                    with nc.allow_low_precision("zeros and ones"):
                        v.tensor_reduce(chosen[:, NJ * b:NJ * (b + 1), :], oh4.rearrange("p j k e -> p j e k"), AX.X,
                                        ALU.add).then_inc(sg["chosen_ready"], 1)
                elif kind == "r_weights":
                    b, = a
                    oh4 = oh.rearrange("p (j k e) -> p j k e", j=NJ, k=TOPK)
                    ohp4 = ohp.rearrange("p (j k e) -> p j k e", j=NJ, k=TOPK)
                    link(v.tensor_tensor(
                        ohp4, oh4, sc[:, 1, :].rearrange("p (j o e) -> p j o e", j=NJ, o=1
                                                         ).broadcast_to([P, NJ, TOPK, E]), ALU.mult))
                    wk = slotf[:, 0, :].rearrange("p (j k) -> p j k", j=NJ)
                    link(v.tensor_reduce(wk, ohp4, AX.X, ALU.add))
                    ws_ = rt[:, 10, 0:NJ]
                    link(v.tensor_reduce(ws_, wk, AX.X, ALU.add))
                    link(v.tensor_scalar(ws_, ws_, 1e-20, None, ALU.add))
                    link(v.reciprocal(ws_, ws_))
                    link(v.tensor_scalar(ws_, ws_, 2.5, None, ALU.mult))
                    v.tensor_tensor(h3[:, b % 2, :, W_WT:W_EX], wk,
                                    ws_.rearrange("p (j o) -> p j o", o=1).broadcast_to([P, NJ, TOPK]), ALU.mult
                                    ).then_inc(sg["weights_ready"], 1)
                elif kind == "r_slots":
                    b, = a
                    item = ("pos", b)
                    wait_filled(dve, item)
                    pos = bank(item)[:, 0:NJ * E]
                    oh4 = oh.rearrange("p (j k e) -> p j k e", j=NJ, k=TOPK)
                    ohp4 = ohp.rearrange("p (j k e) -> p j k e", j=NJ, k=TOPK)
                    v.tensor_scalar(rt[:, 0, :], pos, float(CAP), NOSLOT, ALU.is_ge, ALU.mult)
                    empties(v.tensor_tensor(
                        rt[:, 1, :].rearrange("p (j e) -> p j e", j=NJ), pos.rearrange("p (j e) -> p j e", j=NJ),
                        c_(C_SLOT0, E).rearrange("p (o e) -> p o e", o=1).broadcast_to([P, NJ, E]), ALU.add), item)
                    wait_emptied(dve, item)
                    link(v.tensor_tensor(rt[:, 0, :], rt[:, 0, :], rt[:, 1, :], ALU.add))
                    link(v.tensor_tensor(
                        ohp4, oh4, rt[:, 0, :].rearrange("p (j o e) -> p j o e", j=NJ, o=1
                                                         ).broadcast_to([P, NJ, TOPK, E]), ALU.mult))
                    sl = slotf[:, 1, :]
                    link(v.tensor_reduce(sl.rearrange("p (j k) -> p j k", j=NJ), ohp4, AX.X, ALU.add))
                    tt = slice(NJ * b, NJ * (b + 1))
                    dve.wait_ge(sg["weights_ready"], b + 1)
                    v.tensor_copy(scat[:, tt, :].rearrange("p j k -> p (j k)"), sl).then_inc(sg["slots_ready"], 1)
                    link(v.tensor_scalar(slotf[:, 3, :], sl, float(SLOTS - 1), None, ALU.min))
                    v.scalar_tensor_tensor(gath[:, tt, :].rearrange("p j k -> p (j k)"),
                                           tif[:].rearrange("p j k -> p (j k)"), float(XR - CAP), slotf[:, 3, :],
                                           ALU.mult, ALU.add)
                    link(v.tensor_scalar(slotf[:, 2, :], sl, float(SLOTS), None, ALU.is_lt))
                    v.tensor_tensor(wtok[:, tt, :], h3[:, b % 2, :, W_WT:W_EX],
                                    slotf[:, 2, :].rearrange("p (j k) -> p j k", j=NJ), ALU.mult
                                    ).then_inc(sg["gather_ready"], 1)
                elif kind == "s_silu":
                    b, = a
                    dve.wait_ge(sg["shared_tanh"], b + 1)
                    empties(v.scalar_tensor_tensor(es[:, 1, :], es[:, 0, :], 1.0, bank(("sg", b)),
                                                   ALU.add, ALU.mult), ("sg", b))
                elif kind == "s_mul":
                    b, = a
                    wait_emptied(dve, ("sg", b))
                    wait_filled(dve, ("su", b))
                    if b >= 2:
                        wait_filled(dve, ("sd", b - 2))
                    empties(v.scalar_tensor_tensor(act_s[:, b % 2].rearrange("p k t -> p (k t)"), es[:, 1, :], 0.5,
                                                   bank(("su", b)), ALU.mult, ALU.mult), ("su", b))
                elif kind == "s_add":
                    b, = a
                    item = ("sd", b)
                    wait_filled(dve, item)
                    xb = xres[:, NJ * b:NJ * (b + 1), :].rearrange("p j d -> p (j d)")
                    empties(v.tensor_tensor(xb, bank(item), xb, ALU.add), item)
                elif kind == "xpT" and a[0] % 2 == 1:
                    i, = a
                    wait_filled(dve, step)
                    empties(v.tensor_copy(xpT[:, :, i * 256:(i + 1) * 256],
                                          bank(step).rearrange("p (k s) -> p k s", k=KD)), step)
                elif kind == "gate_up":
                    g, = a
                    item = ("gu", g)
                    dve.wait_ge(sg["expert_tanh"], g + 1)
                    gu4 = bank(item).rearrange("p (i two m) -> p i two m", i=2, two=2)
                    tg = th[:, g % 2, :].rearrange("p (i m) -> p i m", i=2)
                    gg = th[:, 2 + g % 2, :].rearrange("p (i m) -> p i m", i=2)
                    link(v.scalar_tensor_tensor(gg, tg, 1.0, gu4[:, :, 0, :], ALU.add, ALU.mult))
                    if g >= 2:
                        wait_filled(dve, ("hidT", g - 2))
                    empties(v.scalar_tensor_tensor(hE[:, g % 2, :].rearrange("p (i m) -> p i m", i=2), gg, 0.5,
                                                   gu4[:, :, 1, :], ALU.mult, ALU.mult), item)
                elif kind == "slot_weights":
                    dve.wait_ge(ld["late"], 16)
                    dve.wait_ge(ld["meta"], 32)
                    sel = wsel[:, 0:TOPK, :].rearrange("p k i -> p i k")
                    link(v.tensor_tensor(
                        sel, meta[:, :, 1 + TOPK:],
                        late[:, 0:NPAIR].rearrange("p (i o) -> p i o", o=1).broadcast_to([P, NPAIR, TOPK]),
                        ALU.is_equal))
                    link(v.tensor_tensor(sel, sel, meta[:, :, 1:1 + TOPK], ALU.mult))
                    link(v.tensor_reduce(wsel[:, TOPK, :], sel, AX.X, ALU.add))
                elif kind == "onehot":
                    i, = a
                    if i == 0:
                        wait_filled(dve, ("dn", (SLOTS_A + SLOTS_B - 1) // XG))
                    v.tensor_scalar(onehot[:, i, :], late[:, NPAIR:], meta[:, i, 0:1], wsel[:, TOPK, i:i + 1],
                                    ALU.is_equal, ALU.mult).then_inc(sg["onehot_ready"], 1)
                elif kind == "mix":
                    t, = a
                    wait_filled(dve, step)
                    wait_emptied(dve, ("sd", t // NJ))
                    v.tensor_tensor(xres[:, t, :], bank(step)[:, 0:D], xres[:, t, :], ALU.add
                                    ).then_inc(sg["combined"], 1)
                elif kind == "combine":
                    t, = a
                    if t == 0:
                        for b in range(B):
                            wait_emptied(dve, ("sd", b))
                    for k in range(TOPK):
                        n = (t % 2) * TOPK + k
                        dve.wait_ge(gathered[n], 16 * (t // 2 + 1))
                        ins = v.scalar_tensor_tensor(xres[:, t, :], gbuf[:, n, :], wtok[:, t, k:k + 1],
                                                     xres[:, t, :], ALU.mult, ALU.add)
                        if k < TOPK - 1:
                            link(ins)
                    ins.then_inc(sg["combined"], 1)

        @block.gpsimd
        def _(pool):
            g = nc.gpsimd
            chain = [0]

            def link(ins):
                chain[0] += 1
                ins.then_inc(sg["pool_chain"], 1)
                pool.wait_ge(sg["pool_chain"], chain[0])

            for step in steps:
                kind, a = step[0], step[1:]
                if kind == "setup":
                    g.memset(neg_half[:], -0.5).then_inc(sg["halves_ready"], 1)
                    g.memset(pos_half[:], 0.5).then_inc(sg["halves_ready"], 1)
                    pool.wait_ge(sg["halves_ready"], 2)
                elif kind in ("ln1_stats", "x_stats", "r_stats"):
                    b, = a
                    tag = ("ln1_stats", "x_stats", "r_stats").index(kind)
                    tt = slice(NJ * b, NJ * (b + 1))
                    pool.wait_ge(sg["ln_stats"], nth(*step) + 1)
                    link(g.tensor_scalar(vtmp[:, tag, tt], mv[:, tag, tt, 1], EPS_LN, None, ALU.add))
                    g.tensor_tensor(rstd[:, tag, tt], vtmp[:, tag, tt], neg_half[:].broadcast_to([P, NJ]), ALU.pow
                                    ).then_inc(sg["ln_rstd"], 1)
                elif kind == "fused":
                    t, = a
                    pool.wait_ge(sg["squares_ready"], t + 1)
                    link(g.tensor_scalar(weps[:, t, :], ssq[:, t, :], EPS_RMS, None, ALU.add))
                    g.tensor_tensor(rrms[:, t, :], weps[:, t, :], neg_half[:].broadcast_to([P, 2]), ALU.pow
                                    ).then_inc(sg["rms_ready"], 1)
                elif kind == "rope":
                    u = nth(*step)
                    pool.wait_ge(sg["rope_parts"], u + 1)
                    qp = qs[:, u % 2].rearrange("p (h m) -> p h m", h=HC)[:, :, KL:]
                    g.tensor_tensor(qp, qp, qr[:, u % 2].rearrange("p (h x) -> p h x", h=HC), ALU.add
                                    ).then_inc(sg["rope_added"], 1)
                elif kind == "x_T":
                    b, = a
                    pool.wait_ge(sg["ratio_ready"], b + 1)
                    g.tensor_tensor(sm[:, b, 4:6], sm[:, b, 2:4], pos_half[:].broadcast_to([P, 2]), ALU.pow
                                    ).then_inc(sg["smooth_root"], 1)
                elif kind == "x_gate":
                    b, = a
                    pool.wait_ge(sg["ratio2_ready"], b + 1)
                    g.tensor_tensor(sm[:, b, 20:21], sm[:, b, 19:20], pos_half[:], ALU.pow
                                    ).then_inc(sg["smooth_root2"], 1)
                elif kind == "r_choose":
                    b, = a
                    pool.wait_ge(sg["chosen_ready"], b + 1)
                    h = h3[:, b % 2]
                    g.tensor_copy(h[:, :, W_TOK:W_WT], c_(C_TOKEN + NJ * b, NJ).rearrange("p (j o) -> p j o", o=1))
                    link(g.tensor_copy(h[:, :, W_EX:], tif[:]))
                elif kind == "scatter":
                    b, i = a
                    if i == 0:
                        pool.wait_ge(sg["slots_ready"], b + 1)
                        if b == 0:
                            pool.wait_ge(sg["xp_zeroed"], 16 * NZ)
                    j, k = i // TOPK, i % TOPK
                    g.indirect_dma_start(
                        out=xp_dram, out_offset=bass.IndirectOffsetOnAxis(ap=scat[:, NJ * b + j, k:k + 1], axis=0),
                        in_=h3[:, b % 2, j, :], in_offset=None, bounds_check=SLOTS - 1, oob_is_err=False
                    ).then_inc(scattered[b], 16)
                elif kind == "gather":
                    t, = a
                    if t == 0:
                        pool.wait_ge(sg["gather_ready"], B)
                        for i in range(NG_E):
                            pool.wait_ge(y_stored[i], 16)
                    if t >= 2:
                        pool.wait_ge(sg["combined"], FINISH.index(("combine", t - 2)) + 1)
                    for k in range(TOPK):
                        n = (t % 2) * TOPK + k
                        g.indirect_dma_start(
                            out=gbuf[:, n, :], out_offset=None, in_=y_dram,
                            in_offset=bass.IndirectOffsetOnAxis(ap=gath[:, t, k:k + 1], axis=0),
                            bounds_check=E * XR - 1, oob_is_err=False).then_inc(gathered[n], 16)


def shape_constants():
    import numpy as np

    c = np.zeros((P, NCONST + NLATE), np.float32)
    i = np.arange(P)
    c[:, C_ID:C_ID + P] = np.eye(P)
    c[:, C_MASK:C_MASK + P] = np.where(i[None, :] > i[:, None], -1e30, 0.0)
    c[:, C_TRI:C_TRI + P] = i[:, None] < i[None, :]
    freq = (1.0 / np.float32(10000.0) ** (np.arange(0, DR, 2, dtype=np.float32) / np.float32(DR))).astype(np.float32)
    for j in range(NJ):
        angle = (np.arange(P, dtype=np.float32) + np.float32(j * P))[:, None] * freq[None, :]
        cos, sin = np.cos(angle).astype(np.float32), np.sin(angle).astype(np.float32)
        o = j * DR
        c[:, C_COS + o:C_COS + o + DR] = np.concatenate([cos, cos], 1)
        c[:, C_SIN + o:C_SIN + o + DR] = np.concatenate([sin, -sin], 1)
    c[:, C_I32:C_I32 + E] = np.arange(E)
    c[:, C_I8:C_I8 + NG] = np.arange(NG)
    c[:, C_SLOT0:C_SLOT0 + E] = np.arange(E) * CAP
    c[:, C_TOKEN:C_TOKEN + NT] = np.arange(NT)[None, :] * P + i[:, None]
    c[:, C_EXPERT:C_EXPERT + NPAIR] = 2 * np.arange(NPAIR)[None, :] + i[:, None] // XR
    c[:, C_MIXED:] = np.concatenate([np.arange(t * P, (t + 1) * P) for t in MIXED])
    return c


_INS = ['x', 'fside_BxS2xS2_0', 'ctx_1024', 'L0_attn_w_kv_a', 'L0_attn_q_a_gamma', 'L0_attn_w_qb',
        'L0_attn_kv_a_gamma', 'L0_attn_w_kvb', 'L0_attn_w_o', 'L0_ffn_router_w', 'L0_ffn_e_bias', 'L0_ffn_W_gate',
        'L0_ffn_W_up', 'L0_ffn_W_down', 'L0_ffn_shared_gate', 'L0_ffn_shared_up', 'L0_ffn_shared_down']


def kernel(**inputs):
    import numpy as _np
    import concourse.bacc as _bacc
    from concourse import mybir as _mybir
    from concourse.bass_utils import run_bass_kernel_spmd as _run

    nc = _bacc.Bacc("TRN2", target_bir_lowering=False, num_devices=1)
    arrays, args = {}, []
    given = {name: _np.ascontiguousarray(inputs[name]) for name in _INS}
    given["shape_constants"] = shape_constants()
    for name, a in given.items():
        arrays[f"in_{name}_dram"] = a
        args.append(nc.dram_tensor(f"in_{name}_dram", a.shape, _mybir.dt.from_np(a.dtype), kind="ExternalInput").ap())
    args.append(nc.dram_tensor("out_0_dram", (B, S, D), F32, kind="ExternalOutput").ap())
    decoder_layer(nc, *args)
    r = _run(nc, [arrays], core_ids=[0])
    return r.results[0]["out_0_dram"]
```
